# Optimizing a Trainium2 kernel written in Bass

```python
import numpy as np
import jax
import jax.numpy as jnp

def _softmax(x, axis=-1):
    return jax.nn.softmax(x, axis=axis)

def _gelu(x):
    return jax.nn.gelu(x, approximate=True)

def _silu(x):
    return jax.nn.silu(x)

def _sigmoid(x):
    return jax.nn.sigmoid(x)

def _layernorm(x, axis=-1, eps=1e-05):
    m = jnp.mean(x, axis=axis, keepdims=True)
    v = jnp.var(x, axis=axis, keepdims=True)
    return (x - m) / jnp.sqrt(v + eps)

def _scatter_add(tgt, idx, src, axis=0):
    return tgt.at[idx].add(src)

def _segment_sum(src, seg, n):
    return jax.ops.segment_sum(src, seg, n)
kernel_name = 'mk_recurrent_d1_jaxref_r4_c27aff'

def setup_inputs(seed: int=0):
    np.random.seed(seed)
    _w = jnp.asarray

    def _L0_attn_setup():
        import jax, jax.numpy as jnp
        import numpy as np
        HIDDEN = 1024
        N_HEADS = 32
        N_KV = 8
        HEAD_DIM = HIDDEN // N_HEADS
        Q_PER_KV = N_HEADS // N_KV
        SEQ = 512
        ROPE_BASE = 1000000.0
        POS_SCALE = 1.0
        SM_SCALE = 1.0 / HEAD_DIM
        BLOCK = 64
        LOCAL_BLOCKS = 16
        VERT_STRIDE = 8

        def _blocksparse_mask(seq_len):
            nb = seq_len // BLOCK
            qb = np.arange(nb)[:, None]
            kb = np.arange(nb)[None, :]
            bmask = (kb <= qb) & ((qb - kb < LOCAL_BLOCKS) | ((kb + 1) % VERT_STRIDE == 0))
            emask = np.kron(bmask, np.ones((BLOCK, BLOCK), dtype=bool))
            i = np.arange(seq_len)
            emask &= i[:, None] >= i[None, :]
            return jnp.asarray(emask)

        def _rope(x, cos, sin):
            x1, x2 = jnp.split(x, 2, axis=-1)
            rot = jnp.concatenate([-x2, x1], axis=-1)
            return x * cos[None, :, None, :] + rot * sin[None, :, None, :]
        key = jax.random.key(seed)
        k1, k2, k3, k4, k5 = jax.random.split(key, 5)
        qkv_out = (N_HEADS + 2 * N_KV) * HEAD_DIM
        return {'hidden_states': jax.random.normal(k1, (1, SEQ, HIDDEN), dtype=jnp.float32), 'w_qkv': jax.random.normal(k2, (qkv_out, HIDDEN), dtype=jnp.float32) * 0.02, 'b_qkv': jnp.zeros((qkv_out,), dtype=jnp.float32), 'w_dense': jax.random.normal(k3, (HIDDEN, HIDDEN), dtype=jnp.float32) * 0.02, 'b_dense': jnp.zeros((HIDDEN,), dtype=jnp.float32)}
    _L0_attn_in = _L0_attn_setup()

    def _L0_ffn_setup():
        import jax, jax.numpy as jnp
        import numpy as np
        NUM_EXPERTS = 8
        RANK = 32
        ALPHA = 16.0
        TOP_K = 2
        TEMPERATURE = 1.0
        GAMMA = 0.5
        SOFT_TOPK_TEMP = 0.5
        N_GRAM = 2
        EPS = 1e-06
        key = jax.random.key(seed)
        ks = jax.random.split(key, 6)
        d_in, d_out = (1024, 1024)
        Bsz, T = (4, 512)
        x = jax.random.normal(ks[0], (Bsz, T, d_in), dtype=jnp.float32)
        W = jax.random.normal(ks[1], (d_out, d_in), dtype=jnp.float32) / np.sqrt(d_in)
        b = jax.random.normal(ks[2], (d_out,), dtype=jnp.float32) * 0.01
        A = jax.random.normal(ks[3], (d_in, RANK), dtype=jnp.float32) / np.sqrt(d_in)
        Bmat = jax.random.normal(ks[4], (RANK, d_out), dtype=jnp.float32) * 0.01
        LiMEs = jax.random.normal(ks[5], (NUM_EXPERTS, RANK), dtype=jnp.float32) * 0.1
        return {'x': x, 'W': W, 'b': b, 'A': A, 'Bmat': Bmat, 'LiMEs': LiMEs}
    _L0_ffn_in = _L0_ffn_setup()
    _d = {'L0_attn_hidden_states': _L0_attn_in['hidden_states'], 'L0_attn_w_qkv': _L0_attn_in['w_qkv'], 'L0_attn_b_qkv': _L0_attn_in['b_qkv'], 'L0_attn_w_dense': _L0_attn_in['w_dense'], 'L0_attn_b_dense': _L0_attn_in['b_dense'], 'L0_ffn_W': _L0_ffn_in['W'], 'L0_ffn_b': _L0_ffn_in['b'], 'L0_ffn_A': _L0_ffn_in['A'], 'L0_ffn_Bmat': _L0_ffn_in['Bmat'], 'L0_ffn_LiMEs': _L0_ffn_in['LiMEs']}
    _x0 = _d['L0_attn_hidden_states']
    _d['L0_attn_hidden_states'] = jax.random.normal(jax.random.fold_in(jax.random.key(seed), 1), (2, 2048, 1024), dtype=_x0.dtype)
    del _x0
    return _d

def reference(L0_attn_hidden_states, L0_attn_w_qkv, L0_attn_b_qkv, L0_attn_w_dense, L0_attn_b_dense, L0_ffn_W, L0_ffn_b, L0_ffn_A, L0_ffn_Bmat, L0_ffn_LiMEs):

    def _L0_attn_ref(hidden_states, w_qkv, b_qkv, w_dense, b_dense):
        import jax, jax.numpy as jnp
        import numpy as np
        HIDDEN = 1024
        N_HEADS = 32
        N_KV = 8
        HEAD_DIM = HIDDEN // N_HEADS
        Q_PER_KV = N_HEADS // N_KV
        SEQ = 512
        ROPE_BASE = 1000000.0
        POS_SCALE = 1.0
        SM_SCALE = 1.0 / HEAD_DIM
        BLOCK = 64
        LOCAL_BLOCKS = 16
        VERT_STRIDE = 8

        def _blocksparse_mask(seq_len):
            nb = seq_len // BLOCK
            qb = np.arange(nb)[:, None]
            kb = np.arange(nb)[None, :]
            bmask = (kb <= qb) & ((qb - kb < LOCAL_BLOCKS) | ((kb + 1) % VERT_STRIDE == 0))
            emask = np.kron(bmask, np.ones((BLOCK, BLOCK), dtype=bool))
            i = np.arange(seq_len)
            emask &= i[:, None] >= i[None, :]
            return jnp.asarray(emask)

        def _rope(x, cos, sin):
            x1, x2 = jnp.split(x, 2, axis=-1)
            rot = jnp.concatenate([-x2, x1], axis=-1)
            return x * cos[None, :, None, :] + rot * sin[None, :, None, :]
        B, S, _ = hidden_states.shape
        qkv = jnp.einsum('bsh,oh->bso', hidden_states, w_qkv) + b_qkv
        qkv = qkv.reshape(B, S, N_KV, Q_PER_KV + 2, HEAD_DIM)
        q = qkv[:, :, :, :Q_PER_KV].reshape(B, S, N_HEADS, HEAD_DIM)
        k = qkv[:, :, :, Q_PER_KV]
        v = qkv[:, :, :, Q_PER_KV + 1]
        inv_freq = 1.0 / ROPE_BASE ** (jnp.arange(0, HEAD_DIM, 2, dtype=jnp.float32) / HEAD_DIM)
        t = jnp.arange(S, dtype=jnp.float32) * POS_SCALE
        freqs = jnp.outer(t, inv_freq)
        emb = jnp.concatenate([freqs, freqs], axis=-1)
        cos, sin = (jnp.cos(emb), jnp.sin(emb))
        q = _rope(q, cos, sin)
        k = _rope(k, cos, sin)
        k = jnp.repeat(k, Q_PER_KV, axis=2)
        v = jnp.repeat(v, Q_PER_KV, axis=2)
        mask = _blocksparse_mask(S)
        scores = jnp.einsum('bqhd,bkhd->bhqk', q, k) * SM_SCALE
        scores = jnp.where(mask[None, None], scores, jnp.finfo(scores.dtype).min)
        probs = jax.nn.softmax(scores, axis=-1)
        ctx = jnp.einsum('bhqk,bkhd->bqhd', probs, v).reshape(B, S, HIDDEN)
        out = jnp.einsum('bsh,oh->bso', ctx, w_dense) + b_dense
        return out

    def _L0_ffn_ref(x, W, b, A, Bmat, LiMEs):
        import jax, jax.numpy as jnp
        import numpy as np
        NUM_EXPERTS = 8
        RANK = 32
        ALPHA = 16.0
        TOP_K = 2
        TEMPERATURE = 1.0
        GAMMA = 0.5
        SOFT_TOPK_TEMP = 0.5
        N_GRAM = 2
        EPS = 1e-06
        Bsz, T, d_in = x.shape
        E = LiMEs.shape[0]
        scaling = ALPHA / RANK
        H = jnp.einsum('btd,od->bto', x, W) + b
        z = jnp.einsum('btd,dr->btr', x, A)
        anchors = jnp.arange(N_GRAM - 1, T, N_GRAM)
        H_slice = H[:, anchors, :E]
        delta_slice = jnp.einsum('bar,er->bae', z[:, anchors], LiMEs)
        H_scale = jnp.maximum(jnp.max(jnp.abs(H_slice)), EPS)
        d_scale = jnp.maximum(jnp.max(jnp.abs(delta_slice)), EPS)
        logits = ((1.0 - GAMMA) * (H_slice / H_scale) + GAMMA * (delta_slice / d_scale)) / TEMPERATURE
        probs = jax.nn.softmax(logits, axis=-1)
        topk_vals, _ = jax.lax.top_k(probs, TOP_K)
        thresh = topk_vals[..., -1:]
        mask = jax.nn.sigmoid((probs - thresh) / SOFT_TOPK_TEMP)
        weights = probs * mask
        weights = weights / (jnp.sum(weights, axis=-1, keepdims=True) + 1e-09)
        weights_full = jnp.repeat(weights, N_GRAM, axis=1)
        p_mix = jnp.einsum('bte,er->btr', weights_full, LiMEs)
        delta = jnp.einsum('btr,ro->bto', z * p_mix, Bmat) * scaling
        return H + delta
    x = L0_attn_hidden_states
    xn = _layernorm(x, axis=-1)
    s = _L0_attn_ref(xn, L0_attn_w_qkv, L0_attn_b_qkv, L0_attn_w_dense, L0_attn_b_dense)
    g = _silu(_L0_ffn_ref(xn, L0_ffn_W, L0_ffn_b, L0_ffn_A, L0_ffn_Bmat, L0_ffn_LiMEs))
    x = x + s * g
    return x

_drawn_inputs = setup_inputs


def setup_inputs(seed=0):
    import zlib

    import numpy as np

    out = dict(_drawn_inputs(seed))
    spreads = {'L0_attn_b_qkv': (0.0, 0.1), 'L0_attn_b_dense': (0.0, 0.1)}
    factors = {'L0_ffn_b': 64.0, 'L0_ffn_A': 8.0, 'L0_ffn_Bmat': 8.0, 'L0_ffn_LiMEs': 8.0}
    for name, (base, spread) in spreads.items():
        noise = np.random.default_rng([zlib.crc32(name.encode()), seed]).standard_normal(out[name].shape)
        drawn = base * np.exp(spread * noise) if base else spread * noise
        out[name] = jnp.asarray(drawn.astype(out[name].dtype))
    for name, factor in factors.items():
        out[name] = (out[name] * factor).astype(out[name].dtype)
    return out
```

```python
from contextlib import ExitStack

import concourse.bass as bass
from concourse import mybir

ALU = mybir.AluOpType
ACT = mybir.ActivationFunctionType
F32 = mybir.dt.float32
F16 = mybir.dt.float16
BF16 = mybir.dt.bfloat16
AX = mybir.AxisListType
RMAX = bass.bass_isa.ReduceOp.max

P = 128
B, S, D = 2, 2048, 1024
KC = D // P
N_KV, QH, HD = 8, 4, 32
HALF = HD // 2
GROUPS = B * N_KV
TG = 512
STEPS = B * S // TG
E, RANK = 8, 32
NQK = N_KV * (QH + 1) * HD
NF = NQK // P
NV = N_KV * HD
NAT = E + RANK
W1N = NQK + NV + NAT
BLK, LOCAL, VERT = 64, 16, 8
NT = S // P
NCH = S // TG
SM_SCALE = 1.0 / HD
ALPHA_OVER_RANK = 16.0 / RANK
WS = 256.0
CS = 256.0
SHIFT = 2048.0
NEG = -1.0e30
LOWEST = -3.0e38
LN_EPS = 1e-5
SCALE_EPS = 1e-6
ONES_ROW = 256.0
PSUM_BANK = 512
STACK = 3 * HD
ZROWS = 3 * RANK + 3
MAXRING, SCORERING, PROBRING, ADDRING = 3, 3, 5, 2
HOP, PLACING, LEAD, PACE_SLACK = 180.0, 4000.0, 10000, 0



def is_vertical(block):
    return (block + 1) % VERT == 0


def max_banks(t):
    banks = []
    if 2 * t + 1 < LOCAL:
        start, n = 0, P * (t + 1)
    else:
        start, n = BLK * (2 * t - LOCAL + 2), P * (LOCAL // 2)
    full, rest = n // PSUM_BANK, n % PSUM_BANK
    for seg in range(full):
        for h in range(QH):
            banks.append(dict(t=t, heads=[h], pieces=[(start + seg * PSUM_BANK, PSUM_BANK)], seg=seg,
                              mask="diagonal" if rest == 0 and seg == full - 1 else None))
    if rest:
        per = min(QH, PSUM_BANK // rest)
        for h in range(0, QH, per):
            banks.append(dict(t=t, heads=list(range(h, h + per)), pieces=[(start + full * PSUM_BANK, rest)],
                              seg=full, mask="diagonal"))
    if start > 0:
        oldest = 2 * t - LOCAL + 1
        pieces = [(BLK * oldest, BLK)]
        pieces += [(BLK * j, BLK) for j in range(oldest) if is_vertical(j)]
        banks.append(dict(t=t, heads=list(range(QH)), pieces=pieces, seg=full,
                          mask=None if is_vertical(oldest) else "late queries"))
    return banks


def key_units(c):
    per = TG // BLK
    units = []
    for j in range(min(NT, (c + 1) * TG // P)):
        lo, hi = max(per * c, 2 * j), min(per * c + per - 1, 2 * j + LOCAL)
        if is_vertical(2 * j + 1):
            hi = per * c + per - 1
        if lo > hi:
            continue
        far = max(0, hi - max(lo, 2 * j + LOCAL) + 1)
        units.append((j, lo, hi - lo + 1, 2 * j >= per * c, far))
    return sorted(units, key=lambda u: (-(u[2] == per), u[1], u[2] if u[1] == per * c else -u[2]))


def sum_groups(c):
    units = key_units(c)
    spans = [((lo - c * (TG // BLK)) * BLK, n * BLK) for _, lo, n, _, _ in units]
    groups, i = [], 0
    while i < len(units):
        a, wa = spans[i]
        if i + 1 < len(units):
            b, wb = spans[i + 1]
            start, end = max(a, b), min(a + wa, b + wb)
            if end - start >= 2 * BLK:
                direct = []
                for j, (x, w) in ((i, spans[i]), (i + 1, spans[i + 1])):
                    if x < start:
                        direct.append((j, x, start - x))
                    if x + w > end:
                        direct.append((j, end, x + w - end))
                groups.append(((i, i + 1), (start, end - start), direct))
                i += 2
                continue
        groups.append(((i,), None, [(i, a, wa)]))
        i += 1
    return groups


def max_stream():
    out, due = [], []
    for c in range(NCH):
        for t in range(c * NCH, c * NCH + TG // P):
            for bank in max_banks(t):
                out.append(("bank", bank))
                due = [(n - 1, d) for n, d in due]
                while due and due[0][0] == 0:
                    out.append(("row", due.pop(0)[1]))
        out.append(("fold", c))
        due.append((3, c))
    out += [("row", d) for _, d in due]
    return out


def bank_columns(bank):
    return len(bank["heads"]) * sum(w for _, w in bank["pieces"])


def work_of(kind, item):
    if kind == "bank":
        columns = bank_columns(item)
        return 0.42 * columns + (56 if item["mask"] else 0) + 20, 1.04 * columns + 70
    if kind == "row":
        return 60, 150
    if kind == "fold":
        return 0, 250
    if kind == "scores":
        _, _, n, diagonal, far = item
        return 27 * n + 27 * far + (56 if diagonal else 0), 54 * n + 60
    if kind == "values":
        return 117 * item[2], 0
    if kind == "sums":
        _, added, direct = item
        added = added[1] if added else 0
        return 1.83 * (added + sum(w for _, _, w in direct)), 9.0 * added + 80
    raise ValueError(kind)


def attention_order():
    maxima = max_stream()
    units = [(c, i, u) for c in range(NCH) for i, u in enumerate(key_units(c))]
    total = sum(bank_columns(m[1]) for m in maxima if m[0] == "bank")
    done, row_at = 0, {}
    for kind, m in maxima:
        if kind == "bank":
            done += bank_columns(m)
        elif kind == "row":
            row_at[m] = done
    begin, at = {}, 0
    span = sum(QH * BLK * u[2] for _, _, u in units)
    for c, i, u in units:
        if i == 0:
            begin[c] = at * total / span
        at += QH * BLK * u[2]
    lead = max(row_at[c] - begin[c] for c in range(NCH)) + LEAD
    ahead, done = 0, 0
    while done < lead:
        if maxima[ahead][0] == "bank":
            done += bank_columns(maxima[ahead][1])
        ahead += 1
    stream = [(0, m) for m in maxima[ahead:]] + [(1, m) for m in maxima] + [(2, m) for m in maxima[:ahead]]

    scores = [(s, c, i, u, h) for s in range(2) for c, i, u in units for h in range(QH)]
    order, inversions = [], []
    pe = act = dve = pool = 0.0
    read, exps, unit_exps = [0.0] * MAXRING, [0.0] * SCORERING, {}
    values, sums, free = [], [], {}
    placed, shifted = {}, {}
    pos = at = taken = 0
    n_scores = n_values = n_adds = 0
    unit_at = {(s, c, i): n for n, (s, c, i) in
               enumerate((s, c, i) for s in range(2) for c, i, _ in units)}
    add_free, out_at = [0.0] * ADDRING, [0.0, 0.0]
    while at < len(scores) or pos < len(stream) or values or sums:
        options = []
        if at < len(scores):
            s, c, i, u, h = scores[at]
            ready = max(exps[-SCORERING], free.get(unit_at[s, c, i] - PROBRING, 0.0) - 700)
            blocked = any(m == ("row", c) and g == s for g, m in stream[pos:])
            ready = max(ready, placed.get((s, c), 0.0))
            pace = n_scores * total / span + PACE_SLACK
            before = unit_at[s, c, i] - PROBRING
            blocked = blocked or before >= n_values or any(
                before == unit_at[x[1], x[2], m] for x in sums for m in x[4][0])
            if not blocked:
                options.append((ready, 2 if taken >= pace - PACE_SLACK else 3, "scores"))
        if pos < len(stream):
            g, (kind, m) = stream[pos]
            ready = read[-MAXRING] if kind != "fold" else 0.0
            if kind == "row":
                ready = max(ready, shifted[g, m])
            options.append((ready, 3 if n_scores * total / span <= taken else 2, "max"))
        if values:
            options.append((values[0][0], 1, "values"))
        if sums:
            options.append((sums[0][0], 0, "sums"))
        now = [o for o in options if o[0] <= pe]
        ready, _, kind = min(now, key=lambda o: (o[1], o[0])) if now else min(options, key=lambda o: (o[0], o[1]))
        pe = max(pe, ready)
        if kind == "scores":
            mine, next_one = work_of("scores", u)
            pe += mine
            act = max(act, pe + HOP) + next_one
            exps.append(act + HOP)
            order.append(("scores", s, c, i, u, h))
            at += 1
            n_scores += BLK * u[2]
            if h == QH - 1:
                unit_exps[s, c, i] = act + HOP
                values.append((act + HOP, s, c, i, u))
                for n, group in enumerate(sum_groups(c)):
                    if group[0][-1] == i:
                        wait = max(unit_exps[s, c, i], pool, add_free[-ADDRING])
                        if group[1] is not None:
                            pool = wait + work_of("sums", group)[1]
                            for m in group[0]:
                                free[unit_at[s, c, m]] = pool + HOP
                        sums.append((pool + HOP if group[1] is not None else act + HOP, s, c, n, group))
                        if group[1] is not None:
                            add_free.append(pool + 3000)
        elif kind == "max":
            g, (kind, m) = stream[pos]
            pos += 1
            mine, next_one = work_of(kind, m)
            pe += mine
            order.append((kind, g, m))
            dve = max(dve, pe + HOP) + next_one
            if kind == "fold":
                shifted[g, m] = dve + HOP
                continue
            read.append(dve + HOP)
            if kind == "bank":
                taken += bank_columns(m)
            else:
                placed[g, m] = dve + PLACING
            if inversions:
                o = inversions.pop(0)
                order.append(o)
                if o[0] == "invert":
                    dve += 870
                else:
                    pool = max(pool, dve) + 3500
        elif kind == "values":
            _, s, c, i, u = values.pop(0)
            pe = max(pe, out_at[0] if i == 0 else 0.0) + work_of("values", u)[0]
            n_values += 1
            k = unit_at[s, c, i]
            free[k] = max(free.get(k, 0.0), pe + HOP)
            last = i == len(key_units(c)) - 1
            order.append(("values", s, c, i, u, last))
            if last:
                order.append(("context", s, c))
                act = max(act, pe + HOP) + 480
                out_at[0] = act + HOP
        else:
            _, s, c, n, group = sums.pop(0)
            pe = max(pe, out_at[1] if n == 0 else 0.0) + work_of("sums", group)[0]
            for m, _, _ in group[2]:
                k = unit_at[s, c, m]
                free[k] = max(free.get(k, 0.0), pe + HOP)
            last = n == len(sum_groups(c)) - 1
            order.append(("sums", s, c, n, group, last))
            if last:
                order.append(("totals", s, c))
                act = max(act, pe + HOP) + 480
                out_at[1] = act + HOP
                inversions += [("invert", s, c, piece) for piece in range(TG // P)] + [("split", s, c)]
    return order + inversions, maxima[:ahead]



def mk_recurrent_d1(nc, x, w1, b_qk, b_v, w_out, b_out, b_ffn, adapter_out, limes, limes_t, rope, consts, out):
    q_parts = nc.dram_tensor("q_parts", [2, GROUPS + 1, P, S], F16).ap()
    k_parts = nc.dram_tensor("k_parts", [2, GROUPS + 1, HD, S], F16).ap()
    xt_parts = nc.dram_tensor("xt_parts", [2, STEPS, P, KC * TG], F16).ap()
    ctx_parts = nc.dram_tensor("ctx_parts", [2, GROUPS, NCH, P, TG], F16).ap()
    v_parts = nc.dram_tensor("v_parts", [GROUPS + 1, P, NT * HD], F32).ap()

    with ExitStack() as whole:
        def keep(name, shape, dt):
            return whole.enter_context(nc.sbuf_tensor(name, shape, dt))

        ident32 = keep("ident32", [P, P], F32)
        ident16 = keep("ident16", [P, P], F16)
        ident_bf = keep("ident_bf", [P, P], BF16)
        pair_odd = keep("pair_odd", [P, P], F32)
        mask_q = keep("mask_q", [P, P], BF16)
        mask_k = keep("mask_k", [P, P], BF16)
        mask_early = keep("mask_early", [P, BLK], BF16)
        mask_late = keep("mask_late", [P, BLK], BF16)
        zstack = keep("zstack", [P, B * S], F16)
        bstack = keep("bstack", [P, D], F16)
        banks = [whole.enter_context(nc.psum_tensor(f"bank{i}", [P, PSUM_BANK], F32)) for i in range(8)]

        with ExitStack() as stage:
            natural = stage.enter_context(nc.sbuf_tensor("natural", [P, B * NT, NAT], F32))
            project(nc, x, w1, b_qk, b_v, rope, consts, q_parts, k_parts, xt_parts, ident32, ident16,
                    ident_bf, pair_odd, mask_q, mask_k, mask_early, mask_late, v_parts, natural, banks)
            route(nc, limes, limes_t, adapter_out, b_ffn, natural, ident32, pair_odd, zstack, bstack, banks)
        with ExitStack() as stage:
            w_hi = stage.enter_context(nc.sbuf_tensor("w_hi", [P, 2 * KC, D], F16))
            w_lo = stage.enter_context(nc.sbuf_tensor("w_lo", [P, 2 * KC, D], F16))
            attend(nc, q_parts, k_parts, v_parts, ctx_parts, w_out, w_hi, w_lo, ident16, ident_bf,
                   mask_q, mask_k, mask_early, mask_late, banks)
            finish(nc, x, xt_parts, ctx_parts, w_hi, w_lo, zstack, bstack, b_out, out, banks)


def project(nc, x, w1, b_qk, b_v, rope, consts, q_parts, k_parts, xt_parts, ident32, ident16,
            ident_bf, pair_odd, mask_q, mask_k, mask_early, mask_late, v_parts, natural, banks):
    WP = P
    pieces = [(c, min(WP, W1N - c)) for c in range(0, W1N, WP)]
    TT = TG // P
    STAGES = 3
    with ExitStack() as ctx:
        def sb(name, shape, dt):
            return ctx.enter_context(nc.sbuf_tensor(name, shape, dt))

        def sem(name):
            return ctx.enter_context(nc.semaphore(name))

        cpack = sb("cpack", [P, 4 * P + 2 * BLK], F32)
        w1_hi = sb("w1_hi", [P, KC, W1N], F16)
        w1_lo = sb("w1_lo", [P, KC, W1N], F16)
        wstage = [sb(f"wstage{i}", [P, KC, WP], F32) for i in range(STAGES)]
        bqk = sb("bqk", [P, NF], F32)
        bv = sb("bv", [P, NV + NAT], F32)
        table = sb("table", [P, 2, S], F32)
        eps = sb("eps", [P, 1], F32)
        xin = sb("xin", [P, TT, D], F32)
        stats = sb("stats", [P, TT, 12], F32)
        moments = sb("moments", [P, TT, 2], F32)
        deviation = sb("deviation", [P, TT], F32)
        rstd = sb("rstd", [P, TT], F32)
        xt_hi = [sb(f"xt_hi{i}", [P, KC, TG], F16) for i in range(2)]
        xt_lo = [sb(f"xt_lo{i}", [P, KC, TG], F16) for i in range(2)]
        raw = [sb(f"raw{i}", [P, TG], F32) for i in range(2)]
        by_cos = [sb(f"by_cos{i}", [P, TG], F32) for i in range(2)]
        by_sin = [sb(f"by_sin{i}", [P, TG], F32) for i in range(2)]
        rotated = [sb(f"rotated{i}", [P, TG], F32) for i in range(2)]
        r_hi = [sb(f"r_hi{i}", [P, TG], F16) for i in range(2)]
        r_lo = [sb(f"r_lo{i}", [P, TG], F16) for i in range(2)]
        vst = [sb(f"vst{i}", [P, N_KV, TT * HD], F32) for i in range(2)]
        zero16, zero32 = xt_hi[0], vst[0]

        TURN, PROJ = banks[0:2], banks[2:6]

        c_loaded = sem("c_loaded")
        small_loaded = sem("small_loaded")
        c_ready = sem("c_ready")
        w_loaded = [sem(f"w_loaded{i}") for i in range(STAGES)]
        w_hi_done = sem("w_hi_done")
        w_lo_done = sem("w_lo_done")
        zeroed = sem("zeroed")
        pad_stored = sem("pad_stored")
        x_loaded = [sem(f"x_loaded{i}") for i in range(TT)]
        stats_done = sem("stats_done")
        moments_done = sem("moments_done")
        deviation_done = sem("deviation_done")
        rstd_done = sem("rstd_done")
        xn_done = sem("xn_done")
        turned = sem("turned")
        xt_hi_done = sem("xt_hi_done")
        xt_lo_done = sem("xt_lo_done")
        xt_stored = [sem(f"xt_stored{i}") for i in range(2)]
        projected = sem("projected")
        raw_done = sem("raw_done")
        v_done = sem("v_done")
        v_stored = [sem(f"v_stored{i}") for i in range(2)]
        parts_done = sem("parts_done")
        rotated_done = sem("rotated_done")
        r_hi_done = sem("r_hi_done")
        r_lo_done = sem("r_lo_done")
        r_stored = [sem(f"r_stored{i}") for i in range(2)]

        TURNED0 = KC
        LO0 = 2
        PROJ0 = 2 * (NF + TT)
        V0 = TT
        RING0 = 2
        STORED0 = 32
        PADS = 5 * 16

        def wait_xt(eng, r, s):
            eng.wait_ge(xt_lo_done, LO0 + r * 2 * KC + (s + 1) * KC)

        TURN_AT = 2

        block = ctx.enter_context(nc.Block())

        @block.sync
        def _(sp):
            sp.dma_start(cpack[:, :], consts).then_inc(c_loaded, 16)
            w_v = w1.rearrange("(k p) n -> p k n", p=P)
            for n, (c, w) in enumerate(pieces):
                if n >= STAGES:
                    sp.wait_ge(w_lo_done, n - STAGES + 1)
                sp.dma_start(wstage[n % STAGES][:, :, 0:w], w_v[:, :, c:c + w]).then_inc(w_loaded[n % STAGES], 16)
                if n == 0:
                    sp.dma_start(bqk[:, :], b_qk).then_inc(small_loaded, 16)
                    sp.dma_start(bv[:, :], b_v.partition_broadcast(P)).then_inc(small_loaded, 16)
                    sp.dma_start(table[:, :, :], rope).then_inc(small_loaded, 16)
            sp.wait_ge(zeroed, 1)
            for part in range(2):
                sp.dma_start(q_parts[part, GROUPS], zero16[:, 0:NCH, :].rearrange("p a b -> p (a b)")).then_inc(pad_stored, 16)
                sp.dma_start(k_parts[part, GROUPS], zero16[0:HD, 0:NCH, :].rearrange("p a b -> p (a b)")).then_inc(pad_stored, 16)
            sp.dma_start(v_parts[GROUPS], zero32[:, 0:N_KV // 2, :].rearrange("p a b -> p (a b)")).then_inc(pad_stored, 16)
            with sp.Fori(0, B) as b:
                with sp.Fori(0, 2) as rr:
                    r = b * 2 + rr

                    def store_xt(s):
                        sp.wait_ge(xt_lo_done, LO0 + r * 2 * KC + (s + 1) * KC)
                        for part, xt in enumerate((xt_hi, xt_lo)):
                            sp.dma_start(xt_parts[part, r * 2 + s],
                                         xt[s][:, :, :].rearrange("p k t -> p (k t)")).then_inc(xt_stored[s], 16)

                    store_xt(0)
                    for s in range(2):
                        for f in range(NF):
                            sp.wait_ge(r_lo_done, RING0 + r * 2 * NF + s * NF + f + 1)
                            for part, half in enumerate((r_hi, r_lo)):
                                toks = bass.ds(rr * 2 * TG + s * TG, TG)
                                for a in range(2):
                                    rows = slice(a * QH * HALF, (a + 1) * QH * HALF)
                                    if f < N_KV:
                                        dst = q_parts[part, b * N_KV + f, rows, toks]
                                    else:
                                        dst = k_parts[part, bass.ds(b * N_KV + (f - N_KV) * QH, QH),
                                                      a * HALF:(a + 1) * HALF, toks]
                                    sp.dma_start(dst, half[f % 2][rows, :]).then_inc(r_stored[f % 2], 16)
                        sp.wait_ge(v_done, V0 + (2 * r + s + 1) * TT)
                        sp.dma_start(v_parts[bass.ds(b * N_KV, N_KV), :, bass.ds((rr * 2 + s) * TT * HD, TT * HD)].rearrange(
                            "g p x -> p g x"), vst[s][:, :, :]).then_inc(v_stored[s], 16)
                        if s == 0:
                            store_xt(1)
            sp.wait_ge(pad_stored, PADS)
            for s in range(2):
                sp.wait_ge(v_stored[s], 16 + 16 * STEPS // 2)
                sp.wait_ge(xt_stored[s], STORED0 + 32 * STEPS // 2)
                sp.wait_ge(r_stored[s], 64 + 64 * STEPS * NF // 2)

        @block.gpsimd
        def _(pool):
            nc.gpsimd.memset(zero16[:, :, :], 0.0)
            nc.gpsimd.memset(zero32[:, :, :], 0.0).then_inc(zeroed, 1)
            pool.sem_inc(rotated_done, RING0)
            with pool.Fori(0, B) as b:
                with pool.Fori(0, 2) as rr:
                    r = b * 2 + rr
                    for s in range(2):
                        for f in range(NF):
                            k = r * 2 * NF + s * NF + f
                            pool.wait_ge(parts_done, RING0 + k + 1)
                            pool.wait_ge(r_lo_done, k + 1)
                            nc.gpsimd.tensor_tensor(rotated[f % 2][:, :], by_cos[f % 2][:, :], by_sin[f % 2][:, :],
                                                    ALU.add).then_inc(rotated_done, 1)

        @block.scalar
        def _(act):
            act.sem_inc(r_stored[0], 64)
            act.sem_inc(r_stored[1], 64)
            act.sem_inc(xt_stored[0], STORED0)
            act.sem_inc(xt_stored[1], STORED0)
            x_v = x.rearrange("(i t p) d -> i t p d", t=TT, p=P)
            for n, (c, w) in enumerate(pieces):
                act.wait_ge(w_loaded[n % STAGES], 16 * (n // STAGES + 1))
                nc.scalar.activation(w1_hi[:, :, c:c + w], wstage[n % STAGES][:, :, 0:w], ACT.Copy,
                                     scale=WS).then_inc(w_hi_done, 1)
            act.wait_ge(small_loaded, 48)
            act.wait_ge(pad_stored, PADS)
            with act.Fori(0, B) as b:
                with act.Fori(0, 2) as rr:
                    r = b * 2 + rr

                    def deviate(s):
                        act.wait_ge(moments_done, r * 2 * TT + (s + 1) * TT)
                        nc.scalar.activation(deviation[:, :], moments[:, :, 1], ACT.Sqrt,
                                             bias=eps[:, 0:1]).then_inc(deviation_done, 1)

                    def split_xt(s, k):
                        if k == 0:
                            act.wait_ge(projected, r * 2 * (NF + TT) + (s + 1) * (NF + TT))
                            act.wait_ge(xt_stored[s], STORED0 + 32 * r)
                        act.wait_ge(turned, TURNED0 + r * 2 * KC + s * KC + k + 1)
                        nc.scalar.activation(xt_hi[s][:, k, :], TURN[k % 2][:, :], ACT.Copy).then_inc(xt_hi_done, 1)

                    def split_rotated(s, f):
                        act.wait_ge(rotated_done, RING0 + r * 2 * NF + s * NF + f + 1)
                        act.wait_ge(r_stored[f % 2], 64 + r * 64 * NF + s * 64 * (NF // 2) + 64 * (f // 2))
                        nc.scalar.activation(r_hi[f % 2][:, :], rotated[f % 2][:, :], ACT.Copy).then_inc(r_hi_done, 1)

                    def load_x(s):
                        act.wait_ge(turned, r * 2 * KC + (s + 1) * KC)
                        for t in range(TT):
                            act.dma_start(xin[:, t, :], x_v[r * 2 + s, t]).then_inc(x_loaded[t], 16)

                    load_x(0)
                    deviate(0)
                    for k in range(KC):
                        split_xt(0, k)
                    for s in range(2):
                        if s == 0:
                            load_x(1)
                            deviate(1)
                        for f in range(NF):
                            if s == 0 and f >= TURN_AT:
                                split_xt(1, f - TURN_AT)
                            use = s * (NF + TT) + f
                            act.wait_ge(projected, PROJ0 + r * 2 * (NF + TT) + use + 1)
                            act.wait_ge(parts_done, r * 2 * NF + s * NF + f + 1)
                            nc.scalar.activation(raw[f % 2][:, :], PROJ[use % 4][:, :], ACT.Identity,
                                                 bias=bqk[:, f:f + 1], scale=1.0 / WS).then_inc(raw_done, 1)
                            if f:
                                split_rotated(s, f - 1)
                        split_rotated(s, NF - 1)

        @block.vector
        def _(dve):
            nc.vector.memset(eps[:, :], LN_EPS)
            dve.sem_inc(xt_lo_done, LO0)
            dve.sem_inc(v_done, V0)
            dve.sem_inc(parts_done, RING0)
            dve.sem_inc(r_lo_done, RING0)
            dve.wait_ge(c_loaded, 16)
            for dst, at, w in ((ident32, 0, P), (ident16, 0, P), (ident_bf, 0, P), (pair_odd, P, P),
                               (mask_q, 2 * P, P), (mask_k, 3 * P, P), (mask_early, 4 * P, BLK),
                               (mask_late, 4 * P + BLK, BLK)):
                nc.vector.tensor_copy(dst[:, :], cpack[:, at:at + w]).then_inc(c_ready, 1)
            for n, (c, w) in enumerate(pieces):
                dve.wait_ge(w_hi_done, n + 1)
                nc.vector.scalar_tensor_tensor(w1_lo[:, :, c:c + w], wstage[n % STAGES][:, :, 0:w], WS,
                                               w1_hi[:, :, c:c + w], ALU.mult, ALU.subtract).then_inc(w_lo_done, 1)
            dve.wait_ge(small_loaded, 48)
            dve.wait_ge(pad_stored, PADS)
            dve.sem_inc(v_stored[0], 16)
            dve.sem_inc(v_stored[1], 16)
            with dve.Fori(0, B) as b:
                with dve.Fori(0, 2) as rr:
                    r = b * 2 + rr

                    def normalise(s):
                        for t in range(TT):
                            dve.wait_ge(x_loaded[t], 32 * r + 16 * (s + 1))
                            for i in range(2):
                                nc.vector.bn_stats(stats[:, t, 6 * i:6 * i + 6],
                                                   xin[:, t, i * 512:(i + 1) * 512]).then_inc(stats_done, 1)
                        dve.wait_ge(stats_done, r * 4 * TT + (s + 1) * 2 * TT)
                        nc.vector.memset(rstd[:, :], 0.0)
                        for t in range(TT):
                            nc.vector.bn_aggr(moments[:, t, :], stats[:, t, :]).then_inc(moments_done, 1)
                        dve.wait_ge(deviation_done, 2 * r + s + 1)
                        nc.vector.reciprocal(rstd[:, :], deviation[:, :]).then_inc(rstd_done, 1)
                        dve.wait_ge(rstd_done, 2 * r + s + 1)
                        for t in range(TT):
                            nc.vector.tensor_scalar(xin[:, t, :], xin[:, t, :], moments[:, t, 0:1], rstd[:, t:t + 1],
                                                    ALU.subtract, ALU.mult).then_inc(xn_done, 1)

                    def split_xt(s, k):
                        dve.wait_ge(xt_hi_done, r * 2 * KC + s * KC + k + 1)
                        nc.vector.tensor_tensor(xt_lo[s][:, k, :], TURN[k % 2][:, :], xt_hi[s][:, k, :],
                                                ALU.subtract).then_inc(xt_lo_done, 1)

                    def split_rotated(s, f):
                        dve.wait_ge(r_hi_done, r * 2 * NF + s * NF + f + 1)
                        nc.vector.tensor_tensor(r_lo[f % 2][:, :], rotated[f % 2][:, :], r_hi[f % 2][:, :],
                                                ALU.subtract).then_inc(r_lo_done, 1)

                    normalise(0)
                    for k in range(KC):
                        split_xt(0, k)
                    for s in range(2):
                        if s == 0:
                            normalise(1)
                        now = bass.ds(rr * 2 * TG + s * TG, TG)
                        for f in range(NF):
                            if s == 0 and f >= TURN_AT:
                                split_xt(1, f - TURN_AT)
                            k = r * 2 * NF + s * NF + f
                            dve.wait_ge(raw_done, k + 1)
                            dve.wait_ge(rotated_done, k + 1)
                            i = f % 2
                            nc.vector.tensor_tensor(by_cos[i][:, :], raw[i][:, :], table[:, 0, now], ALU.mult)
                            nc.vector.tensor_tensor(by_sin[i][64:P, :], raw[i][0:64, :], table[0:64, 1, now], ALU.mult)
                            nc.vector.tensor_tensor(by_sin[i][0:64, :], raw[i][64:P, :], table[64:P, 1, now],
                                                    ALU.mult).then_inc(parts_done, 1)
                            if f:
                                split_rotated(s, f - 1)
                        for t in range(TT):
                            use = s * (NF + TT) + NF + t
                            dve.wait_ge(projected, PROJ0 + r * 2 * (NF + TT) + use + 1)
                            bank = PROJ[use % 4]
                            if t == 0:
                                dve.wait_ge(v_stored[s], 16 * r + 16)
                            nc.vector.scalar_tensor_tensor(
                                vst[s][:, :, t * HD:(t + 1) * HD],
                                bank[:, 0:NV].rearrange("p (g d) -> p g d", d=HD), 1.0 / WS,
                                bv[:, 0:NV].rearrange("p (g d) -> p g d", d=HD), ALU.mult, ALU.add)
                            nc.vector.scalar_tensor_tensor(natural[:, r * 2 * TT + s * TT + t, :], bank[:, NV:NV + NAT],
                                                           1.0 / WS, bv[:, NV:NV + NAT], ALU.mult,
                                                           ALU.add).then_inc(v_done, 1)
                            if t == 0:
                                split_rotated(s, NF - 1)

        @block.tensor
        def _(pe):
            pe.sem_inc(turned, TURNED0)
            pe.sem_inc(projected, PROJ0)
            pe.wait_ge(c_ready, 8)
            pe.wait_ge(w_lo_done, len(pieces))
            with pe.Fori(0, B) as b:
                with pe.Fori(0, 2) as rr:
                    r = b * 2 + rr

                    def turn(s, k):
                        if k == 0:
                            pe.wait_ge(xn_done, r * 2 * TT + (s + 1) * TT)
                        pe.wait_ge(xt_lo_done, r * 2 * KC + s * KC + k + 1)
                        for t in range(TT):
                            last = nc.tensor.transpose(TURN[k % 2][:, t * P:(t + 1) * P],
                                                       xin[:, t, k * P:(k + 1) * P], ident32[:, :])
                        last.then_inc(turned, 1)

                    for k in range(KC):
                        turn(0, k)
                    for s in range(2):
                        wait_xt(pe, r, s)
                        for i in range(NF + TT):
                            if s == 0 and TURN_AT <= i < NF:
                                turn(1, i - TURN_AT)
                            use = s * (NF + TT) + i
                            if i < 4:
                                pe.wait_ge(v_done, (2 * r + s) * TT + i + 1)
                            else:
                                pe.wait_ge(raw_done, (2 * r + s) * NF + i - 3)
                            for k in range(KC):
                                if i < NF:
                                    cols = slice(i * P, (i + 1) * P)
                                    pairs = ((w1_hi[:, k, cols], xt_hi[s][:, k, :]), (w1_hi[:, k, cols], xt_lo[s][:, k, :]),
                                             (w1_lo[:, k, cols], xt_hi[s][:, k, :]))
                                    dst = PROJ[use % 4][:, :]
                                else:
                                    toks = slice((i - NF) * P, (i - NF + 1) * P)
                                    pairs = ((xt_hi[s][:, k, toks], w1_hi[:, k, NQK:W1N]), (xt_hi[s][:, k, toks], w1_lo[:, k, NQK:W1N]),
                                             (xt_lo[s][:, k, toks], w1_hi[:, k, NQK:W1N]))
                                    dst = PROJ[use % 4][:, 0:NV + NAT]
                                for m, (stay, move) in enumerate(pairs):
                                    last = nc.tensor.matmul(dst, stay, move, start=(k == 0 and m == 0),
                                                            stop=(k == KC - 1 and m == 2))
                            last.then_inc(projected, 1)


def route(nc, limes, limes_t, adapter_out, b_ffn, natural, ident32, pair_odd, zstack, bstack, banks):
    NTOK = B * NT
    with ExitStack() as ctx:
        def sb(name, shape, dt):
            return ctx.enter_context(nc.sbuf_tensor(name, shape, dt))

        def sem(name):
            return ctx.enter_context(nc.semaphore(name))

        lim = sb("lim", [E, RANK], F32)
        lim_t = sb("lim_t", [RANK, E], F32)
        z_t = sb("z_t", [RANK, STEPS, TG], F32)
        both = sb("both", [P, 2, NTOK * E], F32)
        tops = sb("tops", [P, 2], F32)
        top_all = sb("top_all", [P, 2], F32)
        half_inv = sb("half_inv", [P, 2], F32)
        u = sb("u", [P, NTOK * E], F32)
        logits = sb("logits", [P, NTOK, E], F32)
        work = sb("work", [P, NTOK, E], F32)
        probs = sb("probs", [P, NTOK, E], F32)
        equal = sb("equal", [P, NTOK, E], F32)
        m1 = sb("m1", [P, NTOK], F32)
        m2 = sb("m2", [P, NTOK], F32)
        ties = sb("ties", [P, NTOK], F32)
        weights = sb("weights", [P, NTOK, E], F32)
        w_t = sb("w_t", [E, STEPS, TG], F32)
        zp = sb("zp", [RANK, 2, TG], F32)
        amat = sb("amat", [RANK, D], F32)
        brow = sb("brow", [1, D], F32)
        rest = sb("rest", [1, 2, D], F32)
        bparts = sb("bparts", [1, 3, D], F16)

        loaded = sem("loaded")
        b_steps = sem("b_steps")
        b_placed = sem("b_placed")
        pe_step = sem("pe_step")
        act_step = sem("act_step")
        dve_step = sem("dve_step")
        reduced = sem("reduced")
        mixed = sem("mixed")
        zstacked = sem("zstacked")

        block = ctx.enter_context(nc.Block())

        @block.sync
        def _(sp):
            sp.dma_start(lim[:, :], limes).then_inc(loaded, 16)
            sp.dma_start(lim_t[:, :], limes_t).then_inc(loaded, 16)
            sp.dma_start(amat[:, :], adapter_out).then_inc(loaded, 16)
            sp.dma_start(brow[:, :], b_ffn).then_inc(loaded, 16)
            sp.wait_ge(b_steps, 5)
            for i in range(3):
                sp.dma_start(bstack[3 * RANK + i:3 * RANK + i + 1, :], bparts[0:1, i, :]).then_inc(b_placed, 16)
            sp.wait_ge(b_placed, 48)

        @block.tensor
        def _(pe):
            pe.wait_ge(loaded, 64)
            for i in range(STEPS):
                for t in range(TG // P):
                    last = nc.tensor.matmul(banks[i][0:RANK, t * P:(t + 1) * P], natural[:, i * 4 + t, E:NAT],
                                            ident32[:, :], start=(t == 0), stop=(t == 3))
                last.then_inc(pe_step, 1)
            pe.wait_ge(act_step, STEPS)
            for t in range(NTOK):
                last = nc.tensor.matmul(banks[0][:, t * E:(t + 1) * E], z_t[:, t // 4, (t % 4) * P:(t % 4 + 1) * P],
                                        lim_t[:, :], start=(t == 0), stop=(t == NTOK - 1))
            last.then_inc(pe_step, 1)
            pe.wait_ge(dve_step, 2)
            nc.tensor.matmul(banks[1][:, :], pair_odd[:, :], both[:, :, :].rearrange("p a n -> p (a n)"),
                             start=True, stop=True).then_inc(pe_step, 1)
            pe.wait_ge(mixed, 1)
            for i in range(STEPS):
                for t in range(TG // P):
                    last = nc.tensor.matmul(banks[i][0:E, t * P:(t + 1) * P], weights[:, i * 4 + t, :],
                                            ident32[:, :], start=(t == 0), stop=(t == 3))
                last.then_inc(pe_step, 1)
            for i in range(STEPS):
                pe.wait_ge(act_step, STEPS + 3 + i)
                nc.tensor.matmul(banks[i][0:RANK, :], lim[:, :], w_t[:, i, :], start=True,
                                 stop=True).then_inc(pe_step, 1)

        @block.scalar
        def _(act):
            for i in range(STEPS):
                act.wait_ge(pe_step, i + 1)
                nc.scalar.activation(z_t[:, i, :], banks[i][0:RANK, :], ACT.Copy).then_inc(act_step, 1)
            act.wait_ge(reduced, 1)
            nc.scalar.activation(work[:, :, :], work[:, :, :], ACT.Exp).then_inc(act_step, 1)
            act.wait_ge(reduced, 2)
            nc.scalar.activation(logits[:, :, :], equal[:, :, :], ACT.Exp, scale=-2.0).then_inc(act_step, 1)
            for i in range(STEPS):
                act.wait_ge(pe_step, STEPS + 2 + i + 1)
                nc.scalar.activation(w_t[:, i, :], banks[i][0:E, :], ACT.Copy).then_inc(act_step, 1)

        @block.gpsimd
        def _(pool):
            pool.wait_ge(dve_step, 3)
            nc.gpsimd.partition_all_reduce(top_all[:, :], tops[:, :], P, RMAX).then_inc(zstacked, 1)

        @block.vector
        def _(dve):
            count = [0]

            def step(ins):
                count[0] += 1
                ins.then_inc(b_steps, 1)
                dve.wait_ge(b_steps, count[0])

            def wide(t):
                return t[:, :].unsqueeze(2).to_broadcast([P, NTOK, E])

            dve.wait_ge(loaded, 64)
            step(nc.vector.tensor_copy(bparts[:, 0, :], brow[:, :]))
            step(nc.vector.tensor_tensor(rest[:, 0, :], brow[:, :], bparts[:, 0, :], ALU.subtract))
            step(nc.vector.tensor_copy(bparts[:, 1, :], rest[:, 0, :]))
            step(nc.vector.tensor_tensor(rest[:, 1, :], rest[:, 0, :], bparts[:, 1, :], ALU.subtract))
            step(nc.vector.tensor_copy(bparts[:, 2, :], rest[:, 1, :]))
            step(nc.vector.tensor_scalar(bstack[0:RANK, :], amat[:, :], WS, None, ALU.mult))
            nc.vector.tensor_scalar(bstack[RANK:2 * RANK, :], amat[:, :], WS, None, ALU.mult)
            nc.vector.scalar_tensor_tensor(bstack[2 * RANK:3 * RANK, :], amat[:, :], WS, bstack[0:RANK, :],
                                           ALU.mult, ALU.subtract)
            nc.vector.memset(zstack[3 * RANK:ZROWS, :], ONES_ROW)
            nc.vector.tensor_copy(both[:, 0, :].rearrange("p (t e) -> p t e", e=E), natural[:, :, 0:E]).then_inc(dve_step, 1)
            dve.wait_ge(pe_step, STEPS + 1)
            nc.vector.tensor_copy(both[:, 1, :], banks[0][:, 0:NTOK * E]).then_inc(dve_step, 1)
            dve.wait_ge(pe_step, STEPS + 2)
            nc.vector.tensor_reduce(tops[:, :], banks[1][:, :].rearrange("p (a n) -> p a n", a=2), AX.X, ALU.max,
                                    apply_absolute_value=True).then_inc(dve_step, 1)
            dve.wait_ge(zstacked, 1)
            step(nc.vector.tensor_scalar(top_all[:, :], top_all[:, :], SCALE_EPS, None, ALU.max))
            step(nc.vector.reciprocal(half_inv[:, :], top_all[:, :]))
            step(nc.vector.tensor_scalar(half_inv[:, :], half_inv[:, :], 0.5, None, ALU.mult))
            step(nc.vector.tensor_scalar(u[:, :], banks[1][:, 0:NTOK * E], half_inv[:, 0:1], None, ALU.mult))
            step(nc.vector.scalar_tensor_tensor(logits[:, :, :].rearrange("p t e -> p (t e)"),
                                                banks[1][:, NTOK * E:2 * NTOK * E], half_inv[:, 1:2], u[:, :],
                                                ALU.mult, ALU.add))
            step(nc.vector.tensor_reduce(m1[:, :], logits[:, :, :], AX.X, ALU.max))
            nc.vector.tensor_tensor(work[:, :, :], logits[:, :, :], wide(m1), ALU.subtract).then_inc(reduced, 1)
            dve.wait_ge(act_step, STEPS + 1)
            step(nc.vector.tensor_reduce(m2[:, :], work[:, :, :], AX.X, ALU.add))
            step(nc.vector.reciprocal(m2[:, :], m2[:, :]))
            step(nc.vector.tensor_tensor(probs[:, :, :], work[:, :, :], wide(m2), ALU.mult))
            step(nc.vector.tensor_reduce(m1[:, :], probs[:, :, :], AX.X, ALU.max))
            step(nc.vector.tensor_tensor(equal[:, :, :], probs[:, :, :], wide(m1), ALU.is_equal))
            step(nc.vector.tensor_reduce(ties[:, :], equal[:, :, :], AX.X, ALU.add))
            step(nc.vector.scalar_tensor_tensor(work[:, :, :].rearrange("p t e -> p (t e)"),
                                                equal[:, :, :].rearrange("p t e -> p (t e)"), -2.0,
                                                probs[:, :, :].rearrange("p t e -> p (t e)"), ALU.mult, ALU.add))
            step(nc.vector.tensor_reduce(m2[:, :], work[:, :, :], AX.X, ALU.max))
            step(nc.vector.tensor_scalar(ties[:, :], ties[:, :], 2.0, None, ALU.is_ge))
            step(nc.vector.tensor_tensor(ties[:, :], ties[:, :], m1[:, :], ALU.mult))
            step(nc.vector.tensor_tensor(m2[:, :], m2[:, :], ties[:, :], ALU.max))
            nc.vector.tensor_tensor(equal[:, :, :], probs[:, :, :], wide(m2), ALU.subtract).then_inc(reduced, 1)
            dve.wait_ge(act_step, STEPS + 2)
            step(nc.vector.tensor_scalar(logits[:, :, :], logits[:, :, :], 1.0, None, ALU.add))
            step(nc.vector.reciprocal(logits[:, :, :], logits[:, :, :]))
            step(nc.vector.tensor_tensor(work[:, :, :], probs[:, :, :], logits[:, :, :], ALU.mult))
            step(nc.vector.tensor_reduce(m1[:, :], work[:, :, :], AX.X, ALU.add))
            step(nc.vector.tensor_scalar(m1[:, :], m1[:, :], 1e-9, None, ALU.add))
            step(nc.vector.reciprocal(m1[:, :], m1[:, :]))
            nc.vector.tensor_tensor(weights[:, :, :], work[:, :, :], wide(m1), ALU.mult).then_inc(mixed, 1)
            for i in range(STEPS):
                dve.wait_ge(pe_step, 2 * STEPS + 2 + i + 1)
                toks = slice(i * TG, (i + 1) * TG)
                step(nc.vector.scalar_tensor_tensor(zp[:, i % 2, :], banks[i][0:RANK, :], ALPHA_OVER_RANK,
                                                    z_t[:, i, :], ALU.mult, ALU.mult))
                step(nc.vector.tensor_copy(zstack[0:RANK, toks], zp[:, i % 2, :]))
                nc.vector.tensor_copy(zstack[2 * RANK:3 * RANK, toks], zp[:, i % 2, :])
                nc.vector.tensor_tensor(zstack[RANK:2 * RANK, toks], zp[:, i % 2, :], zstack[0:RANK, toks], ALU.subtract)
            nc.vector.tensor_copy(m1[:, :], m2[:, :]).then_inc(mixed, 1)
            dve.wait_ge(mixed, 2)


def attend(nc, q_parts, k_parts, v_parts, ctx_parts, w_out, w_hi, w_lo, ident16, ident_bf,
           mask_q, mask_k, mask_early, mask_late, banks):
    order, lead = attention_order()
    UNITS = len([1 for o in order if o[0] == "values"])
    BANKS = len([1 for o in order if o[0] in ("bank", "row")])
    LEAD_BANKS = len([1 for k, _ in lead if k in ("bank", "row")])
    LEAD_ROWS = len([1 for k, _ in lead if k == "row"])
    LEAD_FOLDS = len([1 for k, _ in lead if k == "fold"])
    SUMS = [o for o in order if o[0] == "sums"]
    ADDS = [o for o in SUMS if o[4][1] is not None]
    STEPS2 = GROUPS // 2
    with ExitStack() as ctx:
        def sb(name, shape, dt):
            return ctx.enter_context(nc.sbuf_tensor(name, shape, dt))

        def sem(name):
            return ctx.enter_context(nc.semaphore(name))

        q_stack = [sb(f"q_stack{i}", [STACK + 1, QH, S], F16) for i in range(2)]
        k_stack = [sb(f"k_stack{i}", [STACK + 1, S], F16) for i in range(2)]
        v_slot = [sb(f"v_slot{i}", [P, NT, HD], F32) for i in range(2)]
        ones = sb("ones", [P, HD], F32)
        partial = [sb(f"partial{i}", [P, NCH, 3, QH * (TG // P)], F32) for i in range(2)]
        top = [sb(f"top{i}", [P, NCH, QH * (TG // P)], F32) for i in range(2)]
        shift = [sb(f"shift{i}", [P, NCH, QH * (TG // P)], F16) for i in range(2)]
        shift_row = [sb(f"shift_row{i}", [QH * (TG // P), P], F16) for i in range(2)]
        probs = [sb(f"probs{i}", [P, QH, TG], F32) for i in range(PROBRING)]
        pair = [sb(f"pair{i}", [P, QH, TG], F32) for i in range(ADDRING)]
        total = [sb(f"total{i}", [P, TG], F32) for i in range(2)]
        context = [sb(f"context{i}", [P, TG], F32) for i in range(2)]
        scaled = sb("scaled", [P, TG], F32)
        c_hi = [sb(f"c_hi{i}", [P, TG], F16) for i in range(2)]
        c_lo = [sb(f"c_lo{i}", [P, TG], F16) for i in range(2)]
        wst = sb("wst", [P, D], F32)

        MAXB, SCOREB, CTXB, SUMB = banks[0:3], banks[3:6], banks[6], banks[7]

        qk_loaded = [sem(f"qk_loaded{i}") for i in range(2)]
        set_up = sem("set_up")
        max_full = sem("max_full")
        max_read = sem("max_read")
        folded = sem("folded")
        shift_done = sem("shift_done")
        row_placed = [sem(f"row_placed{i}") for i in range(2)]
        score_full = sem("score_full")
        prob_done = sem("prob_done")
        values_done = sem("values_done")
        pair_added = sem("pair_added")
        summed = sem("summed")
        total_out = sem("total_out")
        context_out = sem("context_out")
        inverted = sem("inverted")
        scaled_done = sem("scaled_done")
        c_lo_done = sem("c_lo_done")
        c_stored = [sem(f"c_stored{i}") for i in range(2)]
        wst_loaded = sem("wst_loaded")
        wst_hi = sem("wst_hi")
        wst_lo = sem("wst_lo")

        TILES = TG // P

        MAX0 = MAXRING
        PROB0 = SCORERING
        VAL0 = PROBRING
        CTX0 = 2
        PLACED = 16 * QH
        ROW0 = PLACED
        ONE0 = 1

        def group_of(r, g):
            return r * 2 + g

        def load_group(eng, slot, n):
            q = q_stack[slot]
            k = k_stack[slot]
            for row, part in enumerate((0, 1, 0)):
                for a in range(2):
                    at = row * HD + a * HALF
                    eng.dma_start(q[at:at + HALF, :, :],
                                  q_parts[part, n, a * QH * HALF:(a + 1) * QH * HALF, :].rearrange("(h r) t -> r h t", r=HALF)
                                  ).then_inc(qk_loaded[slot], 16)
            for row, part in enumerate((0, 0, 1)):
                eng.dma_start(k[row * HD:(row + 1) * HD, :], k_parts[part, n]).then_inc(qk_loaded[slot], 16)
            eng.dma_start(v_slot[slot][:, :, :].rearrange("p t d -> p (t d)"), v_parts[n]).then_inc(qk_loaded[slot], 16)

        LOADS = 10 * 16

        def unit_end(s, c):
            return sum(len(key_units(i)) for i in range(NCH)) * s + sum(len(key_units(i)) for i in range(c + 1))

        def prob_slot(unit):
            return unit % PROBRING

        def first_unit(s, c):
            return unit_end(s, c) - len(key_units(c))

        def sums_before(s, c):
            return len([1 for o in SUMS if (o[1], o[2]) < (s, c)])

        def freed_by(unit):
            adds = sums = 0
            before = unit - PROBRING
            a = 0
            for n, (_, s, c, _, (members, added, direct), _) in enumerate(SUMS):
                a += added is not None
                if before >= 0 and before in [first_unit(s, c) + m for m in members]:
                    if added is not None:
                        adds = a
                    if before in [first_unit(s, c) + m for m, _, _ in direct]:
                        sums = n + 1
            return adds, sums

        block = ctx.enter_context(nc.Block())

        @block.sync
        def _(sp):
            w_v = w_out.rearrange("(m p) d -> m p d", p=P)

            def load_weights(r, i):
                sp.wait_ge(wst_lo, ONE0 + 2 * r + i)
                sp.dma_start(wst[:, :], w_v[r * 2 + i]).then_inc(wst_loaded, 16)

            def store(r, s, c):
                k = (s * NCH + c) % 2
                sp.wait_ge(c_lo_done, CTX0 + r * 2 * NCH + s * NCH + c + 1)
                for part, half in enumerate((c_hi, c_lo)):
                    sp.dma_start(ctx_parts[part, group_of(r, s), c], half[k][:, :]).then_inc(c_stored[k], 16)

            def place_row(r, k, n, c, slot):
                sp.wait_ge(max_read, MAX0 + r * BANKS + k + 1)
                for h in range(QH):
                    sp.dma_start(q_stack[slot][STACK:STACK + 1, h, c * TG:(c + 1) * TG],
                                 shift_row[n % 2][h * TILES:(h + 1) * TILES, :]).then_inc(row_placed[n % 2], 16)

            load_group(sp, 0, 0)
            k = n = 0
            for kind, m in lead:
                if kind == "row":
                    place_row(0, k, n, m, 0)
                    n += 1
                k += kind != "fold"
            with sp.Fori(0, STEPS2) as r:
                sp.wait_ge(values_done, VAL0 + r * UNITS)
                load_group(sp, 1, r * 2 + 1)
                load_weights(r, 0)
                k, n = LEAD_BANKS, LEAD_ROWS
                for o in order:
                    if o[0] == "row":
                        place_row(r, k, n, o[2], o[1] % 2)
                        n += 1
                    if o[0] in ("bank", "row"):
                        k += 1
                    if o[0] == "split":
                        _, s, c = o
                        if s * NCH + c:
                            store(r, (s * NCH + c - 1) // NCH, (s * NCH + c - 1) % NCH)
                    if o[0] == "context":
                        _, s, c = o
                        if (s, c) == (0, 2):
                            load_weights(r, 1)
                        if (s, c) == (0, NCH - 1):
                            sp.wait_ge(values_done, VAL0 + r * UNITS + UNITS // 2)
                            load_group(sp, 0, r * 2 + 2)
                store(r, 1, NCH - 1)
            sp.wait_ge(qk_loaded[0], LOADS * (STEPS2 + 1))
            for i in range(2):
                sp.wait_ge(row_placed[i], ROW0 + PLACED * (GROUPS * NCH // 2 + (LEAD_ROWS + 1 - i) // 2))
            for i in range(2):
                sp.wait_ge(c_stored[i], 32 + 32 * GROUPS * NCH // 2)

        @block.gpsimd
        def _(pool):
            for i in range(2):
                nc.gpsimd.memset(k_stack[i][STACK:STACK + 1, :], SHIFT).then_inc(set_up, 1)
            pool.sem_inc(pair_added, ONE0)
            pool.sem_inc(c_lo_done, CTX0)
            pool.sem_inc(c_stored[0], 32)
            pool.sem_inc(c_stored[1], 32)

            def split(r, s, c):
                k = (s * NCH + c) % 2
                n = r * 2 * NCH + s * NCH + c + 1
                pool.wait_ge(context_out, CTX0 + n)
                pool.wait_ge(c_stored[k], 32 + r * 32 * NCH + 32 * ((s * NCH + c) // 2))
                pool.wait_ge(c_lo_done, CTX0 + n - 1)
                pool.wait_ge(inverted, r * 2 * NCH * TILES + (s * NCH + c + 1) * TILES)
                nc.gpsimd.tensor_tensor(c_hi[k][:, :], context[k][:, :], total[k][:, :], ALU.mult)
                nc.gpsimd.tensor_tensor(scaled[:, :], context[k][:, :], total[k][:, :], ALU.mult).then_inc(scaled_done, 1)
                pool.wait_ge(scaled_done, n)
                nc.gpsimd.tensor_tensor(c_lo[k][:, :], scaled[:, :], c_hi[k][:, :],
                                        ALU.subtract).then_inc(c_lo_done, 1)

            def add(r, a):
                _, s, c, n, (members, (start, width), _), _ = ADDS[a]
                at = [(key_units(c)[m][1] - c * (TG // BLK)) * BLK for m in members]
                units = [first_unit(s, c) + m for m in members]
                pool.wait_ge(prob_done, PROB0 + r * QH * UNITS + (units[1] + 1) * QH)
                pool.wait_ge(summed, ONE0 + r * len(SUMS) + (SUMS.index(ADDS[a - ADDRING]) + 1 if a >= ADDRING else 0))
                first, second = (probs[prob_slot(u)][:, :, start - x:start - x + width] for u, x in zip(units, at))
                nc.gpsimd.tensor_tensor(pair[a % ADDRING][:, :, 0:width], first, second, ALU.add).then_inc(pair_added, 1)

            with pool.Fori(0, STEPS2) as r:
                a = unit = 0
                for o in order:
                    if o[0] == "scores" and o[5] == QH - 1:
                        unit += 1
                        if a < len(ADDS):
                            _, s, c, _, (members, _, _), _ = ADDS[a]
                            if first_unit(s, c) + members[1] + 1 == unit:
                                add(r, a)
                                a += 1
                    elif o[0] == "split":
                        split(r, o[1], o[2])

        @block.scalar
        def _(act):
            act.sem_inc(prob_done, PROB0)
            act.sem_inc(context_out, CTX0)
            act.sem_inc(total_out, ONE0)
            with act.Fori(0, STEPS2) as r:
                k = 0
                unit = -1
                for o in order:
                    if o[0] == "scores":
                        _, s, c, i, (j, lo, n, diagonal, far), h = o
                        if h == 0:
                            unit += 1
                            act.wait_ge(values_done, r * UNITS + max(unit + 1, VAL0))
                            adds, sums = freed_by(unit)
                            if adds or unit < PROBRING:
                                act.wait_ge(pair_added, ONE0 + r * len(ADDS) + adds)
                            if sums or unit < PROBRING:
                                act.wait_ge(summed, ONE0 + r * len(SUMS) + sums)
                        act.wait_ge(score_full, r * QH * UNITS + k + 1)
                        nc.scalar.activation(probs[prob_slot(unit)][:, h, 0:BLK * n], SCOREB[k % SCORERING][:, 0:BLK * n],
                                             ACT.Exp, scale=SM_SCALE).then_inc(prob_done, 1)
                        k += 1
                    elif o[0] == "context":
                        _, s, c = o
                        q = s * NCH + c
                        act.wait_ge(values_done, VAL0 + r * UNITS + unit_end(s, c))
                        act.wait_ge(c_lo_done, r * 2 * NCH + q + 1)
                        nc.scalar.activation(context[q % 2][:, :], CTXB[:, :], ACT.Copy).then_inc(context_out, 1)
                        if q in (1, 5):
                            i = q // 4
                            act.wait_ge(wst_loaded, 32 * r + 16 * i + 16)
                            nc.scalar.activation(w_hi[:, r * 2 + i, :], wst[:, :], ACT.Copy,
                                                 scale=WS).then_inc(wst_hi, 1)
                    elif o[0] == "totals":
                        _, s, c = o
                        q = s * NCH + c
                        act.wait_ge(summed, ONE0 + r * len(SUMS) + sums_before(s, c) + len(sum_groups(c)))
                        act.wait_ge(c_lo_done, r * 2 * NCH + q + 1)
                        nc.scalar.activation(total[q % 2][:, :], SUMB[:, :], ACT.Copy,
                                             scale=1.0 / CS).then_inc(total_out, 1)

        @block.vector
        def _(dve):
            for i in range(2):
                nc.vector.memset(partial[i][:, :, :, :], LOWEST).then_inc(set_up, 1)
            nc.vector.memset(ones[:, :], 1.0).then_inc(set_up, 1)
            dve.sem_inc(max_read, MAX0)
            dve.sem_inc(wst_lo, ONE0)
            dve.wait_ge(set_up, 5)

            def take(r, k, bank, slot):
                t, c = bank["t"], bank["t"] // TILES
                heads = bank["heads"]
                w = sum(x for _, x in bank["pieces"])
                dve.wait_ge(max_full, r * BANKS + k + 1)
                dst = partial[slot][:, c, bank["seg"], heads[0] * TILES + t % TILES:heads[-1] * TILES + t % TILES + 1:TILES]
                src = MAXB[k % MAXRING][:, 0:len(heads) * w].rearrange("p (h w) -> p h w", w=w)
                nc.vector.tensor_reduce(dst, src, AX.X, ALU.max).then_inc(max_read, 1)

            def fold(r, k, c, slot, n):
                dve.wait_ge(max_read, MAX0 + r * BANKS + k)
                nc.vector.tensor_reduce(top[slot][:, c, :], partial[slot][:, c, :, :].rearrange("p s n -> p n s"),
                                        AX.X, ALU.max).then_inc(folded, 1)
                dve.wait_ge(folded, r * 2 * NCH + n + 1)
                nc.vector.tensor_scalar(shift[slot][:, c, :], top[slot][:, c, :], -1.0 / SHIFT, None,
                                        ALU.mult).then_inc(shift_done, 1)

            def row(r, k, n):
                dve.wait_ge(max_full, r * BANKS + k + 1)
                dve.wait_ge(row_placed[n % 2], PLACED * (NCH * r + n // 2) + ROW0)
                nc.vector.tensor_copy(shift_row[n % 2][:, :], MAXB[k % MAXRING][0:QH * TILES, 0:P]).then_inc(max_read, 1)

            dve.sem_inc(row_placed[0], ROW0)
            dve.sem_inc(row_placed[1], ROW0)

            k = n = f = 0
            for kind, m in lead:
                if kind == "bank":
                    take(0, k, m, 0)
                    k += 1
                elif kind == "fold":
                    fold(0, k, m, 0, f)
                    f += 1
                else:
                    row(0, k, n)
                    n += 1
                    k += 1
            with dve.Fori(0, STEPS2) as r:
                k, n, f = LEAD_BANKS, LEAD_ROWS, LEAD_FOLDS
                for o in order:
                    if o[0] == "bank":
                        take(r, k, o[2], o[1] % 2)
                        k += 1
                    elif o[0] == "fold":
                        fold(r, k, o[2], o[1] % 2, f)
                        f += 1
                    elif o[0] == "row":
                        row(r, k, n)
                        n += 1
                        k += 1
                    elif o[0] == "invert":
                        _, s, c, piece = o
                        q = s * NCH + c
                        now = slice(piece * P, (piece + 1) * P)
                        if piece == 0:
                            dve.wait_ge(total_out, ONE0 + r * 2 * NCH + q + 1)
                        nc.vector.reciprocal(total[q % 2][:, now], total[q % 2][:, now]).then_inc(inverted, 1)
                        if piece == 0 and q in (1, 5):
                            i = q // 4
                            dve.wait_ge(wst_hi, 2 * r + i + 1)
                            nc.vector.scalar_tensor_tensor(w_lo[:, r * 2 + i, :], wst[:, :], WS, w_hi[:, r * 2 + i, :],
                                                           ALU.mult, ALU.subtract).then_inc(wst_lo, 1)

        @block.tensor
        def _(pe):
            pe.sem_inc(values_done, VAL0)
            pe.sem_inc(summed, ONE0)
            pe.wait_ge(set_up, 5)

            def wait_max_bank(r, k):
                if isinstance(r, int):
                    if k >= MAXRING:
                        pe.wait_ge(max_read, k + 1)
                else:
                    pe.wait_ge(max_read, r * BANKS + max(k + 1, LEAD_BANKS + MAX0))

            def max_bank(r, k, bank, slot):
                dst = MAXB[k % MAXRING]
                wait_max_bank(r, k)
                t = bank["t"]
                w = sum(x for _, x in bank["pieces"])
                first = True
                mms = []
                for i, h in enumerate(bank["heads"]):
                    at = i * w
                    for start, width in bank["pieces"]:
                        mms.append((dst[:, at:at + width], q_stack[slot][0:STACK, h, t * P:(t + 1) * P],
                                    k_stack[slot][0:STACK, start:start + width]))
                        at += width
                whole = dst[:, 0:len(bank["heads"]) * w].rearrange("p (h w) -> p h w", w=w)
                if bank["mask"] == "diagonal":
                    mms.append((whole[:, :, w - P:w], ident_bf[:, :],
                                mask_q[:, :].unsqueeze(1).to_broadcast([P, len(bank["heads"]), P])))
                elif bank["mask"] == "late queries":
                    mms.append((whole[:, :, 0:BLK], ident_bf[:, :],
                                mask_late[:, :].unsqueeze(1).to_broadcast([P, QH, BLK])))
                for m, (o, a, b) in enumerate(mms):
                    last = nc.tensor.matmul(o, a, b, start=(m == 0), stop=(m == len(mms) - 1), skip_group_check=True)
                last.then_inc(max_full, 1)

            def max_row(r, k, n, c, slot):
                wait_max_bank(r, k)
                pe.wait_ge(shift_done, r * 2 * NCH + n + 1)
                nc.tensor.matmul(MAXB[k % MAXRING][0:QH * TILES, 0:P], shift[slot][:, c, :], ident16[:, :], start=True,
                                 stop=True).then_inc(max_full, 1)

            def scores(r, k, s, u, h):
                j, lo, n, diagonal, far = u
                dst = SCOREB[k % SCORERING]
                pe.wait_ge(prob_done, r * QH * UNITS + max(k + 1, PROB0))
                mms = [(dst[:, 0:BLK * n], k_stack[s][:, j * P:(j + 1) * P], q_stack[s][:, h, lo * BLK:(lo + n) * BLK])]
                if diagonal:
                    mms.append((dst[:, 0:P], ident_bf[:, :], mask_k[:, :]))
                if far:
                    mms.append((dst[:, BLK * (n - far):BLK * n].rearrange("p (a w) -> p a w", w=BLK), ident_bf[:, :],
                                mask_early[:, :].unsqueeze(1).to_broadcast([P, far, BLK])))
                for m, (o, a, b) in enumerate(mms):
                    last = nc.tensor.matmul(o, a, b, start=(m == 0), stop=(m == len(mms) - 1), skip_group_check=True)
                last.then_inc(score_full, 1)

            def products(r, unit, s, c, i, u, last_of_chunk):
                j, lo, n, diagonal, far = u
                at = (lo - c * (TG // BLK)) * BLK
                pe.wait_ge(prob_done, PROB0 + r * QH * UNITS + (unit + 1) * QH)
                if i == 0:
                    pe.wait_ge(context_out, CTX0 + r * 2 * NCH + s * NCH + c)
                for h in range(QH):
                    last = nc.tensor.matmul(CTXB[h * HD:(h + 1) * HD, at:at + BLK * n], v_slot[s][:, j, :],
                                            probs[prob_slot(unit)][:, h, 0:BLK * n], start=(i == 0),
                                            stop=last_of_chunk, skip_group_check=True, tile_position=(0, h * HD))
                last.then_inc(values_done, 1)

            def sums(r, a, s, c, n, group, last_of_chunk):
                members, added, direct = group
                if n == 0:
                    pe.wait_ge(total_out, ONE0 + r * 2 * NCH + s * NCH + c)
                if direct:
                    pe.wait_ge(prob_done, PROB0 + r * QH * UNITS + (first_unit(s, c) + members[-1] + 1) * QH)
                if added is not None:
                    pe.wait_ge(pair_added, ONE0 + r * len(ADDS) + a + 1)
                pieces = [] if added is None else [(pair[a % ADDRING], 0, *added)]
                for m, start, width in direct:
                    at = (key_units(c)[m][1] - c * (TG // BLK)) * BLK
                    pieces.append((probs[prob_slot(first_unit(s, c) + m)], start - at, start, width))
                for x, (src, at, start, width) in enumerate(pieces):
                    for h in range(QH):
                        last = nc.tensor.matmul(SUMB[h * HD:(h + 1) * HD, start:start + width], ones[:, :],
                                                src[:, h, at:at + width], start=(n == 0 and x == 0),
                                                stop=last_of_chunk and x == len(pieces) - 1,
                                                skip_group_check=True, tile_position=(0, h * HD))
                last.then_inc(summed, 1)

            pe.wait_ge(qk_loaded[0], LOADS)
            k = n = 0
            for kind, m in lead:
                if kind == "bank":
                    max_bank(0, k, m, 0)
                    k += 1
                elif kind == "row":
                    max_row(0, k, n, m, 0)
                    k += 1
                    n += 1
            with pe.Fori(0, STEPS2) as r:
                k, n = LEAD_BANKS, LEAD_ROWS
                kk = 0
                unit = a = 0
                seen = set()
                for o in order:
                    if o[0] == "bank":
                        if o[1] > 0 and o[1] not in seen:
                            seen.add(o[1])
                            pe.wait_ge(qk_loaded[o[1] % 2], LOADS * r + (LOADS if o[1] == 1 else 2 * LOADS))
                        max_bank(r, k, o[2], o[1] % 2)
                        k += 1
                    elif o[0] == "row":
                        max_row(r, k, n, o[2], o[1] % 2)
                        k += 1
                        n += 1
                    elif o[0] == "scores":
                        _, s, c, i, u, h = o
                        if i == 0 and h == 0:
                            q = s * NCH + c
                            pe.wait_ge(row_placed[q % 2], ROW0 + PLACED * (NCH * r + q // 2 + 1))
                        scores(r, kk, s, u, h)
                        kk += 1
                    elif o[0] == "values":
                        _, s, c, i, u, last = o
                        products(r, unit, s, c, i, u, last)
                        unit += 1
                    elif o[0] == "sums":
                        _, s, c, i, group, last = o
                        sums(r, a, s, c, i, group, last)
                        a += group[1] is not None


def finish(nc, x, xt_parts, ctx_parts, w_hi, w_lo, zstack, bstack, b_out, out, banks):
    TT, NH = TG // P, D // PSUM_BANK
    PAIRS = TT * NH
    with ExitStack() as ctx:
        def sb(name, shape, dt):
            return ctx.enter_context(nc.sbuf_tensor(name, shape, dt))

        def sem(name):
            return ctx.enter_context(nc.semaphore(name))

        xt = [[sb(f"xt{s}_{part}", [P, KC, TG], F16) for part in range(2)] for s in range(2)]
        ct = [[sb(f"ct{s}_{part}", [P, N_KV, TG], F16) for part in range(2)] for s in range(2)]
        xres = [sb(f"xres{s}", [P, TT, D], F32) for s in range(2)]
        bias = sb("bias", [P, D], F32)
        gate = [sb(f"gate{i}", [P, PSUM_BANK], F32) for i in range(2)]
        dense = [sb(f"dense{i}", [P, PSUM_BANK], F32) for i in range(2)]
        gated = [sb(f"gated{i}", [P, PSUM_BANK], F32) for i in range(2)]
        result = [sb(f"result{i}", [P, PSUM_BANK], F32) for i in range(2)]

        GATEB, DENSEB = banks[0:4], banks[4:8]

        bias_loaded = sem("bias_loaded")
        in_loaded = [sem(f"in_loaded{s}") for s in range(2)]
        xres_loaded = [sem(f"xres_loaded{s}") for s in range(2)]
        gate_full = sem("gate_full")
        dense_full = sem("dense_full")
        gate_done = sem("gate_done")
        dense_done = sem("dense_done")
        gated_done = sem("gated_done")
        result_done = sem("result_done")
        stored = [sem(f"stored{i}") for i in range(2)]

        RING4, RING2 = 4, 2
        FULL0 = RESULTS0 = 2 * PAIRS
        LOADS = 16 * (2 + 2 * N_KV)

        block = ctx.enter_context(nc.Block())

        @block.sync
        def _(sp):
            x_v = x.rearrange("(i t p) d -> i p t d", t=TT, p=P)
            sp.dma_start(bias[:, :], b_out.partition_broadcast(P)).then_inc(bias_loaded, 16)
            with sp.Fori(0, B) as b:
                with sp.Fori(0, 2) as rr:
                    r = b * 2 + rr
                    for s in range(2):
                        sp.wait_ge(dense_full, r * 2 * PAIRS + (s + 1) * PAIRS)
                        sp.wait_ge(result_done, r * 2 * PAIRS + (s + 1) * PAIRS)
                        sp.dma_start(xres[s][:, :, :], x_v[r * 2 + s]).then_inc(xres_loaded[s], 16)
                        for part in range(2):
                            sp.dma_start(xt[s][part][:, :, :].rearrange("p k t -> p (k t)"),
                                         xt_parts[part, r * 2 + s]).then_inc(in_loaded[s], 16)
                            for g in range(N_KV):
                                sp.dma_start(ct[s][part][:, g, :],
                                             ctx_parts[part, b * N_KV + g, rr * 2 + s]).then_inc(in_loaded[s], 16)

        @block.gpsimd
        def _(pool):
            pool.sem_inc(result_done, RESULTS0)
            with pool.Fori(0, STEPS // 2) as r:
                for n in range(2 * PAIRS):
                    s, t, half = n // PAIRS, n % PAIRS // NH, n % NH
                    if n % PAIRS == 0:
                        pool.wait_ge(xres_loaded[s], 16 * r + 16)
                    pool.wait_ge(stored[n % 2], 16 + r * 16 * PAIRS + 16 * (n // 2))
                    pool.wait_ge(gated_done, RING2 + r * 2 * PAIRS + n + 1)
                    nc.gpsimd.tensor_tensor(result[n % 2][:, :], gated[n % 2][:, :],
                                            xres[s][:, t, half * PSUM_BANK:(half + 1) * PSUM_BANK],
                                            ALU.add).then_inc(result_done, 1)

        @block.scalar
        def _(act):
            act.sem_inc(gate_done, RING4)
            act.sem_inc(stored[0], 16)
            act.sem_inc(stored[1], 16)
            o_v = out.rearrange("(i t p) d -> i t p d", t=TT, p=P)
            with act.Fori(0, STEPS // 2) as r:

                def store(n):
                    act.wait_ge(result_done, RESULTS0 + r * 2 * PAIRS + n + 1)
                    s, t, half = n // PAIRS, n % PAIRS // NH, n % NH
                    act.dma_start(o_v[r * 2 + s, t][:, half * PSUM_BANK:(half + 1) * PSUM_BANK],
                                  result[n % 2][:, :]).then_inc(stored[n % 2], 16)

                for n in range(2 * PAIRS):
                    act.wait_ge(gate_full, r * 2 * PAIRS + n + 1)
                    act.wait_ge(gated_done, r * 2 * PAIRS + n + 1)
                    nc.scalar.activation(gate[n % 2][:, :], GATEB[n % 4][:, :], ACT.Silu,
                                         scale=1.0 / WS).then_inc(gate_done, 1)
                    if n:
                        store(n - 1)
                store(2 * PAIRS - 1)
            for i in range(2):
                act.wait_ge(stored[i], 16 + 16 * STEPS * PAIRS // 2)

        @block.vector
        def _(dve):
            dve.sem_inc(dense_done, RING4)
            dve.sem_inc(gated_done, RING2)
            dve.wait_ge(bias_loaded, 16)
            with dve.Fori(0, STEPS // 2) as r:
                for n in range(2 * PAIRS):
                    half = n % NH
                    dve.wait_ge(dense_full, FULL0 + r * 2 * PAIRS + n + 1)
                    nc.vector.scalar_tensor_tensor(dense[n % 2][:, :], DENSEB[n % 4][:, :], 1.0 / (WS * CS),
                                                   bias[:, half * PSUM_BANK:(half + 1) * PSUM_BANK],
                                                   ALU.mult, ALU.add).then_inc(dense_done, 1)
                    dve.wait_ge(dense_done, RING4 + r * 2 * PAIRS + n + 1)
                    dve.wait_ge(gate_done, RING4 + r * 2 * PAIRS + n + 1)
                    dve.wait_ge(result_done, RESULTS0 - RING2 + r * 2 * PAIRS + n + 1)
                    nc.vector.tensor_tensor(gated[n % 2][:, :], dense[n % 2][:, :], gate[n % 2][:, :],
                                            ALU.mult).then_inc(gated_done, 1)

        @block.tensor
        def _(pe):
            pe.sem_inc(dense_full, FULL0)
            with pe.Fori(0, STEPS // 2) as r:
                for n in range(2 * PAIRS):
                    s, t, half = n // PAIRS, n % PAIRS // NH, n % NH
                    if n % PAIRS == 0:
                        pe.wait_ge(in_loaded[s], LOADS * r + LOADS)
                    toks = slice(t * P, (t + 1) * P)
                    cols = slice(half * PSUM_BANK, (half + 1) * PSUM_BANK)
                    pe.wait_ge(gate_done, r * 2 * PAIRS + n + 1)
                    for k in range(KC):
                        for m, (part, w) in enumerate(((0, w_hi), (0, w_lo), (1, w_hi))):
                            nc.tensor.matmul(GATEB[n % 4][:, :], xt[s][part][:, k, toks], w[:, KC + k, cols],
                                             start=(k == 0 and m == 0), stop=False)
                    nc.tensor.matmul(GATEB[n % 4][:, :], zstack[0:ZROWS, bass.ds(r * 2 * TG + s * TG + t * P, P)],
                                     bstack[0:ZROWS, cols], start=False, stop=True).then_inc(gate_full, 1)
                    pe.wait_ge(dense_done, r * 2 * PAIRS + n + 1)
                    for k in range(KC):
                        for m, (part, w) in enumerate(((0, w_hi), (0, w_lo), (1, w_hi))):
                            last = nc.tensor.matmul(DENSEB[n % 4][:, :], ct[s][part][:, k, toks], w[:, k, cols],
                                                    start=(k == 0 and m == 0), stop=(k == KC - 1 and m == 2))
                    last.then_inc(dense_full, 1)



def kernel(L0_attn_hidden_states, L0_attn_w_qkv, L0_attn_b_qkv, L0_attn_w_dense, L0_attn_b_dense,
           L0_ffn_W, L0_ffn_b, L0_ffn_A, L0_ffn_Bmat, L0_ffn_LiMEs):
    import numpy as np
    import concourse.bacc as bacc
    from concourse.bass_utils import run_bass_kernel_spmd

    w = np.asarray(L0_attn_w_qkv).reshape(N_KV, QH + 2, 2, HALF, D)
    bias = np.asarray(L0_attn_b_qkv).reshape(N_KV, QH + 2, 2, HALF)
    w_q = w[:, :QH].transpose(0, 2, 1, 3, 4).reshape(N_KV * QH * HD, D)
    b_q = bias[:, :QH].transpose(0, 2, 1, 3).reshape(-1)
    w_k = w[:, QH].reshape(2, N_KV // 2, 2, HALF, D).transpose(0, 2, 1, 3, 4).reshape(N_KV * HD, D)
    b_k = bias[:, QH].reshape(2, N_KV // 2, 2, HALF).transpose(0, 2, 1, 3).reshape(-1)
    w_v = w[:, QH + 1].reshape(NV, D)
    b_v = np.concatenate([bias[:, QH + 1].reshape(-1), np.asarray(L0_ffn_b)[:E], np.zeros(RANK, np.float32)]).reshape(1, -1)
    ffn_w = np.asarray(L0_ffn_W)
    w1 = np.concatenate([w_q.T, w_k.T, w_v.T, ffn_w[:E].T, np.asarray(L0_ffn_A)], axis=1)
    w_out = np.concatenate([np.asarray(L0_attn_w_dense).T, ffn_w.T], axis=0)

    f32 = np.float32
    inv_freq = (1.0 / 1000000.0 ** (np.arange(0, HD, 2) / HD)).astype(f32)
    angle = np.arange(S, dtype=f32)[None, :] * inv_freq[:, None]
    cos, sin = np.cos(angle.astype(np.float64)), np.sin(angle.astype(np.float64))
    rope = np.stack([np.tile(cos, (2 * QH, 1)), np.concatenate([np.tile(sin, (QH, 1)), np.tile(-sin, (QH, 1))])], axis=1)
    i = np.arange(P)
    later = np.where(i[None, :] > i[:, None], NEG, 0.0)
    consts = np.concatenate([np.eye(P), i[:, None] == 2 * (i[None, :] // 2) + 1, later, later.T,
                             np.repeat(np.where(i < BLK, NEG, 0.0)[:, None], BLK, axis=1),
                             np.repeat(np.where(i >= BLK, NEG, 0.0)[:, None], BLK, axis=1)], axis=1)
    arrays = {
        "x": np.asarray(L0_attn_hidden_states).reshape(B * S, D),
        "w1": w1,
        "b_qk": np.concatenate([b_q, b_k]).reshape(NF, P).T,
        "b_v": b_v,
        "w_out": w_out,
        "b_out": np.asarray(L0_attn_b_dense).reshape(1, D),
        "b_ffn": np.asarray(L0_ffn_b).reshape(1, D),
        "adapter_out": np.asarray(L0_ffn_Bmat),
        "limes": np.asarray(L0_ffn_LiMEs),
        "limes_t": np.asarray(L0_ffn_LiMEs).T,
        "rope": rope.astype(f32),
        "consts": consts.astype(f32),
    }
    arrays = {name: np.ascontiguousarray(a) for name, a in arrays.items()}
    nc = bacc.Bacc("TRN2", target_bir_lowering=False, num_devices=1)
    args = [nc.dram_tensor(name, a.shape, F32, kind="ExternalInput").ap() for name, a in arrays.items()]
    out = nc.dram_tensor("out", (B * S, D), F32, kind="ExternalOutput").ap()
    mk_recurrent_d1(nc, *args, out)
    r = run_bass_kernel_spmd(nc, [arrays], core_ids=[0])
    return r.results[0]["out"].reshape(B, S, D)
```

```python
from contextlib import ExitStack

import concourse.bass as bass
from concourse import mybir

ALU = mybir.AluOpType
ACT = mybir.ActivationFunctionType
F32 = mybir.dt.float32
F16 = mybir.dt.float16
BF16 = mybir.dt.bfloat16
AX = mybir.AxisListType
RMAX = bass.bass_isa.ReduceOp.max

P = 128
B, S, D = 2, 2048, 1024
KC = D // P
N_KV, QH, HD = 8, 4, 32
HALF = HD // 2
GROUPS = B * N_KV
TG = 512
STEPS = B * S // TG
E, RANK = 8, 32
NQK = N_KV * (QH + 1) * HD
NF = NQK // P
NV = N_KV * HD
NAT = E + RANK
W1N = NQK + NV + NAT
BLK, LOCAL, VERT = 64, 16, 8
NT = S // P
NCH = S // TG
SM_SCALE = 1.0 / HD
ALPHA_OVER_RANK = 16.0 / RANK
WS = 256.0
CS = 256.0
SHIFT = 2048.0
NEG = -1.0e30
LOWEST = -3.0e38
LN_EPS = 1e-5
SCALE_EPS = 1e-6
ONES_ROW = 256.0
PSUM_BANK = 512
STACK = 3 * HD
ZROWS = 3 * RANK + 3
MAXRING, SCORERING, PROBRING, ADDRING = 3, 3, 6, 2
GROUP = 3
HOP, PLACING, LEAD, RESERVE = 200.0, 3500.0, 5000, 3000



def is_vertical(block):
    return (block + 1) % VERT == 0


def max_banks(t):
    banks = []
    if 2 * t + 1 < LOCAL:
        start, n = 0, P * (t + 1)
    else:
        start, n = BLK * (2 * t - LOCAL + 2), P * (LOCAL // 2)
    full, rest = n // PSUM_BANK, n % PSUM_BANK
    for seg in range(full):
        for h in range(QH):
            banks.append(dict(t=t, heads=[h], pieces=[(start + seg * PSUM_BANK, PSUM_BANK)], seg=seg,
                              mask="diagonal" if rest == 0 and seg == full - 1 else None))
    if rest:
        per = min(QH, PSUM_BANK // rest)
        for h in range(0, QH, per):
            banks.append(dict(t=t, heads=list(range(h, h + per)), pieces=[(start + full * PSUM_BANK, rest)],
                              seg=full, mask="diagonal"))
    if start > 0:
        oldest = 2 * t - LOCAL + 1
        pieces = [(BLK * oldest, BLK)]
        pieces += [(BLK * j, BLK) for j in range(oldest) if is_vertical(j)]
        banks.append(dict(t=t, heads=list(range(QH)), pieces=pieces, seg=full,
                          mask=None if is_vertical(oldest) else "late queries"))
    return banks


def key_units(c):
    per = TG // BLK
    units = []
    for j in range(min(NT, (c + 1) * TG // P)):
        lo, hi = max(per * c, 2 * j), min(per * c + per - 1, 2 * j + LOCAL)
        if is_vertical(2 * j + 1):
            hi = per * c + per - 1
        if lo > hi:
            continue
        far = max(0, hi - max(lo, 2 * j + LOCAL) + 1)
        units.append((j, lo, hi - lo + 1, 2 * j >= per * c, far))
    return sorted(units, key=lambda u: (-(u[2] == per), u[1], u[2] if u[1] == per * c else -u[2]))


def sum_groups(c):
    units = key_units(c)
    spans = [((lo - c * (TG // BLK)) * BLK, (lo - c * (TG // BLK) + n) * BLK) for _, lo, n, _, _ in units]
    groups, i = [], 0
    while i < len(units):
        members, direct = [i], []
        start, end = spans[i]
        adds = []
        while len(members) < GROUP and i + 1 < len(units):
            a, b = max(start, spans[i + 1][0]), min(end, spans[i + 1][1])
            if b - a < 2 * BLK:
                break
            if len(members) == 1:
                direct += [(i, start, a - start), (i, b, end - b)]
                start, end = a, b
            i += 1
            members.append(i)
            adds.append((i, a, b - a))
            direct += [(i, spans[i][0], a - spans[i][0]), (i, b, spans[i][1] - b)]
        if not adds:
            direct = [(i, start, end - start)]
        direct = [d for d in direct if d[2] > 0]
        groups.append((tuple(members), (start, end - start) if adds else None, adds, direct))
        i += 1
    return groups


def max_stream():
    out, due = [], []
    for c in range(NCH):
        for t in range(c * NCH, c * NCH + TG // P):
            for bank in max_banks(t):
                out.append(("bank", bank))
                due = [(n - 1, d) for n, d in due]
                while due and due[0][0] == 0:
                    out.append(("row", due.pop(0)[1]))
        out.append(("fold", c))
        due.append((3, c))
    out += [("row", d) for _, d in due]
    return out


def bank_columns(bank):
    return len(bank["heads"]) * sum(w for _, w in bank["pieces"])


def work_of(kind, item):
    if kind == "bank":
        columns = bank_columns(item)
        return 0.42 * columns + (56 if item["mask"] else 0) + 20, 1.04 * columns + 70
    if kind == "row":
        return 60, 150
    if kind == "fold":
        return 0, 250
    if kind == "scores":
        _, _, n, diagonal, far = item
        return 27 * n + 27 * far + (56 if diagonal else 0), 54 * n + 60
    if kind == "values":
        return 117 * item[2], 0
    if kind == "sums":
        _, span, _, direct = item
        return 1.83 * ((span[1] if span else 0) + sum(w for _, _, w in direct)), 0
    if kind == "add":
        return 0, 9.0 * item[2] + 80
    raise ValueError(kind)


def attention_order():
    maxima = max_stream()
    units = [(c, i, u) for c in range(NCH) for i, u in enumerate(key_units(c))]
    total = sum(bank_columns(m[1]) for m in maxima if m[0] == "bank")
    done, row_at = 0, {}
    for kind, m in maxima:
        if kind == "bank":
            done += bank_columns(m)
        elif kind == "row":
            row_at[m] = done
    begin, at = {}, 0
    span = sum(QH * BLK * u[2] for _, _, u in units)
    for c, i, u in units:
        if i == 0:
            begin[c] = at * total / span
        at += QH * BLK * u[2]
    lead = max(row_at[c] - begin[c] for c in range(NCH)) + LEAD
    ahead, done = 0, 0
    while done < lead:
        if maxima[ahead][0] == "bank":
            done += bank_columns(maxima[ahead][1])
        ahead += 1
    stream = [(0, m) for m in maxima[ahead:]] + [(1, m) for m in maxima] + [(2, m) for m in maxima[:ahead]]

    scores = [(s, c, i, u, h) for s in range(2) for c, i, u in units for h in range(QH)]
    order, inversions = [], []
    pe = act = dve = pool = 0.0
    read, exps, unit_exps = [0.0] * MAXRING, [0.0] * SCORERING, {}
    values, sums, free = [], [], {}
    placed, shifted = {}, {}
    pos = at = taken = 0
    n_scores = n_values = n_adds = 0
    unit_at = {(s, c, i): n for n, (s, c, i) in
               enumerate((s, c, i) for s in range(2) for c, i, _ in units)}
    add_free, out_at = [0.0] * ADDRING, [0.0, 0.0]
    while at < len(scores) or pos < len(stream) or values or sums:
        options = []
        if at < len(scores):
            s, c, i, u, h = scores[at]
            ready = max(exps[-SCORERING], free.get(unit_at[s, c, i] - PROBRING, 0.0) - 700)
            blocked = any(m == ("row", c) and g == s for g, m in stream[pos:])
            ready = max(ready, placed.get((s, c), 0.0))
            pace = n_scores * (2 * total - RESERVE) / (2 * span)
            before = unit_at[s, c, i] - PROBRING
            blocked = blocked or before >= n_values or any(
                before == unit_at[x[1], x[2], m] for x in sums for m, _, _ in x[4][3])
            if not blocked:
                options.append((ready, 2 if taken >= pace else 3, "scores"))
        if pos < len(stream):
            g, (kind, m) = stream[pos]
            ready = read[-MAXRING] if kind != "fold" else 0.0
            if kind == "row":
                ready = max(ready, shifted[g, m])
            late = taken < n_scores * (2 * total - RESERVE) / (2 * span) or at == len(scores)
            options.append((ready, 2 if late else 3, "max"))
        if values:
            options.append((values[0][0], 1, "values"))
        if sums:
            options.append((sums[0][0], 0, "sums"))
        now = [o for o in options if o[0] <= pe]
        ready, _, kind = min(now, key=lambda o: (o[1], o[0])) if now else min(options, key=lambda o: (o[0], o[1]))
        pe = max(pe, ready)
        if kind == "scores":
            mine, next_one = work_of("scores", u)
            pe += mine
            act = max(act, pe + HOP) + next_one
            exps.append(act + HOP)
            order.append(("scores", s, c, i, u, h))
            at += 1
            n_scores += BLK * u[2]
            if h == QH - 1:
                unit_exps[s, c, i] = act + HOP
                values.append((act + HOP, s, c, i, u))
                for n, group in enumerate(sum_groups(c)):
                    members, _, adds, _ = group
                    for j, add in enumerate(adds):
                        if add[0] == i:
                            pool = max(act + HOP, pool, add_free[-ADDRING] if j == 0 else 0.0) + work_of("add", add)[1]
                            for m in members[:2] if j == 0 else (i,):
                                free[unit_at[s, c, m]] = pool + HOP
                    if members[-1] == i:
                        sums.append((pool + HOP if adds else act + HOP, s, c, n, group))
                        if adds:
                            add_free.append(pool + 3000)
        elif kind == "max":
            g, (kind, m) = stream[pos]
            pos += 1
            mine, next_one = work_of(kind, m)
            pe += mine
            order.append((kind, g, m))
            dve = max(dve, pe + HOP) + next_one
            if kind == "fold":
                shifted[g, m] = dve + HOP
                continue
            read.append(dve + HOP)
            if kind == "bank":
                taken += bank_columns(m)
            else:
                placed[g, m] = dve + PLACING
            if inversions:
                o = inversions.pop(0)
                order.append(o)
                if o[0] == "invert":
                    dve += 870
                else:
                    pool = max(pool, dve) + 3500
        elif kind == "values":
            _, s, c, i, u = values.pop(0)
            pe = max(pe, out_at[0] if i == 0 else 0.0) + work_of("values", u)[0]
            n_values += 1
            k = unit_at[s, c, i]
            free[k] = max(free.get(k, 0.0), pe + HOP)
            last = i == len(key_units(c)) - 1
            order.append(("values", s, c, i, u, last))
            if last:
                order.append(("context", s, c))
                act = max(act, pe + HOP) + 480
                out_at[0] = act + HOP
        else:
            _, s, c, n, group = sums.pop(0)
            pe = max(pe, out_at[1] if n == 0 else 0.0) + work_of("sums", group)[0]
            for m, _, _ in group[3]:
                k = unit_at[s, c, m]
                free[k] = max(free.get(k, 0.0), pe + HOP)
            last = n == len(sum_groups(c)) - 1
            order.append(("sums", s, c, n, group, last))
            if last:
                order.append(("totals", s, c))
                act = max(act, pe + HOP) + 480
                out_at[1] = act + HOP
                inversions += [("invert", s, c, piece) for piece in range(TG // P)] + [("split", s, c)]
    return order + inversions, maxima[:ahead]



def mk_recurrent_d1(nc, x, w1, b_qk, b_v, w_out, b_out, b_ffn, adapter_out, limes, limes_t, rope, consts, out):
    q_parts = nc.dram_tensor("q_parts", [2, N_KV + 1, P, B * S], F16).ap()
    k_parts = nc.dram_tensor("k_parts", [2, N_KV + 1, HD, B * S], F16).ap()
    v_parts = nc.dram_tensor("v_parts", [N_KV + 1, B, P, NT * HD], F32).ap()
    xt_parts = nc.dram_tensor("xt_parts", [2, STEPS, P, KC * TG], F16).ap()
    ctx_parts = nc.dram_tensor("ctx_parts", [2, GROUPS, NCH, P, TG], F16).ap()

    with ExitStack() as whole:
        def keep(name, shape, dt):
            return whole.enter_context(nc.sbuf_tensor(name, shape, dt))

        ident32 = keep("ident32", [P, P], F32)
        ident16 = keep("ident16", [P, P], F16)
        ident_bf = keep("ident_bf", [P, P], BF16)
        pair_odd = keep("pair_odd", [P, P], F32)
        mask_q = keep("mask_q", [P, P], BF16)
        mask_k = keep("mask_k", [P, P], BF16)
        mask_early = keep("mask_early", [P, BLK], BF16)
        mask_late = keep("mask_late", [P, BLK], BF16)
        zstack = keep("zstack", [P, B * S], F16)
        bstack = keep("bstack", [P, D], F16)
        banks = [whole.enter_context(nc.psum_tensor(f"bank{i}", [P, PSUM_BANK], F32)) for i in range(8)]

        with ExitStack() as stage:
            natural = stage.enter_context(nc.sbuf_tensor("natural", [P, B * NT, NAT], F32))
            project(nc, x, w1, b_qk, b_v, rope, consts, q_parts, k_parts, xt_parts, ident32, ident16,
                    ident_bf, pair_odd, mask_q, mask_k, mask_early, mask_late, v_parts, natural, banks)
            route(nc, limes, limes_t, adapter_out, b_ffn, natural, ident32, pair_odd, zstack, bstack, banks)
        with ExitStack() as stage:
            w_hi = stage.enter_context(nc.sbuf_tensor("w_hi", [P, 2 * KC, D], F16))
            w_lo = stage.enter_context(nc.sbuf_tensor("w_lo", [P, 2 * KC, D], F16))
            attend(nc, q_parts, k_parts, v_parts, ctx_parts, w_out, w_hi, w_lo, ident16, ident_bf,
                   mask_q, mask_k, mask_early, mask_late, banks)
            finish(nc, x, xt_parts, ctx_parts, w_hi, w_lo, zstack, bstack, b_out, out, banks)


def project(nc, x, w1, b_qk, b_v, rope, consts, q_parts, k_parts, xt_parts, ident32, ident16,
            ident_bf, pair_odd, mask_q, mask_k, mask_early, mask_late, v_parts, natural, banks):
    WP = P
    pieces = [(c, min(WP, W1N - c)) for c in range(0, W1N, WP)]
    TT = TG // P
    STAGES = 3
    with ExitStack() as ctx:
        def sb(name, shape, dt):
            return ctx.enter_context(nc.sbuf_tensor(name, shape, dt))

        def sem(name):
            return ctx.enter_context(nc.semaphore(name))

        cpack = sb("cpack", [P, 4 * P + 2 * BLK], F32)
        w1_hi = sb("w1_hi", [P, KC, W1N], F16)
        w1_lo = sb("w1_lo", [P, KC, W1N], F16)
        wstage = [sb(f"wstage{i}", [P, KC, WP], F32) for i in range(STAGES)]
        bqk = sb("bqk", [P, NF], F32)
        bv = sb("bv", [P, NV + NAT], F32)
        table = sb("table", [P, 2, S], F32)
        eps = sb("eps", [P, 1], F32)
        xin = [sb(f"xin{i}", [P, TT, D], F32) for i in range(2)]
        stats = sb("stats", [P, TT, 12], F32)
        moments = sb("moments", [P, TT, 2], F32)
        deviation = sb("deviation", [P, TT], F32)
        rstd = sb("rstd", [P, TT], F32)
        xt_hi = [sb(f"xt_hi{i}", [P, KC, TG], F16) for i in range(2)]
        xt_lo = [sb(f"xt_lo{i}", [P, KC, TG], F16) for i in range(2)]
        raw = [sb(f"raw{i}", [P, TG], F32) for i in range(2)]
        by_cos = [sb(f"by_cos{i}", [P, TG], F32) for i in range(2)]
        by_sin = [sb(f"by_sin{i}", [P, TG], F32) for i in range(2)]
        rotated = [sb(f"rotated{i}", [P, TG], F32) for i in range(2)]
        r_hi = [sb(f"r_hi{i}", [P, TG], F16) for i in range(2)]
        r_lo = [sb(f"r_lo{i}", [P, TG], F16) for i in range(2)]
        vst = [sb(f"vst{i}", [P, N_KV, TT * HD], F32) for i in range(2)]
        zero16, zero32 = xt_hi[1], vst[1]

        TURN, PROJ = banks[0:2], banks[2:6]

        c_loaded = sem("c_loaded")
        small_loaded = sem("small_loaded")
        c_ready = sem("c_ready")
        w_loaded = [sem(f"w_loaded{i}") for i in range(STAGES)]
        w_hi_done = sem("w_hi_done")
        w_lo_done = sem("w_lo_done")
        zeroed = sem("zeroed")
        pad_stored = sem("pad_stored")
        x_loaded = [sem(f"x_loaded{i}") for i in range(2)]
        stats_done = sem("stats_done")
        moments_done = sem("moments_done")
        deviation_done = sem("deviation_done")
        rstd_done = sem("rstd_done")
        xn_done = sem("xn_done")
        turned = sem("turned")
        xt_hi_done = sem("xt_hi_done")
        xt_lo_done = sem("xt_lo_done")
        xt_stored = [sem(f"xt_stored{i}") for i in range(2)]
        projected = sem("projected")
        raw_done = sem("raw_done")
        v_done = sem("v_done")
        v_stored = [sem(f"v_stored{i}") for i in range(2)]
        parts_done = sem("parts_done")
        rotated_done = sem("rotated_done")
        r_hi_done = sem("r_hi_done")
        r_lo_done = sem("r_lo_done")
        r_stored = [sem(f"r_stored{i}") for i in range(2)]

        LO0 = 2
        PROJ0 = 2 * (NF + TT)
        V0 = TT
        RING0 = 2
        STORED0 = 64
        PADS = 5 * 16

        EARLY = 3
        TURN_AT = 4

        def following(r, s):
            return (r, 1) if s == 0 else (r + 1, 0)

        def step_of(r, s):
            return 2 * r + s

        def tokens(r, s):
            return bass.ds(r * TG + s * S, TG)

        def stores_of(f):
            return 2 if f < N_KV else 4

        STEP_STORES = [16 * sum(stores_of(f) for f in range(i, NF, 2)) for i in range(2)]

        def for_all_steps(eng, body):
            with eng.Fori(0, NCH - 1) as r:
                body(r, False)
            body(NCH - 1, True)

        block = ctx.enter_context(nc.Block())

        @block.sync
        def _(sp):
            sp.dma_start(cpack[:, :], consts).then_inc(c_loaded, 16)
            w_v = w1.rearrange("(k p) n -> p k n", p=P)
            for n, (c, w) in enumerate(pieces):
                if n >= STAGES:
                    sp.wait_ge(w_lo_done, n - STAGES + 1)
                sp.dma_start(wstage[n % STAGES][:, :, 0:w], w_v[:, :, c:c + w]).then_inc(w_loaded[n % STAGES], 16)
                if n == STAGES:
                    sp.dma_start(bqk[:, :], b_qk).then_inc(small_loaded, 16)
                    sp.dma_start(bv[:, :], b_v.partition_broadcast(P)).then_inc(small_loaded, 16)
                    sp.dma_start(table[:, :, :], rope).then_inc(small_loaded, 16)
            sp.wait_ge(zeroed, 1)
            for part in range(2):
                sp.dma_start(q_parts[part, N_KV, :, 0:S], zero16[:, 0:NCH, :].rearrange("p a b -> p (a b)")).then_inc(pad_stored, 16)
                sp.dma_start(k_parts[part, N_KV, :, 0:S], zero16[0:HD, 0:NCH, :].rearrange("p a b -> p (a b)")).then_inc(pad_stored, 16)
            sp.dma_start(v_parts[N_KV, 0], zero32[:, 0:N_KV // 2, :].rearrange("p a b -> p (a b)")).then_inc(pad_stored, 16)

            def body(r, _):
                for s in range(B):
                    sp.wait_ge(xt_lo_done, LO0 + (step_of(r, s) + 1) * KC)
                    for part, xt in enumerate((xt_hi, xt_lo)):
                        sp.dma_start(xt_parts[part, s * NCH + r],
                                     xt[s][:, :, :].rearrange("p k t -> p (k t)")).then_inc(xt_stored[s], 16)
                    for f in range(NF):
                        sp.wait_ge(r_lo_done, RING0 + step_of(r, s) * NF + f + 1)
                        for part, half in enumerate((r_hi, r_lo)):
                            if f < N_KV:
                                sp.dma_start(q_parts[part, f, :, tokens(r, s)], half[f % 2][:, :]).then_inc(r_stored[f % 2], 16)
                                continue
                            for a in range(2):
                                sp.dma_start(k_parts[part, (f - N_KV) * QH:(f - N_KV + 1) * QH,
                                                     a * HALF:(a + 1) * HALF, tokens(r, s)],
                                             half[f % 2][a * QH * HALF:(a + 1) * QH * HALF, :]).then_inc(r_stored[f % 2], 16)
                    sp.wait_ge(v_done, V0 + (step_of(r, s) + 1) * TT)
                    sp.dma_start(v_parts[0:N_KV, s, :, bass.ds(r * TT * HD, TT * HD)].rearrange("g p x -> p g x"),
                                 vst[s][:, :, :]).then_inc(v_stored[s], 16)

            for_all_steps(sp, body)
            sp.wait_ge(pad_stored, PADS)
            for s in range(2):
                sp.wait_ge(v_stored[s], 16 + 16 * NCH)
                sp.wait_ge(xt_stored[s], STORED0 + 32 * NCH)
                sp.wait_ge(r_stored[s], STORED0 + STEP_STORES[s] * STEPS)

        @block.gpsimd
        def _(pool):
            nc.gpsimd.memset(zero16[:, :, :], 0.0)
            nc.gpsimd.memset(zero32[:, :, :], 0.0).then_inc(zeroed, 1)
            pool.sem_inc(rotated_done, RING0)
            with pool.Fori(0, NCH) as r:
                for s in range(B):
                    for f in range(NF):
                        k = step_of(r, s) * NF + f
                        pool.wait_ge(parts_done, RING0 + k + 1)
                        pool.wait_ge(r_lo_done, k + 1)
                        nc.gpsimd.tensor_tensor(rotated[f % 2][:, :], by_cos[f % 2][:, :], by_sin[f % 2][:, :],
                                                ALU.add).then_inc(rotated_done, 1)

        @block.scalar
        def _(act):
            x_v = x.rearrange("(i t p) d -> i t p d", t=TT, p=P)

            def load_x(r, s):
                for t in range(TT):
                    act.dma_start(xin[s][:, t, :], x_v[s * NCH + r, t]).then_inc(x_loaded[s], 16)

            def split_weights(n):
                c, w = pieces[n]
                act.wait_ge(w_loaded[n % STAGES], 16 * (n // STAGES + 1))
                nc.scalar.activation(w1_hi[:, :, c:c + w], wstage[n % STAGES][:, :, 0:w], ACT.Copy,
                                     scale=WS).then_inc(w_hi_done, 1)

            def deviate(r, s):
                act.wait_ge(moments_done, (step_of(r, s) + 1) * TT)
                nc.scalar.activation(deviation[:, :], moments[:, :, 1], ACT.Sqrt,
                                     bias=eps[:, 0:1]).then_inc(deviation_done, 1)

            def split_xt(r, s, k):
                if k == 0:
                    act.wait_ge(projected, (step_of(r, s) + 1) * (NF + TT))
                    act.wait_ge(xt_stored[s], STORED0 + 32 * r)
                act.wait_ge(turned, step_of(r, s) * KC + k + 1)
                nc.scalar.activation(xt_hi[s][:, k, :], TURN[k % 2][:, :], ACT.Copy).then_inc(xt_hi_done, 1)

            load_x(0, 0)
            for i in range(2):
                act.sem_inc(r_stored[i], STORED0)
                act.sem_inc(xt_stored[i], STORED0)
            for n in range(EARLY):
                split_weights(n)
            deviate(0, 0)
            load_x(0, 1)
            for k in range(KC):
                split_xt(0, 0, k)
                if EARLY + k < len(pieces):
                    split_weights(EARLY + k)
            for n in range(EARLY + KC, len(pieces)):
                split_weights(n)
            act.wait_ge(small_loaded, 48)
            act.wait_ge(pad_stored, PADS)

            def body(r, last):

                def split_rotated(s, f):
                    act.wait_ge(rotated_done, RING0 + step_of(r, s) * NF + f + 1)
                    before = sum(16 * stores_of(i) for i in range(f % 2, f, 2))
                    act.wait_ge(r_stored[f % 2], STORED0 + step_of(r, s) * STEP_STORES[f % 2] + before)
                    nc.scalar.activation(r_hi[f % 2][:, :], rotated[f % 2][:, :], ACT.Copy).then_inc(r_hi_done, 1)

                for s in range(B):
                    more = not (last and s == 1)
                    if not last:
                        act.wait_ge(turned, (step_of(r, s) + 1) * KC)
                        load_x(r + 1, s)
                    if more:
                        deviate(*following(r, s))
                    for i in range(NF + TT):
                        if more and TURN_AT <= i < TURN_AT + KC:
                            split_xt(*following(r, s), i - TURN_AT)
                        if i < NF:
                            act.wait_ge(projected, PROJ0 + step_of(r, s) * (NF + TT) + i + 1)
                            act.wait_ge(parts_done, step_of(r, s) * NF + i + 1)
                            nc.scalar.activation(raw[i % 2][:, :], PROJ[(s * (NF + TT) + i) % 4][:, :], ACT.Identity,
                                                 bias=bqk[:, i:i + 1], scale=1.0 / WS).then_inc(raw_done, 1)
                        if 0 < i <= NF:
                            split_rotated(s, i - 1)

            for_all_steps(act, body)

        @block.vector
        def _(dve):

            def split_weights(n):
                c, w = pieces[n]
                dve.wait_ge(w_hi_done, n + 1)
                nc.vector.scalar_tensor_tensor(w1_lo[:, :, c:c + w], wstage[n % STAGES][:, :, 0:w], WS,
                                               w1_hi[:, :, c:c + w], ALU.mult, ALU.subtract).then_inc(w_lo_done, 1)

            def normalise(r, s):
                n = step_of(r, s) + 1
                dve.wait_ge(x_loaded[s], 16 * TT * r + 16 * TT)
                for t in range(TT):
                    for i in range(2):
                        nc.vector.bn_stats(stats[:, t, 6 * i:6 * i + 6],
                                           xin[s][:, t, i * 512:(i + 1) * 512]).then_inc(stats_done, 1)
                dve.wait_ge(stats_done, n * 2 * TT)
                nc.vector.memset(rstd[:, :], 0.0)
                for t in range(TT):
                    nc.vector.bn_aggr(moments[:, t, :], stats[:, t, :]).then_inc(moments_done, 1)
                dve.wait_ge(deviation_done, n)
                nc.vector.reciprocal(rstd[:, :], deviation[:, :]).then_inc(rstd_done, 1)
                dve.wait_ge(rstd_done, n)
                for t in range(TT):
                    nc.vector.tensor_scalar(xin[s][:, t, :], xin[s][:, t, :], moments[:, t, 0:1], rstd[:, t:t + 1],
                                            ALU.subtract, ALU.mult).then_inc(xn_done, 1)

            def split_xt(r, s, k):
                dve.wait_ge(xt_hi_done, step_of(r, s) * KC + k + 1)
                nc.vector.tensor_tensor(xt_lo[s][:, k, :], TURN[k % 2][:, :], xt_hi[s][:, k, :],
                                        ALU.subtract).then_inc(xt_lo_done, 1)

            nc.vector.memset(eps[:, :], LN_EPS)
            dve.sem_inc(xt_lo_done, LO0)
            dve.sem_inc(v_done, V0)
            dve.sem_inc(parts_done, RING0)
            dve.sem_inc(r_lo_done, RING0)
            dve.sem_inc(v_stored[0], 16)
            dve.sem_inc(v_stored[1], 16)
            dve.wait_ge(c_loaded, 16)
            for dst, at, w in ((ident32, 0, P), (ident16, 0, P), (ident_bf, 0, P), (pair_odd, P, P),
                               (mask_q, 2 * P, P), (mask_k, 3 * P, P), (mask_early, 4 * P, BLK),
                               (mask_late, 4 * P + BLK, BLK)):
                nc.vector.tensor_copy(dst[:, :], cpack[:, at:at + w]).then_inc(c_ready, 1)
            normalise(0, 0)
            for n in range(EARLY):
                split_weights(n)
            for k in range(KC):
                split_xt(0, 0, k)
                if EARLY + k < len(pieces):
                    split_weights(EARLY + k)
            for n in range(EARLY + KC, len(pieces)):
                split_weights(n)
            dve.wait_ge(small_loaded, 48)
            dve.wait_ge(pad_stored, PADS)

            def body(r, last):

                def split_rotated(s, f):
                    dve.wait_ge(r_hi_done, step_of(r, s) * NF + f + 1)
                    nc.vector.tensor_tensor(r_lo[f % 2][:, :], rotated[f % 2][:, :], r_hi[f % 2][:, :],
                                            ALU.subtract).then_inc(r_lo_done, 1)

                for s in range(B):
                    more = not (last and s == 1)
                    if more:
                        normalise(*following(r, s))
                    now = bass.ds(r * TG, TG)
                    for n in range(NF + TT):
                        if more and TURN_AT <= n < TURN_AT + KC:
                            split_xt(*following(r, s), n - TURN_AT)
                        if n < NF:
                            k = step_of(r, s) * NF + n
                            dve.wait_ge(raw_done, k + 1)
                            dve.wait_ge(rotated_done, k + 1)
                            i = n % 2
                            nc.vector.tensor_tensor(by_cos[i][:, :], raw[i][:, :], table[:, 0, now], ALU.mult)
                            nc.vector.tensor_tensor(by_sin[i][64:P, :], raw[i][0:64, :], table[0:64, 1, now], ALU.mult)
                            nc.vector.tensor_tensor(by_sin[i][0:64, :], raw[i][64:P, :], table[64:P, 1, now],
                                                    ALU.mult).then_inc(parts_done, 1)
                            if n:
                                split_rotated(s, n - 1)
                            continue
                        t = n - NF
                        dve.wait_ge(projected, PROJ0 + step_of(r, s) * (NF + TT) + n + 1)
                        bank = PROJ[(s * (NF + TT) + n) % 4]
                        if t == 0:
                            dve.wait_ge(v_stored[s], 16 * r + 16)
                        nc.vector.scalar_tensor_tensor(
                            vst[s][:, :, t * HD:(t + 1) * HD],
                            bank[:, 0:NV].rearrange("p (g d) -> p g d", d=HD), 1.0 / WS,
                            bv[:, 0:NV].rearrange("p (g d) -> p g d", d=HD), ALU.mult, ALU.add)
                        nc.vector.scalar_tensor_tensor(natural[:, (s * NCH + r) * TT + t, :], bank[:, NV:NV + NAT],
                                                       1.0 / WS, bv[:, NV:NV + NAT], ALU.mult,
                                                       ALU.add).then_inc(v_done, 1)
                        if t == 0:
                            split_rotated(s, NF - 1)

            for_all_steps(dve, body)

        @block.tensor
        def _(pe):

            def turn(r, s, k):
                n = step_of(r, s)
                if k == 0:
                    pe.wait_ge(xn_done, (n + 1) * TT)
                pe.wait_ge(xt_lo_done, n * KC + k + 1)
                for t in range(TT):
                    last = nc.tensor.transpose(TURN[k % 2][:, t * P:(t + 1) * P],
                                               xin[s][:, t, k * P:(k + 1) * P], ident32[:, :])
                last.then_inc(turned, 1)

            pe.sem_inc(projected, PROJ0)
            pe.wait_ge(c_ready, 8)
            for k in range(KC):
                turn(0, 0, k)

            def body(r, last):
                for s in range(B):
                    n = step_of(r, s)
                    pe.wait_ge(xt_lo_done, LO0 + (n + 1) * KC)
                    for i in range(NF + TT):
                        if not (last and s == 1) and TURN_AT <= i < TURN_AT + KC:
                            turn(*following(r, s), i - TURN_AT)
                        if s == 0 and not last and i <= NF:
                            pe.wait_ge(w_lo_done, i + 1 if i < NF else len(pieces))
                        if i < 4:
                            pe.wait_ge(v_done, n * TT + i + 1)
                        else:
                            pe.wait_ge(raw_done, n * NF + i - 3)
                        dst = PROJ[(s * (NF + TT) + i) % 4]
                        for k in range(KC):
                            if i < NF:
                                cols = slice(i * P, (i + 1) * P)
                                pairs = ((w1_hi[:, k, cols], xt_hi[s][:, k, :]), (w1_hi[:, k, cols], xt_lo[s][:, k, :]),
                                         (w1_lo[:, k, cols], xt_hi[s][:, k, :]))
                                width = TG
                            else:
                                toks = slice((i - NF) * P, (i - NF + 1) * P)
                                pairs = ((xt_hi[s][:, k, toks], w1_hi[:, k, NQK:W1N]), (xt_hi[s][:, k, toks], w1_lo[:, k, NQK:W1N]),
                                         (xt_lo[s][:, k, toks], w1_hi[:, k, NQK:W1N]))
                                width = NV + NAT
                            for m, (stay, move) in enumerate(pairs):
                                mm = nc.tensor.matmul(dst[:, 0:width], stay, move, start=(k == 0 and m == 0),
                                                      stop=(k == KC - 1 and m == 2))
                        mm.then_inc(projected, 1)

            for_all_steps(pe, body)


def route(nc, limes, limes_t, adapter_out, b_ffn, natural, ident32, pair_odd, zstack, bstack, banks):
    NTOK = B * NT
    with ExitStack() as ctx:
        def sb(name, shape, dt):
            return ctx.enter_context(nc.sbuf_tensor(name, shape, dt))

        def sem(name):
            return ctx.enter_context(nc.semaphore(name))

        lim = sb("lim", [E, RANK], F32)
        lim_t = sb("lim_t", [RANK, E], F32)
        z_t = sb("z_t", [RANK, STEPS, TG], F32)
        both = sb("both", [P, 2, NTOK * E], F32)
        tops = sb("tops", [P, 2], F32)
        top_all = sb("top_all", [P, 2], F32)
        half_inv = sb("half_inv", [P, 2], F32)
        u = sb("u", [P, NTOK * E], F32)
        logits = sb("logits", [P, NTOK, E], F32)
        work = sb("work", [P, NTOK, E], F32)
        probs = sb("probs", [P, NTOK, E], F32)
        equal = sb("equal", [P, NTOK, E], F32)
        m1 = sb("m1", [P, NTOK], F32)
        m2 = sb("m2", [P, NTOK], F32)
        ties = sb("ties", [P, NTOK], F32)
        weights = sb("weights", [P, NTOK, E], F32)
        w_t = sb("w_t", [E, STEPS, TG], F32)
        zp = sb("zp", [RANK, 2, TG], F32)
        amat = sb("amat", [RANK, D], F32)
        brow = sb("brow", [1, D], F32)
        rest = sb("rest", [1, 2, D], F32)
        bparts = sb("bparts", [1, 3, D], F16)

        loaded = sem("loaded")
        b_steps = sem("b_steps")
        b_placed = sem("b_placed")
        pe_step = sem("pe_step")
        act_step = sem("act_step")
        dve_step = sem("dve_step")
        reduced = sem("reduced")
        mixed = sem("mixed")
        zstacked = sem("zstacked")

        block = ctx.enter_context(nc.Block())

        @block.sync
        def _(sp):
            sp.dma_start(lim[:, :], limes).then_inc(loaded, 16)
            sp.dma_start(lim_t[:, :], limes_t).then_inc(loaded, 16)
            sp.dma_start(amat[:, :], adapter_out).then_inc(loaded, 16)
            sp.dma_start(brow[:, :], b_ffn).then_inc(loaded, 16)
            sp.wait_ge(b_steps, 5)
            for i in range(3):
                sp.dma_start(bstack[3 * RANK + i:3 * RANK + i + 1, :], bparts[0:1, i, :]).then_inc(b_placed, 16)
            sp.wait_ge(b_placed, 48)

        @block.tensor
        def _(pe):
            pe.wait_ge(loaded, 64)
            for i in range(STEPS):
                for t in range(TG // P):
                    last = nc.tensor.matmul(banks[i][0:RANK, t * P:(t + 1) * P], natural[:, i * 4 + t, E:NAT],
                                            ident32[:, :], start=(t == 0), stop=(t == 3))
                last.then_inc(pe_step, 1)
            pe.wait_ge(act_step, STEPS)
            for t in range(NTOK):
                last = nc.tensor.matmul(banks[0][:, t * E:(t + 1) * E], z_t[:, t // 4, (t % 4) * P:(t % 4 + 1) * P],
                                        lim_t[:, :], start=(t == 0), stop=(t == NTOK - 1))
            last.then_inc(pe_step, 1)
            pe.wait_ge(dve_step, 2)
            nc.tensor.matmul(banks[1][:, :], pair_odd[:, :], both[:, :, :].rearrange("p a n -> p (a n)"),
                             start=True, stop=True).then_inc(pe_step, 1)
            pe.wait_ge(mixed, 1)
            for i in range(STEPS):
                for t in range(TG // P):
                    last = nc.tensor.matmul(banks[i][0:E, t * P:(t + 1) * P], weights[:, i * 4 + t, :],
                                            ident32[:, :], start=(t == 0), stop=(t == 3))
                last.then_inc(pe_step, 1)
            for i in range(STEPS):
                pe.wait_ge(act_step, STEPS + 3 + i)
                nc.tensor.matmul(banks[i][0:RANK, :], lim[:, :], w_t[:, i, :], start=True,
                                 stop=True).then_inc(pe_step, 1)

        @block.scalar
        def _(act):
            for i in range(STEPS):
                act.wait_ge(pe_step, i + 1)
                nc.scalar.activation(z_t[:, i, :], banks[i][0:RANK, :], ACT.Copy).then_inc(act_step, 1)
            act.wait_ge(reduced, 1)
            nc.scalar.activation(work[:, :, :], work[:, :, :], ACT.Exp).then_inc(act_step, 1)
            act.wait_ge(reduced, 2)
            nc.scalar.activation(logits[:, :, :], equal[:, :, :], ACT.Exp, scale=-2.0).then_inc(act_step, 1)
            for i in range(STEPS):
                act.wait_ge(pe_step, STEPS + 2 + i + 1)
                nc.scalar.activation(w_t[:, i, :], banks[i][0:E, :], ACT.Copy).then_inc(act_step, 1)

        @block.gpsimd
        def _(pool):
            pool.wait_ge(dve_step, 3)
            nc.gpsimd.partition_all_reduce(top_all[:, :], tops[:, :], P, RMAX).then_inc(zstacked, 1)

        @block.vector
        def _(dve):
            count = [0]

            def step(ins):
                count[0] += 1
                ins.then_inc(b_steps, 1)
                dve.wait_ge(b_steps, count[0])

            def wide(t):
                return t[:, :].unsqueeze(2).to_broadcast([P, NTOK, E])

            dve.wait_ge(loaded, 64)
            step(nc.vector.tensor_copy(bparts[:, 0, :], brow[:, :]))
            step(nc.vector.tensor_tensor(rest[:, 0, :], brow[:, :], bparts[:, 0, :], ALU.subtract))
            step(nc.vector.tensor_copy(bparts[:, 1, :], rest[:, 0, :]))
            step(nc.vector.tensor_tensor(rest[:, 1, :], rest[:, 0, :], bparts[:, 1, :], ALU.subtract))
            step(nc.vector.tensor_copy(bparts[:, 2, :], rest[:, 1, :]))
            step(nc.vector.tensor_scalar(bstack[0:RANK, :], amat[:, :], WS, None, ALU.mult))
            nc.vector.tensor_scalar(bstack[RANK:2 * RANK, :], amat[:, :], WS, None, ALU.mult)
            nc.vector.scalar_tensor_tensor(bstack[2 * RANK:3 * RANK, :], amat[:, :], WS, bstack[0:RANK, :],
                                           ALU.mult, ALU.subtract)
            nc.vector.memset(zstack[3 * RANK:ZROWS, :], ONES_ROW)
            nc.vector.tensor_copy(both[:, 0, :].rearrange("p (t e) -> p t e", e=E), natural[:, :, 0:E]).then_inc(dve_step, 1)
            dve.wait_ge(pe_step, STEPS + 1)
            nc.vector.tensor_copy(both[:, 1, :], banks[0][:, 0:NTOK * E]).then_inc(dve_step, 1)
            dve.wait_ge(pe_step, STEPS + 2)
            nc.vector.tensor_reduce(tops[:, :], banks[1][:, :].rearrange("p (a n) -> p a n", a=2), AX.X, ALU.max,
                                    apply_absolute_value=True).then_inc(dve_step, 1)
            dve.wait_ge(zstacked, 1)
            step(nc.vector.tensor_scalar(top_all[:, :], top_all[:, :], SCALE_EPS, None, ALU.max))
            step(nc.vector.reciprocal(half_inv[:, :], top_all[:, :]))
            step(nc.vector.tensor_scalar(half_inv[:, :], half_inv[:, :], 0.5, None, ALU.mult))
            step(nc.vector.tensor_scalar(u[:, :], banks[1][:, 0:NTOK * E], half_inv[:, 0:1], None, ALU.mult))
            step(nc.vector.scalar_tensor_tensor(logits[:, :, :].rearrange("p t e -> p (t e)"),
                                                banks[1][:, NTOK * E:2 * NTOK * E], half_inv[:, 1:2], u[:, :],
                                                ALU.mult, ALU.add))
            step(nc.vector.tensor_reduce(m1[:, :], logits[:, :, :], AX.X, ALU.max))
            nc.vector.tensor_tensor(work[:, :, :], logits[:, :, :], wide(m1), ALU.subtract).then_inc(reduced, 1)
            dve.wait_ge(act_step, STEPS + 1)
            step(nc.vector.tensor_reduce(m2[:, :], work[:, :, :], AX.X, ALU.add))
            step(nc.vector.reciprocal(m2[:, :], m2[:, :]))
            step(nc.vector.tensor_tensor(probs[:, :, :], work[:, :, :], wide(m2), ALU.mult))
            step(nc.vector.tensor_reduce(m1[:, :], probs[:, :, :], AX.X, ALU.max))
            step(nc.vector.tensor_tensor(equal[:, :, :], probs[:, :, :], wide(m1), ALU.is_equal))
            step(nc.vector.tensor_reduce(ties[:, :], equal[:, :, :], AX.X, ALU.add))
            step(nc.vector.scalar_tensor_tensor(work[:, :, :].rearrange("p t e -> p (t e)"),
                                                equal[:, :, :].rearrange("p t e -> p (t e)"), -2.0,
                                                probs[:, :, :].rearrange("p t e -> p (t e)"), ALU.mult, ALU.add))
            step(nc.vector.tensor_reduce(m2[:, :], work[:, :, :], AX.X, ALU.max))
            step(nc.vector.tensor_scalar(ties[:, :], ties[:, :], 2.0, None, ALU.is_ge))
            step(nc.vector.tensor_tensor(ties[:, :], ties[:, :], m1[:, :], ALU.mult))
            step(nc.vector.tensor_tensor(m2[:, :], m2[:, :], ties[:, :], ALU.max))
            nc.vector.tensor_tensor(equal[:, :, :], probs[:, :, :], wide(m2), ALU.subtract).then_inc(reduced, 1)
            dve.wait_ge(act_step, STEPS + 2)
            step(nc.vector.tensor_scalar(logits[:, :, :], logits[:, :, :], 1.0, None, ALU.add))
            step(nc.vector.reciprocal(logits[:, :, :], logits[:, :, :]))
            step(nc.vector.tensor_tensor(work[:, :, :], probs[:, :, :], logits[:, :, :], ALU.mult))
            step(nc.vector.tensor_reduce(m1[:, :], work[:, :, :], AX.X, ALU.add))
            step(nc.vector.tensor_scalar(m1[:, :], m1[:, :], 1e-9, None, ALU.add))
            step(nc.vector.reciprocal(m1[:, :], m1[:, :]))
            nc.vector.tensor_tensor(weights[:, :, :], work[:, :, :], wide(m1), ALU.mult).then_inc(mixed, 1)
            for i in range(STEPS):
                dve.wait_ge(pe_step, 2 * STEPS + 2 + i + 1)
                toks = slice(i * TG, (i + 1) * TG)
                step(nc.vector.scalar_tensor_tensor(zp[:, i % 2, :], banks[i][0:RANK, :], ALPHA_OVER_RANK,
                                                    z_t[:, i, :], ALU.mult, ALU.mult))
                step(nc.vector.tensor_copy(zstack[0:RANK, toks], zp[:, i % 2, :]))
                nc.vector.tensor_copy(zstack[2 * RANK:3 * RANK, toks], zp[:, i % 2, :])
                nc.vector.tensor_tensor(zstack[RANK:2 * RANK, toks], zp[:, i % 2, :], zstack[0:RANK, toks], ALU.subtract)
            nc.vector.tensor_copy(m1[:, :], m2[:, :]).then_inc(mixed, 1)
            dve.wait_ge(mixed, 2)


def attend(nc, q_parts, k_parts, v_parts, ctx_parts, w_out, w_hi, w_lo, ident16, ident_bf,
           mask_q, mask_k, mask_early, mask_late, banks):
    order, lead = attention_order()
    UNITS = len([1 for o in order if o[0] == "values"])
    BANKS = len([1 for o in order if o[0] in ("bank", "row")])
    LEAD_BANKS = len([1 for k, _ in lead if k in ("bank", "row")])
    LEAD_ROWS = len([1 for k, _ in lead if k == "row"])
    LEAD_FOLDS = len([1 for k, _ in lead if k == "fold"])
    SUMS = [o for o in order if o[0] == "sums"]
    ADDED = [o for o in SUMS if o[4][1] is not None]
    ADDS = [(g, j) for g, o in enumerate(ADDED) for j in range(len(o[4][2]))]
    STEPS2 = GROUPS // 2
    with ExitStack() as ctx:
        def sb(name, shape, dt):
            return ctx.enter_context(nc.sbuf_tensor(name, shape, dt))

        def sem(name):
            return ctx.enter_context(nc.semaphore(name))

        q_stack = [sb(f"q_stack{i}", [STACK + 1, QH, S], F16) for i in range(2)]
        k_stack = [sb(f"k_stack{i}", [STACK + 1, S], F16) for i in range(2)]
        v_slot = [sb(f"v_slot{i}", [P, NT, HD], F32) for i in range(2)]
        ones = sb("ones", [P, HD], F32)
        partial = [sb(f"partial{i}", [P, NCH, 3, QH * (TG // P)], F32) for i in range(2)]
        top = [sb(f"top{i}", [P, NCH, QH * (TG // P)], F32) for i in range(2)]
        shift = [sb(f"shift{i}", [P, NCH, QH * (TG // P)], F16) for i in range(2)]
        shift_row = [sb(f"shift_row{i}", [QH * (TG // P), P], F16) for i in range(2)]
        probs = [sb(f"probs{i}", [P, QH, TG], F32) for i in range(PROBRING)]
        added = [sb(f"added{i}", [P, QH, TG], F32) for i in range(ADDRING)]
        total = [sb(f"total{i}", [P, TG], F32) for i in range(2)]
        context = [sb(f"context{i}", [P, TG], F32) for i in range(2)]
        scaled = sb("scaled", [P, TG], F32)
        c_hi = [sb(f"c_hi{i}", [P, TG], F16) for i in range(2)]
        c_lo = [sb(f"c_lo{i}", [P, TG], F16) for i in range(2)]
        wst = sb("wst", [P, D], F32)

        MAXB, SCOREB, CTXB, SUMB = banks[0:3], banks[3:6], banks[6], banks[7]

        qk_loaded = [sem(f"qk_loaded{i}") for i in range(2)]
        set_up = sem("set_up")
        max_full = sem("max_full")
        max_read = sem("max_read")
        folded = sem("folded")
        shift_done = sem("shift_done")
        row_placed = [sem(f"row_placed{i}") for i in range(2)]
        score_full = sem("score_full")
        prob_done = sem("prob_done")
        values_done = sem("values_done")
        units_added = sem("units_added")
        summed = sem("summed")
        total_out = sem("total_out")
        context_out = sem("context_out")
        inverted = sem("inverted")
        scaled_done = sem("scaled_done")
        c_lo_done = sem("c_lo_done")
        c_stored = [sem(f"c_stored{i}") for i in range(2)]
        wst_loaded = sem("wst_loaded")
        wst_hi = sem("wst_hi")
        wst_lo = sem("wst_lo")

        TILES = TG // P

        MAX0 = MAXRING
        PROB0 = SCORERING
        VAL0 = PROBRING
        CTX0 = 2
        PLACED = 16 * QH
        ROW0 = PLACED
        ONE0 = 1

        def load_group(eng, slot, n):
            q, k = q_stack[slot], k_stack[slot]
            toks = slice(slot * S, (slot + 1) * S)
            for row, part in enumerate((0, 1, 0)):
                for a in range(2):
                    at = row * HD + a * HALF
                    eng.dma_start(q[at:at + HALF, :, :],
                                  q_parts[part, n, a * QH * HALF:(a + 1) * QH * HALF, toks].rearrange("(h r) t -> r h t", r=HALF)
                                  ).then_inc(qk_loaded[slot], 16)
            for row, part in enumerate((0, 0, 1)):
                eng.dma_start(k[row * HD:(row + 1) * HD, :], k_parts[part, n, :, toks]).then_inc(qk_loaded[slot], 16)
            eng.dma_start(v_slot[slot][:, :, :].rearrange("p t d -> p (t d)"), v_parts[n, slot]).then_inc(qk_loaded[slot], 16)

        LOADS = 10 * 16

        def unit_end(s, c):
            return sum(len(key_units(i)) for i in range(NCH)) * s + sum(len(key_units(i)) for i in range(c + 1))

        def prob_slot(unit):
            return unit % PROBRING

        def first_unit(s, c):
            return unit_end(s, c) - len(key_units(c))

        def sums_before(s, c):
            return len([1 for o in SUMS if (o[1], o[2]) < (s, c)])

        def freed_by(unit):
            adds = sums = 0
            before = unit - PROBRING
            a = 0
            for n, (_, s, c, _, (members, _, steps, direct), _) in enumerate(SUMS):
                at = first_unit(s, c)
                for j, (m, _, _) in enumerate(steps):
                    a += 1
                    if before >= 0 and before in [at + x for x in (members[:2] if j == 0 else (m,))]:
                        adds = a
                if before >= 0 and before in [at + m for m, _, _ in direct]:
                    sums = n + 1
            return adds, sums

        block = ctx.enter_context(nc.Block())

        @block.sync
        def _(sp):
            w_v = w_out.rearrange("(m p) d -> m p d", p=P)

            def load_weights(r, i):
                sp.wait_ge(wst_lo, ONE0 + 2 * r + i)
                sp.dma_start(wst[:, :], w_v[r * 2 + i]).then_inc(wst_loaded, 16)

            def store(r, s, c):
                k = (s * NCH + c) % 2
                sp.wait_ge(c_lo_done, CTX0 + r * 2 * NCH + s * NCH + c + 1)
                for part, half in enumerate((c_hi, c_lo)):
                    sp.dma_start(ctx_parts[part, r * 2 + s, c], half[k][:, :]).then_inc(c_stored[k], 16)

            def place_row(r, k, n, c, slot):
                sp.wait_ge(max_read, MAX0 + r * BANKS + k + 1)
                for h in range(QH):
                    sp.dma_start(q_stack[slot][STACK:STACK + 1, h, c * TG:(c + 1) * TG],
                                 shift_row[n % 2][h * TILES:(h + 1) * TILES, :]).then_inc(row_placed[n % 2], 16)

            load_group(sp, 0, 0)
            k = n = 0
            for kind, m in lead:
                if kind == "row":
                    place_row(0, k, n, m, 0)
                    n += 1
                k += kind != "fold"
            with sp.Fori(0, STEPS2) as r:
                sp.wait_ge(values_done, VAL0 + r * UNITS)
                load_group(sp, 1, r)
                load_weights(r, 0)
                k, n = LEAD_BANKS, LEAD_ROWS
                for o in order:
                    if o[0] == "row":
                        place_row(r, k, n, o[2], o[1] % 2)
                        n += 1
                    if o[0] in ("bank", "row"):
                        k += 1
                    if o[0] == "split":
                        _, s, c = o
                        if s * NCH + c:
                            store(r, (s * NCH + c - 1) // NCH, (s * NCH + c - 1) % NCH)
                    if o[0] == "context":
                        _, s, c = o
                        if (s, c) == (0, 2):
                            load_weights(r, 1)
                        if (s, c) == (0, NCH - 1):
                            sp.wait_ge(values_done, VAL0 + r * UNITS + UNITS // 2)
                            load_group(sp, 0, r + 1)
                store(r, 1, NCH - 1)
            sp.wait_ge(qk_loaded[0], LOADS * (STEPS2 + 1))
            for i in range(2):
                sp.wait_ge(row_placed[i], ROW0 + PLACED * (GROUPS * NCH // 2 + (LEAD_ROWS + 1 - i) // 2))
            for i in range(2):
                sp.wait_ge(c_stored[i], 32 + 32 * GROUPS * NCH // 2)

        @block.gpsimd
        def _(pool):
            for i in range(2):
                nc.gpsimd.memset(k_stack[i][STACK:STACK + 1, :], SHIFT).then_inc(set_up, 1)
            pool.sem_inc(units_added, ONE0)
            pool.sem_inc(c_lo_done, CTX0)
            pool.sem_inc(c_stored[0], 32)
            pool.sem_inc(c_stored[1], 32)

            def split(r, s, c):
                k = (s * NCH + c) % 2
                n = r * 2 * NCH + s * NCH + c + 1
                pool.wait_ge(context_out, CTX0 + n)
                pool.wait_ge(c_stored[k], 32 + r * 32 * NCH + 32 * ((s * NCH + c) // 2))
                pool.wait_ge(c_lo_done, CTX0 + n - 1)
                pool.wait_ge(inverted, r * 2 * NCH * TILES + (s * NCH + c + 1) * TILES)
                nc.gpsimd.tensor_tensor(c_hi[k][:, :], context[k][:, :], total[k][:, :], ALU.mult)
                nc.gpsimd.tensor_tensor(scaled[:, :], context[k][:, :], total[k][:, :], ALU.mult).then_inc(scaled_done, 1)
                pool.wait_ge(scaled_done, n)
                nc.gpsimd.tensor_tensor(c_lo[k][:, :], scaled[:, :], c_hi[k][:, :],
                                        ALU.subtract).then_inc(c_lo_done, 1)

            def add(r, a):
                g, j = ADDS[a]
                _, s, c, _, (members, span, steps, _), _ = ADDED[g]
                m, start, width = steps[j]

                def of(member):
                    at = (key_units(c)[member][1] - c * (TG // BLK)) * BLK
                    return probs[prob_slot(first_unit(s, c) + member)][:, :, start - at:start - at + width]

                pool.wait_ge(prob_done, PROB0 + r * QH * UNITS + (first_unit(s, c) + m + 1) * QH)
                dst = added[g % ADDRING][:, :, start - span[0]:start - span[0] + width]
                if j == 0:
                    pool.wait_ge(summed, ONE0 + r * len(SUMS) + (SUMS.index(ADDED[g - ADDRING]) + 1 if g >= ADDRING else 0))
                    nc.gpsimd.tensor_tensor(dst, of(members[0]), of(m), ALU.add).then_inc(units_added, 1)
                else:
                    pool.wait_ge(units_added, ONE0 + r * len(ADDS) + a)
                    nc.gpsimd.tensor_tensor(dst, dst, of(m), ALU.add).then_inc(units_added, 1)

            with pool.Fori(0, STEPS2) as r:
                a = unit = 0
                for o in order:
                    if o[0] == "scores" and o[5] == QH - 1:
                        unit += 1
                        if a < len(ADDS):
                            g, j = ADDS[a]
                            _, s, c, _, (_, _, steps, _), _ = ADDED[g]
                            if first_unit(s, c) + steps[j][0] + 1 == unit:
                                add(r, a)
                                a += 1
                    elif o[0] == "split":
                        split(r, o[1], o[2])

        @block.scalar
        def _(act):
            act.sem_inc(prob_done, PROB0)
            act.sem_inc(context_out, CTX0)
            act.sem_inc(total_out, ONE0)
            with act.Fori(0, STEPS2) as r:
                k = 0
                unit = -1
                for o in order:
                    if o[0] == "scores":
                        _, s, c, i, (j, lo, n, diagonal, far), h = o
                        if h == 0:
                            unit += 1
                            act.wait_ge(values_done, r * UNITS + max(unit + 1, VAL0))
                            adds, sums = freed_by(unit)
                            if adds or unit < PROBRING:
                                act.wait_ge(units_added, ONE0 + r * len(ADDS) + adds)
                            if sums or unit < PROBRING:
                                act.wait_ge(summed, ONE0 + r * len(SUMS) + sums)
                        act.wait_ge(score_full, r * QH * UNITS + k + 1)
                        nc.scalar.activation(probs[prob_slot(unit)][:, h, 0:BLK * n], SCOREB[k % SCORERING][:, 0:BLK * n],
                                             ACT.Exp, scale=SM_SCALE).then_inc(prob_done, 1)
                        k += 1
                    elif o[0] == "context":
                        _, s, c = o
                        q = s * NCH + c
                        act.wait_ge(values_done, VAL0 + r * UNITS + unit_end(s, c))
                        act.wait_ge(c_lo_done, r * 2 * NCH + q + 1)
                        nc.scalar.activation(context[q % 2][:, :], CTXB[:, :], ACT.Copy).then_inc(context_out, 1)
                        if q in (1, 5):
                            i = q // 4
                            act.wait_ge(wst_loaded, 32 * r + 16 * i + 16)
                            nc.scalar.activation(w_hi[:, r * 2 + i, :], wst[:, :], ACT.Copy,
                                                 scale=WS).then_inc(wst_hi, 1)
                    elif o[0] == "totals":
                        _, s, c = o
                        q = s * NCH + c
                        act.wait_ge(summed, ONE0 + r * len(SUMS) + sums_before(s, c) + len(sum_groups(c)))
                        act.wait_ge(c_lo_done, r * 2 * NCH + q + 1)
                        nc.scalar.activation(total[q % 2][:, :], SUMB[:, :], ACT.Copy,
                                             scale=1.0 / CS).then_inc(total_out, 1)

        @block.vector
        def _(dve):
            for i in range(2):
                nc.vector.memset(partial[i][:, :, :, :], LOWEST).then_inc(set_up, 1)
            nc.vector.memset(ones[:, :], 1.0).then_inc(set_up, 1)
            dve.sem_inc(max_read, MAX0)
            dve.sem_inc(wst_lo, ONE0)
            dve.wait_ge(set_up, 5)

            def take(r, k, bank, slot):
                t, c = bank["t"], bank["t"] // TILES
                heads = bank["heads"]
                w = sum(x for _, x in bank["pieces"])
                dve.wait_ge(max_full, r * BANKS + k + 1)
                dst = partial[slot][:, c, bank["seg"], heads[0] * TILES + t % TILES:heads[-1] * TILES + t % TILES + 1:TILES]
                src = MAXB[k % MAXRING][:, 0:len(heads) * w].rearrange("p (h w) -> p h w", w=w)
                nc.vector.tensor_reduce(dst, src, AX.X, ALU.max).then_inc(max_read, 1)

            def fold(r, k, c, slot, n):
                dve.wait_ge(max_read, MAX0 + r * BANKS + k)
                nc.vector.tensor_reduce(top[slot][:, c, :], partial[slot][:, c, :, :].rearrange("p s n -> p n s"),
                                        AX.X, ALU.max).then_inc(folded, 1)
                dve.wait_ge(folded, r * 2 * NCH + n + 1)
                nc.vector.tensor_scalar(shift[slot][:, c, :], top[slot][:, c, :], -1.0 / SHIFT, None,
                                        ALU.mult).then_inc(shift_done, 1)

            def row(r, k, n):
                dve.wait_ge(max_full, r * BANKS + k + 1)
                dve.wait_ge(row_placed[n % 2], PLACED * (NCH * r + n // 2) + ROW0)
                nc.vector.tensor_copy(shift_row[n % 2][:, :], MAXB[k % MAXRING][0:QH * TILES, 0:P]).then_inc(max_read, 1)

            dve.sem_inc(row_placed[0], ROW0)
            dve.sem_inc(row_placed[1], ROW0)

            k = n = f = 0
            for kind, m in lead:
                if kind == "bank":
                    take(0, k, m, 0)
                    k += 1
                elif kind == "fold":
                    fold(0, k, m, 0, f)
                    f += 1
                else:
                    row(0, k, n)
                    n += 1
                    k += 1
            with dve.Fori(0, STEPS2) as r:
                k, n, f = LEAD_BANKS, LEAD_ROWS, LEAD_FOLDS
                for o in order:
                    if o[0] == "bank":
                        take(r, k, o[2], o[1] % 2)
                        k += 1
                    elif o[0] == "fold":
                        fold(r, k, o[2], o[1] % 2, f)
                        f += 1
                    elif o[0] == "row":
                        row(r, k, n)
                        n += 1
                        k += 1
                    elif o[0] == "invert":
                        _, s, c, piece = o
                        q = s * NCH + c
                        now = slice(piece * P, (piece + 1) * P)
                        if piece == 0:
                            dve.wait_ge(total_out, ONE0 + r * 2 * NCH + q + 1)
                        nc.vector.reciprocal(total[q % 2][:, now], total[q % 2][:, now]).then_inc(inverted, 1)
                        if piece == 0 and q in (1, 5):
                            i = q // 4
                            dve.wait_ge(wst_hi, 2 * r + i + 1)
                            nc.vector.scalar_tensor_tensor(w_lo[:, r * 2 + i, :], wst[:, :], WS, w_hi[:, r * 2 + i, :],
                                                           ALU.mult, ALU.subtract).then_inc(wst_lo, 1)

        @block.tensor
        def _(pe):
            pe.sem_inc(values_done, VAL0)
            pe.sem_inc(summed, ONE0)
            pe.wait_ge(set_up, 5)

            def wait_max_bank(r, k):
                if isinstance(r, int):
                    if k >= MAXRING:
                        pe.wait_ge(max_read, k + 1)
                else:
                    pe.wait_ge(max_read, r * BANKS + (max(k + 1, LEAD_BANKS + MAX0) if BANKS % MAXRING else k + 1))

            def max_bank(r, k, bank, slot):
                dst = MAXB[k % MAXRING]
                wait_max_bank(r, k)
                t = bank["t"]
                w = sum(x for _, x in bank["pieces"])
                first = True
                mms = []
                for i, h in enumerate(bank["heads"]):
                    at = i * w
                    for start, width in bank["pieces"]:
                        mms.append((dst[:, at:at + width], q_stack[slot][0:STACK, h, t * P:(t + 1) * P],
                                    k_stack[slot][0:STACK, start:start + width]))
                        at += width
                whole = dst[:, 0:len(bank["heads"]) * w].rearrange("p (h w) -> p h w", w=w)
                if bank["mask"] == "diagonal":
                    mms.append((whole[:, :, w - P:w], ident_bf[:, :],
                                mask_q[:, :].unsqueeze(1).to_broadcast([P, len(bank["heads"]), P])))
                elif bank["mask"] == "late queries":
                    mms.append((whole[:, :, 0:BLK], ident_bf[:, :],
                                mask_late[:, :].unsqueeze(1).to_broadcast([P, QH, BLK])))
                for m, (o, a, b) in enumerate(mms):
                    last = nc.tensor.matmul(o, a, b, start=(m == 0), stop=(m == len(mms) - 1), skip_group_check=True)
                last.then_inc(max_full, 1)

            def max_row(r, k, n, c, slot):
                wait_max_bank(r, k)
                pe.wait_ge(shift_done, r * 2 * NCH + n + 1)
                nc.tensor.matmul(MAXB[k % MAXRING][0:QH * TILES, 0:P], shift[slot][:, c, :], ident16[:, :], start=True,
                                 stop=True).then_inc(max_full, 1)

            def scores(r, k, s, u, h):
                j, lo, n, diagonal, far = u
                dst = SCOREB[k % SCORERING]
                pe.wait_ge(prob_done, r * QH * UNITS + max(k + 1, PROB0))
                mms = [(dst[:, 0:BLK * n], k_stack[s][:, j * P:(j + 1) * P], q_stack[s][:, h, lo * BLK:(lo + n) * BLK])]
                if diagonal:
                    mms.append((dst[:, 0:P], ident_bf[:, :], mask_k[:, :]))
                if far:
                    mms.append((dst[:, BLK * (n - far):BLK * n].rearrange("p (a w) -> p a w", w=BLK), ident_bf[:, :],
                                mask_early[:, :].unsqueeze(1).to_broadcast([P, far, BLK])))
                for m, (o, a, b) in enumerate(mms):
                    last = nc.tensor.matmul(o, a, b, start=(m == 0), stop=(m == len(mms) - 1), skip_group_check=True)
                last.then_inc(score_full, 1)

            def products(r, unit, s, c, i, u, last_of_chunk):
                j, lo, n, diagonal, far = u
                at = (lo - c * (TG // BLK)) * BLK
                pe.wait_ge(prob_done, PROB0 + r * QH * UNITS + (unit + 1) * QH)
                if i == 0:
                    pe.wait_ge(context_out, CTX0 + r * 2 * NCH + s * NCH + c)
                for h in range(QH):
                    last = nc.tensor.matmul(CTXB[h * HD:(h + 1) * HD, at:at + BLK * n], v_slot[s][:, j, :],
                                            probs[prob_slot(unit)][:, h, 0:BLK * n], start=(i == 0),
                                            stop=last_of_chunk, skip_group_check=True, tile_position=(0, h * HD))
                last.then_inc(values_done, 1)

            def sums(r, a, s, c, n, group, last_of_chunk):
                members, span, steps, direct = group
                if n == 0:
                    pe.wait_ge(total_out, ONE0 + r * 2 * NCH + s * NCH + c)
                if direct:
                    pe.wait_ge(prob_done, PROB0 + r * QH * UNITS + (first_unit(s, c) + members[-1] + 1) * QH)
                if steps:
                    last_add = max(i for i, (g, _) in enumerate(ADDS) if g == a)
                    pe.wait_ge(units_added, ONE0 + r * len(ADDS) + last_add + 1)
                pieces = [(added[a % ADDRING], 0, *span)] if steps else []
                for m, start, width in direct:
                    at = (key_units(c)[m][1] - c * (TG // BLK)) * BLK
                    pieces.append((probs[prob_slot(first_unit(s, c) + m)], start - at, start, width))
                for x, (src, at, start, width) in enumerate(pieces):
                    for h in range(QH):
                        last = nc.tensor.matmul(SUMB[h * HD:(h + 1) * HD, start:start + width], ones[:, :],
                                                src[:, h, at:at + width], start=(n == 0 and x == 0),
                                                stop=last_of_chunk and x == len(pieces) - 1,
                                                skip_group_check=True, tile_position=(0, h * HD))
                last.then_inc(summed, 1)

            pe.wait_ge(qk_loaded[0], LOADS)
            k = n = 0
            for kind, m in lead:
                if kind == "bank":
                    max_bank(0, k, m, 0)
                    k += 1
                elif kind == "row":
                    max_row(0, k, n, m, 0)
                    k += 1
                    n += 1
            with pe.Fori(0, STEPS2) as r:
                k, n = LEAD_BANKS, LEAD_ROWS
                kk = 0
                unit = a = 0
                seen = set()
                for o in order:
                    if o[0] == "bank":
                        if o[1] > 0 and o[1] not in seen:
                            seen.add(o[1])
                            pe.wait_ge(qk_loaded[o[1] % 2], LOADS * r + (LOADS if o[1] == 1 else 2 * LOADS))
                        max_bank(r, k, o[2], o[1] % 2)
                        k += 1
                    elif o[0] == "row":
                        max_row(r, k, n, o[2], o[1] % 2)
                        k += 1
                        n += 1
                    elif o[0] == "scores":
                        _, s, c, i, u, h = o
                        if i == 0 and h == 0:
                            q = s * NCH + c
                            pe.wait_ge(row_placed[q % 2], ROW0 + PLACED * (NCH * r + q // 2 + 1))
                        scores(r, kk, s, u, h)
                        kk += 1
                    elif o[0] == "values":
                        _, s, c, i, u, last = o
                        products(r, unit, s, c, i, u, last)
                        unit += 1
                    elif o[0] == "sums":
                        _, s, c, i, group, last = o
                        sums(r, a, s, c, i, group, last)
                        a += group[1] is not None


def finish(nc, x, xt_parts, ctx_parts, w_hi, w_lo, zstack, bstack, b_out, out, banks):
    TT, NH = TG // P, D // PSUM_BANK
    PAIRS = TT * NH
    with ExitStack() as ctx:
        def sb(name, shape, dt):
            return ctx.enter_context(nc.sbuf_tensor(name, shape, dt))

        def sem(name):
            return ctx.enter_context(nc.semaphore(name))

        xt = [[sb(f"xt{s}_{part}", [P, KC, TG], F16) for part in range(2)] for s in range(2)]
        ct = [[sb(f"ct{s}_{part}", [P, N_KV, TG], F16) for part in range(2)] for s in range(2)]
        xres = [sb(f"xres{s}", [P, TT, D], F32) for s in range(2)]
        bias = sb("bias", [P, D], F32)
        gate = [sb(f"gate{i}", [P, PSUM_BANK], F32) for i in range(2)]
        dense = [sb(f"dense{i}", [P, PSUM_BANK], F32) for i in range(2)]
        gated = [sb(f"gated{i}", [P, PSUM_BANK], F32) for i in range(2)]
        result = [sb(f"result{i}", [P, PSUM_BANK], F32) for i in range(2)]

        GATEB, DENSEB = banks[0:4], banks[4:8]

        bias_loaded = sem("bias_loaded")
        xt_loaded = [sem(f"xt_loaded{s}") for s in range(2)]
        ct_loaded = [sem(f"ct_loaded{s}") for s in range(2)]
        xres_loaded = [sem(f"xres_loaded{s}") for s in range(2)]
        gate_full = sem("gate_full")
        dense_full = sem("dense_full")
        gate_done = sem("gate_done")
        dense_done = sem("dense_done")
        gated_done = sem("gated_done")
        result_done = sem("result_done")
        stored = [sem(f"stored{i}") for i in range(2)]

        RING4, RING2 = 4, 2
        FULL0 = RESULTS0 = 2 * PAIRS
        LOADS = 2 * 16

        block = ctx.enter_context(nc.Block())

        @block.sync
        def _(sp):
            x_v = x.rearrange("(i t p) d -> i p t d", t=TT, p=P)
            sp.dma_start(bias[:, :], b_out.partition_broadcast(P)).then_inc(bias_loaded, 16)
            with sp.Fori(0, NCH) as r:
                for s in range(B):
                    sp.wait_ge(dense_full, r * 2 * PAIRS + (s + 1) * PAIRS)
                    sp.wait_ge(result_done, r * 2 * PAIRS + (s + 1) * PAIRS)
                    for part in range(2):
                        sp.dma_start(xt[s][part][:, :, :].rearrange("p k t -> p (k t)"),
                                     xt_parts[part, s * NCH + r]).then_inc(xt_loaded[s], 16)
                    for part in range(2):
                        sp.dma_start(ct[s][part][:, :, :],
                                     ctx_parts[part, s:GROUPS:2, r].rearrange("g p t -> p g t")).then_inc(ct_loaded[s], 16)
                    sp.dma_start(xres[s][:, :, :], x_v[s * NCH + r]).then_inc(xres_loaded[s], 16)

        @block.gpsimd
        def _(pool):
            pool.sem_inc(result_done, RESULTS0)
            with pool.Fori(0, STEPS // 2) as r:
                for n in range(2 * PAIRS):
                    s, t, half = n // PAIRS, n % PAIRS // NH, n % NH
                    if n % PAIRS == 0:
                        pool.wait_ge(xres_loaded[s], 16 * r + 16)
                    pool.wait_ge(stored[n % 2], 16 + r * 16 * PAIRS + 16 * (n // 2))
                    pool.wait_ge(gated_done, RING2 + r * 2 * PAIRS + n + 1)
                    nc.gpsimd.tensor_tensor(result[n % 2][:, :], gated[n % 2][:, :],
                                            xres[s][:, t, half * PSUM_BANK:(half + 1) * PSUM_BANK],
                                            ALU.add).then_inc(result_done, 1)

        @block.scalar
        def _(act):
            act.sem_inc(gate_done, RING4)
            act.sem_inc(stored[0], 16)
            act.sem_inc(stored[1], 16)
            o_v = out.rearrange("(i t p) d -> i t p d", t=TT, p=P)
            with act.Fori(0, STEPS // 2) as r:

                def store(n):
                    act.wait_ge(result_done, RESULTS0 + r * 2 * PAIRS + n + 1)
                    s, t, half = n // PAIRS, n % PAIRS // NH, n % NH
                    act.dma_start(o_v[s * NCH + r, t][:, half * PSUM_BANK:(half + 1) * PSUM_BANK],
                                  result[n % 2][:, :]).then_inc(stored[n % 2], 16)

                for n in range(2 * PAIRS):
                    act.wait_ge(gate_full, r * 2 * PAIRS + n + 1)
                    act.wait_ge(gated_done, r * 2 * PAIRS + n + 1)
                    nc.scalar.activation(gate[n % 2][:, :], GATEB[n % 4][:, :], ACT.Silu,
                                         scale=1.0 / WS).then_inc(gate_done, 1)
                    if n:
                        store(n - 1)
                store(2 * PAIRS - 1)
            for i in range(2):
                act.wait_ge(stored[i], 16 + 16 * STEPS * PAIRS // 2)

        @block.vector
        def _(dve):
            dve.sem_inc(dense_done, RING4)
            dve.sem_inc(gated_done, RING2)
            dve.wait_ge(bias_loaded, 16)
            with dve.Fori(0, STEPS // 2) as r:
                for n in range(2 * PAIRS):
                    half = n % NH
                    dve.wait_ge(dense_full, FULL0 + r * 2 * PAIRS + n + 1)
                    nc.vector.scalar_tensor_tensor(dense[n % 2][:, :], DENSEB[n % 4][:, :], 1.0 / (WS * CS),
                                                   bias[:, half * PSUM_BANK:(half + 1) * PSUM_BANK],
                                                   ALU.mult, ALU.add).then_inc(dense_done, 1)
                    dve.wait_ge(dense_done, RING4 + r * 2 * PAIRS + n + 1)
                    dve.wait_ge(gate_done, RING4 + r * 2 * PAIRS + n + 1)
                    dve.wait_ge(result_done, RESULTS0 - RING2 + r * 2 * PAIRS + n + 1)
                    nc.vector.tensor_tensor(gated[n % 2][:, :], dense[n % 2][:, :], gate[n % 2][:, :],
                                            ALU.mult).then_inc(gated_done, 1)

        @block.tensor
        def _(pe):
            pe.sem_inc(dense_full, FULL0)
            with pe.Fori(0, STEPS // 2) as r:

                def gates(n):
                    s, t, half = n // PAIRS, n % PAIRS // NH, n % NH
                    if n % PAIRS == 0:
                        pe.wait_ge(xt_loaded[s], LOADS * r + LOADS)
                    toks, cols = slice(t * P, (t + 1) * P), slice(half * PSUM_BANK, (half + 1) * PSUM_BANK)
                    pe.wait_ge(gate_done, r * 2 * PAIRS + n + 1)
                    for k in range(KC):
                        for m, (part, w) in enumerate(((0, w_hi), (0, w_lo), (1, w_hi))):
                            nc.tensor.matmul(GATEB[n % 4][:, :], xt[s][part][:, k, toks], w[:, KC + k, cols],
                                             start=(k == 0 and m == 0), stop=False)
                    nc.tensor.matmul(GATEB[n % 4][:, :], zstack[0:ZROWS, bass.ds(r * TG + s * S + t * P, P)],
                                     bstack[0:ZROWS, cols], start=False, stop=True).then_inc(gate_full, 1)

                def outputs(n):
                    s, t, half = n // PAIRS, n % PAIRS // NH, n % NH
                    if n % PAIRS == 0:
                        pe.wait_ge(ct_loaded[s], LOADS * r + LOADS)
                    toks, cols = slice(t * P, (t + 1) * P), slice(half * PSUM_BANK, (half + 1) * PSUM_BANK)
                    pe.wait_ge(dense_done, r * 2 * PAIRS + n + 1)
                    for k in range(KC):
                        for m, (part, w) in enumerate(((0, w_hi), (0, w_lo), (1, w_hi))):
                            last = nc.tensor.matmul(DENSEB[n % 4][:, :], ct[s][part][:, k, toks], w[:, k, cols],
                                                    start=(k == 0 and m == 0), stop=(k == KC - 1 and m == 2))
                    last.then_inc(dense_full, 1)

                gates(0)
                for n in range(2 * PAIRS):
                    if n + 1 < 2 * PAIRS:
                        gates(n + 1)
                    outputs(n)



def kernel(L0_attn_hidden_states, L0_attn_w_qkv, L0_attn_b_qkv, L0_attn_w_dense, L0_attn_b_dense,
           L0_ffn_W, L0_ffn_b, L0_ffn_A, L0_ffn_Bmat, L0_ffn_LiMEs):
    import numpy as np
    import concourse.bacc as bacc
    from concourse.bass_utils import run_bass_kernel_spmd

    w = np.asarray(L0_attn_w_qkv).reshape(N_KV, QH + 2, 2, HALF, D)
    bias = np.asarray(L0_attn_b_qkv).reshape(N_KV, QH + 2, 2, HALF)
    w_q = w[:, :QH].transpose(0, 2, 1, 3, 4).reshape(N_KV * QH * HD, D)
    b_q = bias[:, :QH].transpose(0, 2, 1, 3).reshape(-1)
    w_k = w[:, QH].reshape(2, N_KV // 2, 2, HALF, D).transpose(0, 2, 1, 3, 4).reshape(N_KV * HD, D)
    b_k = bias[:, QH].reshape(2, N_KV // 2, 2, HALF).transpose(0, 2, 1, 3).reshape(-1)
    w_v = w[:, QH + 1].reshape(NV, D)
    b_v = np.concatenate([bias[:, QH + 1].reshape(-1), np.asarray(L0_ffn_b)[:E], np.zeros(RANK, np.float32)]).reshape(1, -1)
    ffn_w = np.asarray(L0_ffn_W)
    w1 = np.concatenate([w_q.T, w_k.T, w_v.T, ffn_w[:E].T, np.asarray(L0_ffn_A)], axis=1)
    w_out = np.concatenate([np.asarray(L0_attn_w_dense).T, ffn_w.T], axis=0)

    f32 = np.float32
    inv_freq = (1.0 / 1000000.0 ** (np.arange(0, HD, 2) / HD)).astype(f32)
    angle = np.arange(S, dtype=f32)[None, :] * inv_freq[:, None]
    cos, sin = np.cos(angle.astype(np.float64)), np.sin(angle.astype(np.float64))
    rope = np.stack([np.tile(cos, (2 * QH, 1)), np.concatenate([np.tile(sin, (QH, 1)), np.tile(-sin, (QH, 1))])], axis=1)
    i = np.arange(P)
    later = np.where(i[None, :] > i[:, None], NEG, 0.0)
    consts = np.concatenate([np.eye(P), i[:, None] == 2 * (i[None, :] // 2) + 1, later, later.T,
                             np.repeat(np.where(i < BLK, NEG, 0.0)[:, None], BLK, axis=1),
                             np.repeat(np.where(i >= BLK, NEG, 0.0)[:, None], BLK, axis=1)], axis=1)
    arrays = {
        "x": np.asarray(L0_attn_hidden_states).reshape(B * S, D),
        "w1": w1,
        "b_qk": np.concatenate([b_q, b_k]).reshape(NF, P).T,
        "b_v": b_v,
        "w_out": w_out,
        "b_out": np.asarray(L0_attn_b_dense).reshape(1, D),
        "b_ffn": np.asarray(L0_ffn_b).reshape(1, D),
        "adapter_out": np.asarray(L0_ffn_Bmat),
        "limes": np.asarray(L0_ffn_LiMEs),
        "limes_t": np.asarray(L0_ffn_LiMEs).T,
        "rope": rope.astype(f32),
        "consts": consts.astype(f32),
    }
    arrays = {name: np.ascontiguousarray(a) for name, a in arrays.items()}
    nc = bacc.Bacc("TRN2", target_bir_lowering=False, num_devices=1)
    args = [nc.dram_tensor(name, a.shape, F32, kind="ExternalInput").ap() for name, a in arrays.items()]
    out = nc.dram_tensor("out", (B * S, D), F32, kind="ExternalOutput").ap()
    mk_recurrent_d1(nc, *args, out)
    r = run_bass_kernel_spmd(nc, [arrays], core_ids=[0])
    return r.results[0]["out"].reshape(B, S, D)
```

```python
from contextlib import ExitStack

import concourse.bass as bass
from concourse import mybir

ALU = mybir.AluOpType
ACT = mybir.ActivationFunctionType
F32 = mybir.dt.float32
F16 = mybir.dt.float16
BF16 = mybir.dt.bfloat16
AX = mybir.AxisListType
RMAX = bass.bass_isa.ReduceOp.max

P = 128
B, S, D = 2, 2048, 1024
KC = D // P
N_KV, QH, HD = 8, 4, 32
HALF = HD // 2
GROUPS = B * N_KV
TG = 512
STEPS = B * S // TG
E, RANK = 8, 32
NQK = N_KV * (QH + 1) * HD
NF = NQK // P
NV = N_KV * HD
NAT = E + RANK
NVA = NV + NAT
W1N = NVA + NQK
BLK, LOCAL, VERT = 64, 16, 8
NT = S // P
NCH = S // TG
SM_SCALE = 1.0 / HD
ALPHA_OVER_RANK = 16.0 / RANK
WS = 256.0
CS = 256.0
SHIFT = 2048.0
NEG = -1.0e30
LOWEST = -3.0e38
LN_EPS = 1e-5
SCALE_EPS = 1e-6
ONES_ROW = 256.0
PSUM_BANK = 512
STACK = 3 * HD
ZROWS = 3 * RANK + 3
STAGES = 4
MAXRING, SCORERING, PROBRING, ADDRING = 3, 3, 6, 2
GROUP = 3
HOP, PLACING, LEAD, RESERVE = 280.0, 2500.0, 4500, 1000



def is_vertical(block):
    return (block + 1) % VERT == 0


def max_banks(t):
    banks = []
    if 2 * t + 1 < LOCAL:
        start, n = 0, P * (t + 1)
    else:
        start, n = BLK * (2 * t - LOCAL + 2), P * (LOCAL // 2)
    full, rest = n // PSUM_BANK, n % PSUM_BANK
    for seg in range(full):
        for h in range(QH):
            banks.append(dict(t=t, heads=[h], pieces=[(start + seg * PSUM_BANK, PSUM_BANK)], seg=seg,
                              mask="diagonal" if rest == 0 and seg == full - 1 else None))
    if rest:
        per = min(QH, PSUM_BANK // rest)
        for h in range(0, QH, per):
            banks.append(dict(t=t, heads=list(range(h, h + per)), pieces=[(start + full * PSUM_BANK, rest)],
                              seg=full, mask="diagonal"))
    if start > 0:
        oldest = 2 * t - LOCAL + 1
        pieces = [(BLK * oldest, BLK)]
        pieces += [(BLK * j, BLK) for j in range(oldest) if is_vertical(j)]
        banks.append(dict(t=t, heads=list(range(QH)), pieces=pieces, seg=full,
                          mask=None if is_vertical(oldest) else "late queries"))
    return banks


def key_units(c):
    per = TG // BLK
    units = []
    for j in range(min(NT, (c + 1) * TG // P)):
        lo, hi = max(per * c, 2 * j), min(per * c + per - 1, 2 * j + LOCAL)
        if is_vertical(2 * j + 1):
            hi = per * c + per - 1
        if lo > hi:
            continue
        far = max(0, hi - max(lo, 2 * j + LOCAL) + 1)
        units.append((j, lo, hi - lo + 1, 2 * j >= per * c, far))
    return sorted(units, key=lambda u: (-(u[2] == per), u[1], u[2] if u[1] == per * c else -u[2]))


def sum_groups(c):
    units = key_units(c)
    spans = [((lo - c * (TG // BLK)) * BLK, (lo - c * (TG // BLK) + n) * BLK) for _, lo, n, _, _ in units]
    groups, i = [], 0
    while i < len(units):
        members, direct = [i], []
        start, end = spans[i]
        adds = []
        while len(members) < GROUP and i + 1 < len(units):
            a, b = max(start, spans[i + 1][0]), min(end, spans[i + 1][1])
            if b - a < 2 * BLK:
                break
            if len(members) == 1:
                direct += [(i, start, a - start), (i, b, end - b)]
                start, end = a, b
            i += 1
            members.append(i)
            adds.append((i, a, b - a))
            direct += [(i, spans[i][0], a - spans[i][0]), (i, b, spans[i][1] - b)]
        if not adds:
            direct = [(i, start, end - start)]
        direct = [d for d in direct if d[2] > 0]
        groups.append((tuple(members), (start, end - start) if adds else None, adds, direct))
        i += 1
    return groups


def max_stream():
    out, due = [], []
    for c in range(NCH):
        for t in range(c * NCH, c * NCH + TG // P):
            for bank in max_banks(t):
                out.append(("bank", bank))
                due = [(n - 1, d) for n, d in due]
                while due and due[0][0] == 0:
                    out.append(("row", due.pop(0)[1]))
        out.append(("fold", c))
        due.append((3, c))
    out += [("row", d) for _, d in due]
    return out


def bank_columns(bank):
    return len(bank["heads"]) * sum(w for _, w in bank["pieces"])


def work_of(kind, item):
    if kind == "bank":
        columns = bank_columns(item)
        return 0.42 * columns + (56 if item["mask"] else 0) + 20, 1.1 * columns + 70
    if kind == "row":
        return 60, 150
    if kind == "fold":
        return 0, 250
    if kind == "scores":
        _, _, n, diagonal, far = item
        return 27 * n + 27 * far + (56 if diagonal else 0), 54 * n + 60
    if kind == "values":
        return 117 * item[2], 0
    if kind == "sums":
        _, span, _, direct = item
        return 1.83 * ((span[1] if span else 0) + sum(w for _, _, w in direct)), 0
    if kind == "add":
        return 0, 9.0 * item[2] + 80
    raise ValueError(kind)


def attention_order():
    maxima = max_stream()
    units = [(c, i, u) for c in range(NCH) for i, u in enumerate(key_units(c))]
    total = sum(bank_columns(m[1]) for m in maxima if m[0] == "bank")
    done, row_at = 0, {}
    for kind, m in maxima:
        if kind == "bank":
            done += bank_columns(m)
        elif kind == "row":
            row_at[m] = done
    begin, at = {}, 0
    span = sum(QH * BLK * u[2] for _, _, u in units)
    for c, i, u in units:
        if i == 0:
            begin[c] = at * total / span
        at += QH * BLK * u[2]
    lead = max(row_at[c] - begin[c] for c in range(NCH)) + LEAD
    ahead, done = 0, 0
    while done < lead:
        if maxima[ahead][0] == "bank":
            done += bank_columns(maxima[ahead][1])
        ahead += 1
    stream = [(0, m) for m in maxima[ahead:]] + [(1, m) for m in maxima] + [(2, m) for m in maxima[:ahead]]

    scores = [(s, c, i, u, h) for s in range(2) for c, i, u in units for h in range(QH)]
    order, inversions = [], []
    pe = act = dve = pool = 0.0
    read, exps = [0.0] * MAXRING, [0.0] * SCORERING
    values, sums, free = [], [], {}
    placed, shifted = {}, {}
    pos = at = taken = 0
    n_scores = n_values = n_adds = 0
    unit_at = {(s, c, i): n for n, (s, c, i) in
               enumerate((s, c, i) for s in range(2) for c, i, _ in units)}
    add_free, out_at = [0.0] * ADDRING, [0.0, 0.0]
    while at < len(scores) or pos < len(stream) or values or sums:
        options = []
        if at < len(scores):
            s, c, i, u, h = scores[at]
            ready = max(exps[-SCORERING], free.get(unit_at[s, c, i] - PROBRING, 0.0) - 700)
            blocked = any(m == ("row", c) and g == s for g, m in stream[pos:])
            ready = max(ready, placed.get((s, c), 0.0))
            pace = n_scores * (2 * total - RESERVE) / (2 * span)
            before = unit_at[s, c, i] - PROBRING
            blocked = blocked or before >= n_values or any(
                before == unit_at[x[1], x[2], m] for x in sums for m, _, _ in x[4][3])
            if not blocked:
                options.append((ready, 2 if taken >= pace else 3, "scores"))
        if pos < len(stream):
            g, (kind, m) = stream[pos]
            ready = read[-MAXRING] if kind != "fold" else 0.0
            if kind == "row":
                ready = max(ready, shifted[g, m])
            late = taken < n_scores * (2 * total - RESERVE) / (2 * span) or at == len(scores)
            options.append((ready, 2 if late else 3, "max"))
        if values:
            options.append((values[0][0], 1, "values"))
        if sums:
            options.append((sums[0][0], 4, "sums"))
        now = [o for o in options if o[0] <= pe]
        ready, _, kind = min(now, key=lambda o: (o[1], o[0])) if now else min(options, key=lambda o: (o[0], o[1]))
        pe = max(pe, ready)
        if kind == "scores":
            mine, next_one = work_of("scores", u)
            pe += mine
            act = max(act, pe + HOP) + next_one
            exps.append(act + HOP)
            order.append(("scores", s, c, i, u, h))
            at += 1
            n_scores += BLK * u[2]
            if h == QH - 1:
                values.append((act + HOP, s, c, i, u))
                for n, group in enumerate(sum_groups(c)):
                    members, _, adds, _ = group
                    for j, add in enumerate(adds):
                        if add[0] == i:
                            pool = max(act + HOP, pool, add_free[-ADDRING] if j == 0 else 0.0) + work_of("add", add)[1]
                            for m in members[:2] if j == 0 else (i,):
                                free[unit_at[s, c, m]] = pool + HOP
                    if members[-1] == i:
                        sums.append((pool + HOP if adds else act + HOP, s, c, n, group))
                        if adds:
                            add_free.append(pool + 3000)
        elif kind == "max":
            g, (kind, m) = stream[pos]
            pos += 1
            mine, next_one = work_of(kind, m)
            pe += mine
            order.append((kind, g, m))
            dve = max(dve, pe + HOP) + next_one
            if kind == "fold":
                shifted[g, m] = dve + HOP
                continue
            read.append(dve + HOP)
            if kind == "bank":
                taken += bank_columns(m)
            else:
                placed[g, m] = dve + PLACING
            if inversions:
                o = inversions.pop(0)
                order.append(o)
                if o[0] == "invert":
                    dve += 750
                else:
                    pool = max(pool, dve) + 3500
        elif kind == "values":
            _, s, c, i, u = values.pop(0)
            pe = max(pe, out_at[0] if i == 0 else 0.0) + work_of("values", u)[0]
            n_values += 1
            k = unit_at[s, c, i]
            free[k] = max(free.get(k, 0.0), pe + HOP)
            last = i == len(key_units(c)) - 1
            order.append(("values", s, c, i, u, last))
            if last:
                order.append(("context", s, c))
                act = max(act, pe + HOP) + 480
                out_at[0] = act + HOP
        else:
            _, s, c, n, group = sums.pop(0)
            pe = max(pe, out_at[1] if n == 0 else 0.0) + work_of("sums", group)[0]
            for m, _, _ in group[3]:
                k = unit_at[s, c, m]
                free[k] = max(free.get(k, 0.0), pe + HOP)
            last = n == len(sum_groups(c)) - 1
            order.append(("sums", s, c, n, group, last))
            if last:
                order.append(("totals", s, c))
                act = max(act, pe + HOP) + 480
                out_at[1] = act + HOP
                inversions += [("invert", s, c, piece) for piece in range(2)] + [("split", s, c)]
    return order + inversions, maxima[:ahead]



def mk_recurrent_d1(nc, x, w1, b_qk, b_v, w_out, b_out, b_ffn, adapter_out, limes, limes_t, rope, consts, out):
    q_parts = nc.dram_tensor("q_parts", [2, N_KV + 1, P, B * S], F16).ap()
    k_parts = nc.dram_tensor("k_parts", [2, N_KV + 1, HD, B * S], F16).ap()
    v_parts = nc.dram_tensor("v_parts", [N_KV + 1, B, P, NT * HD], F32).ap()
    xt_parts = nc.dram_tensor("xt_parts", [2, STEPS, P, KC * TG], F16).ap()
    ctx_parts = nc.dram_tensor("ctx_parts", [2, GROUPS, NCH, P, TG], F16).ap()

    with ExitStack() as whole:
        def keep(name, shape, dt):
            return whole.enter_context(nc.sbuf_tensor(name, shape, dt))

        ident32 = keep("ident32", [P, P], F32)
        ident16 = keep("ident16", [P, P], F16)
        ident_bf = keep("ident_bf", [P, P], BF16)
        pair_odd = keep("pair_odd", [P, P], F32)
        mask_q = keep("mask_q", [P, P], BF16)
        mask_k = keep("mask_k", [P, P], BF16)
        mask_early = keep("mask_early", [P, BLK], BF16)
        mask_late = keep("mask_late", [P, BLK], BF16)
        zstack = keep("zstack", [P, B * S], F16)
        bstack = keep("bstack", [P, D], F16)
        banks = [whole.enter_context(nc.psum_tensor(f"bank{i}", [P, PSUM_BANK], F32)) for i in range(8)]

        in_attention = whole.enter_context(ExitStack())
        with ExitStack() as stage:
            stages = stage.enter_context(nc.sbuf_tensor("stages", [P, STAGES, KC * P], F32))
            both = stage.enter_context(nc.sbuf_tensor("both", [P, 2, B * NT * E], F32))
            project(nc, x, w1, b_qk, b_v, rope, consts, limes_t, adapter_out, b_ffn, q_parts, k_parts, xt_parts,
                    v_parts, ident32, ident16, ident_bf, pair_odd, mask_q, mask_k, mask_early, mask_late,
                    stages, both, zstack, bstack, banks)

            def for_attention(name, shape, dt):
                return in_attention.enter_context(nc.sbuf_tensor(name, shape, dt, side="right"))

            q_stack = [for_attention(f"q_stack{i}", [STACK + 1, QH, S], F16) for i in range(2)]
            k_stack = [for_attention(f"k_stack{i}", [STACK + 1, S], F16) for i in range(2)]
            v_slot = [for_attention(f"v_slot{i}", [P, NT, HD], F32) for i in range(2)]
            qk_loaded = [in_attention.enter_context(nc.semaphore(f"qk_loaded{i}")) for i in range(2)]

            def load_group(eng, slot, n):
                q, k = q_stack[slot], k_stack[slot]
                toks = slice(slot * S, (slot + 1) * S)
                for row, part in enumerate((0, 1, 0)):
                    for a in range(2):
                        at = row * HD + a * HALF
                        eng.dma_start(q[at:at + HALF, :, :],
                                      q_parts[part, n, a * QH * HALF:(a + 1) * QH * HALF, toks].rearrange("(h r) t -> r h t", r=HALF)
                                      ).then_inc(qk_loaded[slot], 16)
                for row, part in enumerate((0, 0, 1)):
                    eng.dma_start(k[row * HD:(row + 1) * HD, :], k_parts[part, n, :, toks]).then_inc(qk_loaded[slot], 16)
                eng.dma_start(v_slot[slot][:, :, :].rearrange("p t d -> p (t d)"), v_parts[n, slot]).then_inc(qk_loaded[slot], 16)

            route(nc, limes, stages, both, ident32, pair_odd, zstack, load_group, banks)
        with ExitStack() as stage:
            w_hi = stage.enter_context(nc.sbuf_tensor("w_hi", [P, 2 * KC, D], F16))
            w_lo = stage.enter_context(nc.sbuf_tensor("w_lo", [P, 2 * KC, D], F16))
            attend(nc, ctx_parts, w_out, w_hi, w_lo, q_stack, k_stack, v_slot, qk_loaded, load_group,
                   ident16, ident_bf, mask_q, mask_k, mask_early, mask_late, banks)
            in_attention.close()
            finish(nc, x, xt_parts, ctx_parts, w_hi, w_lo, zstack, bstack, b_out, out, banks)


def project(nc, x, w1, b_qk, b_v, rope, consts, limes_t, adapter_out, b_ffn, q_parts, k_parts, xt_parts,
            v_parts, ident32, ident16, ident_bf, pair_odd, mask_q, mask_k, mask_early, mask_late,
            stages, both, zstack, bstack, banks):
    WP = P
    pieces = [(c, min(WP, NVA - c)) for c in range(0, NVA, WP)] + [(c, WP) for c in range(NVA, W1N, WP)]
    NVP = len(pieces) - NF
    TT = TG // P
    with ExitStack() as ctx:
        def sb(name, shape, dt):
            return ctx.enter_context(nc.sbuf_tensor(name, shape, dt))

        def sem(name):
            return ctx.enter_context(nc.semaphore(name))

        xin = [sb(f"xin{i}", [P, TT, D], F32) for i in range(2)]
        cpack = sb("cpack", [P, 4 * P + 2 * BLK], F32)
        w1_hi = sb("w1_hi", [P, KC, W1N], F16)
        w1_lo = sb("w1_lo", [P, KC, W1N], F16)
        wstage = [stages[:, i, :].rearrange("p (k n) -> p k n", n=WP) for i in range(STAGES)]
        z_t = stages[0:RANK, :, :].rearrange("p a n -> p (a n)")
        natural_z = [sb(f"natural_z{i}", [P, TT, RANK], F32) for i in range(2)]
        z_step = [sb(f"z_step{i}", [RANK, TG], F32) for i in range(2)]
        lim_t = sb("lim_t", [RANK, E], F32)
        rest, amat, brow = xin[0][0:1, 0:2, :], xin[0][0:RANK, 2, :], xin[0][0:1, 3, :]
        bparts = sb("bparts", [1, 3, D], F16)
        bqk = sb("bqk", [P, NF], F32)
        bv = sb("bv", [P, NV + NAT], F32)
        table = sb("table", [P, 2, S], F32)
        eps = sb("eps", [P, 1], F32)
        stats = sb("stats", [P, TT, 12], F32)
        moments = sb("moments", [P, TT, 2], F32)
        deviation = sb("deviation", [P, TT], F32)
        rstd = sb("rstd", [P, TT], F32)
        xt_hi = [sb(f"xt_hi{i}", [P, KC, TG], F16) for i in range(2)]
        xt_lo = [sb(f"xt_lo{i}", [P, KC, TG], F16) for i in range(2)]
        raw = [sb(f"raw{i}", [P, TG], F32) for i in range(2)]
        by_cos = [sb(f"by_cos{i}", [P, TG], F32) for i in range(2)]
        by_sin = [sb(f"by_sin{i}", [P, TG], F32) for i in range(2)]
        rotated = [sb(f"rotated{i}", [P, TG], F32) for i in range(2)]
        r_hi = [sb(f"r_hi{i}", [P, TG], F16) for i in range(2)]
        r_lo = [sb(f"r_lo{i}", [P, TG], F16) for i in range(2)]
        vst = [sb(f"vst{i}", [P, N_KV, TT * HD], F32) for i in range(2)]
        zero16, zero32 = xt_hi[1], vst[1]

        TURN, PROJ = banks[0:2], banks[2:6]
        ZB, DELTAB = banks[6], banks[7]

        c_loaded = sem("c_loaded")
        small_loaded = sem("small_loaded")
        c_ready = sem("c_ready")
        w_loaded = [sem(f"w_loaded{i}") for i in range(STAGES)]
        w_hi_done = sem("w_hi_done")
        w_lo_done = sem("w_lo_done")
        zeroed = sem("zeroed")
        pad_stored = sem("pad_stored")
        x_loaded = [sem(f"x_loaded{i}") for i in range(2)]
        stats_done = sem("stats_done")
        moments_done = sem("moments_done")
        deviation_done = sem("deviation_done")
        rstd_done = sem("rstd_done")
        xn_done = sem("xn_done")
        turned = sem("turned")
        xt_hi_done = sem("xt_hi_done")
        xt_lo_done = sem("xt_lo_done")
        xt_stored = [sem(f"xt_stored{i}") for i in range(2)]
        projected = sem("projected")
        raw_done = sem("raw_done")
        v_done = sem("v_done")
        z_turned = sem("z_turned")
        z_copied = sem("z_copied")
        delta_full = sem("delta_full")
        delta_out = sem("delta_out")
        adapter_loaded = sem("adapter_loaded")
        b_steps = sem("b_steps")
        b_placed = sem("b_placed")
        v_stored = [sem(f"v_stored{i}") for i in range(2)]
        parts_done = sem("parts_done")
        rotated_done = sem("rotated_done")
        r_hi_done = sem("r_hi_done")
        r_lo_done = sem("r_lo_done")
        r_stored = [sem(f"r_stored{i}") for i in range(2)]

        LO0 = 2
        PROJ0 = 2 * (NF + TT)
        RAW0 = 4
        RING0 = 2
        STORED0 = 64
        PADS = 5 * 16
        B_STEPS = 6

        EARLY = 3
        TURN_AT = 6
        Z_AT, DELTA_AT = 8, 11

        def following(r, s):
            return (r, 1) if s == 0 else (r + 1, 0)

        def step_of(r, s):
            return 2 * r + s

        def tokens(r, s):
            return bass.ds(r * TG + s * S, TG)

        def stores_of(f):
            return 2 if f < N_KV else 4

        STEP_STORES = [16 * sum(stores_of(f) for f in range(i, NF, 2)) for i in range(2)]

        def for_all_steps(eng, body):
            with eng.Fori(0, NCH - 1) as r:
                body(r, False)
            body(NCH - 1, True)

        block = ctx.enter_context(nc.Block())

        @block.sync
        def _(sp):
            sp.dma_start(cpack[:, :], consts).then_inc(c_loaded, 16)
            w_v = w1.rearrange("(k p) n -> p k n", p=P)
            for n, (c, w) in enumerate(pieces):
                if n >= STAGES:
                    sp.wait_ge(w_lo_done, n - STAGES + 1)
                sp.dma_start(wstage[n % STAGES][:, :, 0:w], w_v[:, :, c:c + w]).then_inc(w_loaded[n % STAGES], 16)
                if n == STAGES:
                    sp.dma_start(lim_t[:, :], limes_t).then_inc(small_loaded, 16)
                    sp.dma_start(bqk[:, :], b_qk).then_inc(small_loaded, 16)
                    sp.dma_start(bv[:, :], b_v.partition_broadcast(P)).then_inc(small_loaded, 16)
                    sp.dma_start(table[:, :, :], rope).then_inc(small_loaded, 16)
            sp.wait_ge(zeroed, 2)
            for part in range(2):
                sp.dma_start(q_parts[part, N_KV, :, 0:S], zero16[:, 0:NCH, :].rearrange("p a b -> p (a b)")).then_inc(pad_stored, 16)
                sp.dma_start(k_parts[part, N_KV, :, 0:S], zero16[0:HD, 0:NCH, :].rearrange("p a b -> p (a b)")).then_inc(pad_stored, 16)
            sp.dma_start(v_parts[N_KV, 0], zero32[:, 0:N_KV // 2, :].rearrange("p a b -> p (a b)")).then_inc(pad_stored, 16)


            def body(r, last):
                for s in range(B):
                    sp.wait_ge(xt_lo_done, LO0 + (step_of(r, s) + 1) * KC)
                    if last and s == 1:
                        sp.dma_start(amat, adapter_out).then_inc(adapter_loaded, 16)
                        sp.dma_start(brow, b_ffn).then_inc(adapter_loaded, 16)
                    for part, xt in enumerate((xt_hi, xt_lo)):
                        sp.dma_start(xt_parts[part, s * NCH + r],
                                     xt[s][:, :, :].rearrange("p k t -> p (k t)")).then_inc(xt_stored[s], 16)
                    sp.wait_ge(v_done, (step_of(r, s) + 1) * TT)
                    sp.dma_start(v_parts[0:N_KV, s, :, bass.ds(r * TT * HD, TT * HD)].rearrange("g p x -> p g x"),
                                 vst[s][:, :, :]).then_inc(v_stored[s], 16)
                    for f in range(NF):
                        sp.wait_ge(r_lo_done, RING0 + step_of(r, s) * NF + f + 1)
                        for part, half in enumerate((r_hi, r_lo)):
                            if f < N_KV:
                                sp.dma_start(q_parts[part, f, :, tokens(r, s)], half[f % 2][:, :]).then_inc(r_stored[f % 2], 16)
                                continue
                            for a in range(2):
                                sp.dma_start(k_parts[part, (f - N_KV) * QH:(f - N_KV + 1) * QH,
                                                     a * HALF:(a + 1) * HALF, tokens(r, s)],
                                             half[f % 2][a * QH * HALF:(a + 1) * QH * HALF, :]).then_inc(r_stored[f % 2], 16)

            for_all_steps(sp, body)
            sp.wait_ge(b_steps, B_STEPS)
            for i in range(3):
                sp.dma_start(bstack[3 * RANK + i:3 * RANK + i + 1, :], bparts[0:1, i, :]).then_inc(b_placed, 16)
            sp.wait_ge(pad_stored, PADS)
            sp.wait_ge(b_placed, 48)
            for s in range(2):
                sp.wait_ge(v_stored[s], 16 + 16 * NCH)
                sp.wait_ge(xt_stored[s], STORED0 + 32 * NCH)
                sp.wait_ge(r_stored[s], STORED0 + STEP_STORES[s] * STEPS)

        @block.gpsimd
        def _(pool):
            nc.gpsimd.memset(zero16[:, :, :], 0.0).then_inc(zeroed, 1)
            pool.wait_ge(zeroed, 1)
            nc.gpsimd.memset(zero32[:, :, :], 0.0).then_inc(zeroed, 1)
            pool.wait_ge(zeroed, 2)
            nc.gpsimd.memset(zstack[3 * RANK:ZROWS, :], ONES_ROW).then_inc(zeroed, 1)
            pool.wait_ge(zeroed, 3)
            pool.sem_inc(rotated_done, RING0)
            with pool.Fori(0, NCH) as r:
                for s in range(B):
                    for f in range(NF):
                        k = step_of(r, s) * NF + f
                        pool.wait_ge(parts_done, RING0 + k + 1)
                        pool.wait_ge(r_lo_done, k + 1)
                        nc.gpsimd.tensor_tensor(rotated[f % 2][:, :], by_cos[f % 2][:, :], by_sin[f % 2][:, :],
                                                ALU.add).then_inc(rotated_done, 1)

        @block.scalar
        def _(act):
            x_v = x.rearrange("(i t p) d -> i t p d", t=TT, p=P)

            def load_x(r, s):
                for t in range(TT):
                    act.dma_start(xin[s][:, t, :], x_v[s * NCH + r, t]).then_inc(x_loaded[s], 16)

            def split_weights(n):
                c, w = pieces[n]
                act.wait_ge(w_loaded[n % STAGES], 16 * (n // STAGES + 1))
                nc.scalar.activation(w1_hi[:, :, c:c + w], wstage[n % STAGES][:, :, 0:w], ACT.Copy,
                                     scale=WS).then_inc(w_hi_done, 1)

            def deviate(r, s):
                act.wait_ge(moments_done, (step_of(r, s) + 1) * TT)
                nc.scalar.activation(deviation[:, :], moments[:, :, 1], ACT.Sqrt,
                                     bias=eps[:, 0:1]).then_inc(deviation_done, 1)

            def split_xt(r, s, k):
                if k == 0:
                    act.wait_ge(projected, (step_of(r, s) + 1) * (NF + TT))
                    act.wait_ge(xt_stored[s], STORED0 + 32 * r)
                act.wait_ge(turned, step_of(r, s) * KC + k + 1)
                nc.scalar.activation(xt_hi[s][:, k, :], TURN[k % 2][:, :], ACT.Copy).then_inc(xt_hi_done, 1)

            load_x(0, 0)
            act.sem_inc(raw_done, RAW0)
            act.sem_inc(z_copied, 1)
            for i in range(2):
                act.sem_inc(r_stored[i], STORED0)
                act.sem_inc(xt_stored[i], STORED0)
            for n in range(EARLY):
                split_weights(n)
            deviate(0, 0)
            load_x(0, 1)
            for k in range(KC):
                split_xt(0, 0, k)
            for n in range(EARLY, len(pieces)):
                split_weights(n)
            act.wait_ge(small_loaded, 64)
            act.wait_ge(pad_stored, PADS)
            act.wait_ge(w_lo_done, len(pieces))

            def body(r, last):

                def split_rotated(s, f):
                    act.wait_ge(rotated_done, RING0 + step_of(r, s) * NF + f + 1)
                    before = sum(16 * stores_of(i) for i in range(f % 2, f, 2))
                    act.wait_ge(r_stored[f % 2], STORED0 + step_of(r, s) * STEP_STORES[f % 2] + before)
                    nc.scalar.activation(r_hi[f % 2][:, :], rotated[f % 2][:, :], ACT.Copy).then_inc(r_hi_done, 1)

                for s in range(B):
                    more = not (last and s == 1)
                    if not last:
                        act.wait_ge(turned, (step_of(r, s) + 1) * KC)
                        load_x(r + 1, s)
                    for i in range(TT + NF):
                        f = i - TT
                        if f == 0 and more:
                            deviate(*following(r, s))
                        if more and TURN_AT <= i < TURN_AT + KC:
                            split_xt(*following(r, s), i - TURN_AT)
                        if i == Z_AT + 1:
                            act.wait_ge(z_turned, step_of(r, s) + 1)
                            nc.scalar.activation(z_step[s][:, :], ZB[0:RANK, :], ACT.Copy)
                            nc.scalar.activation(z_t[:, tokens(r, s)], ZB[0:RANK, :], ACT.Copy).then_inc(z_copied, 1)
                        if f >= 0:
                            act.wait_ge(projected, PROJ0 + step_of(r, s) * (NF + TT) + i + 1)
                            act.wait_ge(parts_done, step_of(r, s) * NF + f + 1)
                            nc.scalar.activation(raw[f % 2][:, :], PROJ[(s * (NF + TT) + i) % 4][:, :], ACT.Identity,
                                                 bias=bqk[:, f:f + 1], scale=1.0 / WS).then_inc(raw_done, 1)
                        if f > 0:
                            split_rotated(s, f - 1)
                    split_rotated(s, NF - 1)

            for_all_steps(act, body)

        @block.vector
        def _(dve):

            def split_weights(n):
                c, w = pieces[n]
                dve.wait_ge(w_hi_done, n + 1)
                nc.vector.scalar_tensor_tensor(w1_lo[:, :, c:c + w], wstage[n % STAGES][:, :, 0:w], WS,
                                               w1_hi[:, :, c:c + w], ALU.mult, ALU.subtract).then_inc(w_lo_done, 1)

            def take_stats(r, s, t):
                if t == 0:
                    dve.wait_ge(x_loaded[s], 16 * TT * r + 16 * TT)
                for i in range(2):
                    nc.vector.bn_stats(stats[:, t, 6 * i:6 * i + 6],
                                       xin[s][:, t, i * 512:(i + 1) * 512]).then_inc(stats_done, 1)

            def normalise(r, s):
                n = step_of(r, s) + 1
                dve.wait_ge(stats_done, n * 2 * TT)
                nc.vector.memset(rstd[:, :], 0.0)
                for t in range(TT):
                    nc.vector.bn_aggr(moments[:, t, :], stats[:, t, :]).then_inc(moments_done, 1)
                dve.wait_ge(deviation_done, n)
                nc.vector.reciprocal(rstd[:, :], deviation[:, :]).then_inc(rstd_done, 1)
                dve.wait_ge(rstd_done, n)
                for t in range(TT):
                    nc.vector.tensor_scalar(xin[s][:, t, :], xin[s][:, t, :], moments[:, t, 0:1], rstd[:, t:t + 1],
                                            ALU.subtract, ALU.mult).then_inc(xn_done, 1)

            def split_xt(r, s, k):
                dve.wait_ge(xt_hi_done, step_of(r, s) * KC + k + 1)
                nc.vector.tensor_tensor(xt_lo[s][:, k, :], TURN[k % 2][:, :], xt_hi[s][:, k, :],
                                        ALU.subtract).then_inc(xt_lo_done, 1)

            nc.vector.memset(eps[:, :], LN_EPS)
            dve.sem_inc(xt_lo_done, LO0)
            dve.sem_inc(parts_done, RING0)
            dve.sem_inc(r_lo_done, RING0)
            dve.sem_inc(delta_out, 1)
            dve.sem_inc(v_stored[0], 16)
            dve.sem_inc(v_stored[1], 16)
            dve.wait_ge(c_loaded, 16)
            for dst, at, w in ((ident32, 0, P), (ident16, 0, P), (ident_bf, 0, P), (pair_odd, P, P),
                               (mask_q, 2 * P, P), (mask_k, 3 * P, P), (mask_early, 4 * P, BLK),
                               (mask_late, 4 * P + BLK, BLK)):
                nc.vector.tensor_copy(dst[:, :], cpack[:, at:at + w]).then_inc(c_ready, 1)
            for n in range(EARLY):
                split_weights(n)
            for t in range(TT):
                take_stats(0, 0, t)
            normalise(0, 0)
            for k in range(KC):
                split_xt(0, 0, k)
            for n in range(EARLY, len(pieces)):
                split_weights(n)
            dve.wait_ge(small_loaded, 64)
            dve.wait_ge(pad_stored, PADS)

            def split_adapter():
                dve.wait_ge(adapter_loaded, 32)
                steps = [0]

                def step(ins):
                    steps[0] += 1
                    ins.then_inc(b_steps, 1)
                    dve.wait_ge(b_steps, steps[0])

                step(nc.vector.tensor_copy(bparts[:, 0, :], brow))
                step(nc.vector.tensor_tensor(rest[:, 0, :], brow, bparts[:, 0, :], ALU.subtract))
                step(nc.vector.tensor_copy(bparts[:, 1, :], rest[:, 0, :]))
                step(nc.vector.tensor_tensor(rest[:, 1, :], rest[:, 0, :], bparts[:, 1, :], ALU.subtract))
                step(nc.vector.tensor_copy(bparts[:, 2, :], rest[:, 1, :]))
                step(nc.vector.tensor_scalar(bstack[0:RANK, :], amat, WS, None, ALU.mult))
                nc.vector.tensor_scalar(bstack[RANK:2 * RANK, :], amat, WS, None, ALU.mult)
                nc.vector.scalar_tensor_tensor(bstack[2 * RANK:3 * RANK, :], amat, WS, bstack[0:RANK, :],
                                               ALU.mult, ALU.subtract)

            def body(r, last):

                def split_rotated(s, f):
                    dve.wait_ge(r_hi_done, step_of(r, s) * NF + f + 1)
                    nc.vector.tensor_tensor(r_lo[f % 2][:, :], rotated[f % 2][:, :], r_hi[f % 2][:, :],
                                            ALU.subtract).then_inc(r_lo_done, 1)

                for s in range(B):
                    more = not (last and s == 1)
                    now = bass.ds(r * TG, TG)
                    tile = (s * NCH + r) * TT
                    for n in range(TT + NF):
                        f = n - TT
                        if f < 0:
                            dve.wait_ge(projected, PROJ0 + step_of(r, s) * (NF + TT) + n + 1)
                            bank = PROJ[(s * (NF + TT) + n) % 4]
                            if n == 0:
                                dve.wait_ge(v_stored[s], 16 * r + 16)
                            nc.vector.scalar_tensor_tensor(
                                vst[s][:, :, n * HD:(n + 1) * HD],
                                bank[:, 0:NV].rearrange("p (g d) -> p g d", d=HD), 1.0 / WS,
                                bv[:, 0:NV].rearrange("p (g d) -> p g d", d=HD), ALU.mult, ALU.add)
                            nc.vector.scalar_tensor_tensor(both[:, 0, bass.ds((tile + n) * E, E)], bank[:, NV:NV + E],
                                                           1.0 / WS, bv[:, NV:NV + E], ALU.mult, ALU.add)
                            nc.vector.tensor_scalar(natural_z[s][:, n, :], bank[:, NV + E:NVA], 1.0 / WS, None,
                                                    ALU.mult).then_inc(v_done, 1)
                            if more:
                                take_stats(*following(r, s), n)
                            continue
                        if f == 0 and more:
                            normalise(*following(r, s))
                        if more and TURN_AT <= n < TURN_AT + KC:
                            split_xt(*following(r, s), n - TURN_AT)
                        if n == DELTA_AT + 1:
                            dve.wait_ge(delta_full, step_of(r, s) + 1)
                            nc.vector.tensor_scalar(both[:, 1, bass.ds(tile * E, TT * E)], DELTAB[:, 0:TT * E], 1.0,
                                                    None, ALU.mult).then_inc(delta_out, 1)
                        k = step_of(r, s) * NF + f
                        dve.wait_ge(raw_done, RAW0 + k + 1)
                        dve.wait_ge(rotated_done, k + 1)
                        i = f % 2
                        nc.vector.tensor_tensor(by_cos[i][:, :], raw[i][:, :], table[:, 0, now], ALU.mult)
                        nc.vector.tensor_tensor(by_sin[i][64:P, :], raw[i][0:64, :], table[0:64, 1, now], ALU.mult)
                        nc.vector.tensor_tensor(by_sin[i][0:64, :], raw[i][64:P, :], table[64:P, 1, now],
                                                ALU.mult).then_inc(parts_done, 1)
                        if f:
                            split_rotated(s, f - 1)
                        if last and s == 1 and f == 3:
                            split_adapter()
                    split_rotated(s, NF - 1)

            for_all_steps(dve, body)

        @block.tensor
        def _(pe):

            def turn(r, s, k):
                n = step_of(r, s)
                if k == 0:
                    pe.wait_ge(xn_done, (n + 1) * TT)
                pe.wait_ge(xt_lo_done, n * KC + k + 1)
                for t in range(TT):
                    last = nc.tensor.transpose(TURN[k % 2][:, t * P:(t + 1) * P],
                                               xin[s][:, t, k * P:(k + 1) * P], ident32[:, :])
                last.then_inc(turned, 1)

            pe.sem_inc(projected, PROJ0)
            pe.wait_ge(c_ready, 8)
            for k in range(KC):
                turn(0, 0, k)
            pe.wait_ge(small_loaded, 64)

            def body(r, last):
                for s in range(B):
                    n = step_of(r, s)
                    pe.wait_ge(xt_lo_done, LO0 + (n + 1) * KC)
                    for i in range(TT + NF):
                        f = i - TT
                        if not (last and s == 1) and TURN_AT <= i < TURN_AT + KC:
                            turn(*following(r, s), i - TURN_AT)
                        if i == Z_AT:
                            pe.wait_ge(v_done, (n + 1) * TT)
                            pe.wait_ge(z_copied, n + 1)
                            for t in range(TT):
                                mm = nc.tensor.matmul(ZB[0:RANK, t * P:(t + 1) * P], natural_z[s][:, t, :],
                                                      ident32[:, :], start=(t == 0), stop=(t == TT - 1))
                            mm.then_inc(z_turned, 1)
                        if i == DELTA_AT:
                            pe.wait_ge(z_copied, n + 2)
                            pe.wait_ge(delta_out, n + 1)
                            for t in range(TT):
                                mm = nc.tensor.matmul(DELTAB[:, t * E:(t + 1) * E], z_step[s][:, t * P:(t + 1) * P],
                                                      lim_t[:, :], start=(t == 0), stop=(t == TT - 1))
                            mm.then_inc(delta_full, 1)
                        if s == 0 and not last:
                            pe.wait_ge(w_lo_done, NVP if f < 0 else NVP + f + 1)
                        if TT <= i < 2 * TT:
                            pe.wait_ge(v_done, n * TT + i - TT + 1)
                        else:
                            pe.wait_ge(raw_done, n * NF + i + 1 if i < TT else RAW0 + n * NF + i - 2 * TT + 1)
                        dst = PROJ[(s * (NF + TT) + i) % 4]
                        for k in range(KC):
                            if f >= 0:
                                cols = slice(NVA + f * P, NVA + (f + 1) * P)
                                pairs = ((w1_hi[:, k, cols], xt_hi[s][:, k, :]), (w1_hi[:, k, cols], xt_lo[s][:, k, :]),
                                         (w1_lo[:, k, cols], xt_hi[s][:, k, :]))
                                width = TG
                            else:
                                toks = slice(i * P, (i + 1) * P)
                                pairs = ((xt_hi[s][:, k, toks], w1_hi[:, k, 0:NVA]), (xt_hi[s][:, k, toks], w1_lo[:, k, 0:NVA]),
                                         (xt_lo[s][:, k, toks], w1_hi[:, k, 0:NVA]))
                                width = NVA
                            for m, (stay, move) in enumerate(pairs):
                                mm = nc.tensor.matmul(dst[:, 0:width], stay, move, start=(k == 0 and m == 0),
                                                      stop=(k == KC - 1 and m == 2))
                        mm.then_inc(projected, 1)

            for_all_steps(pe, body)


def route(nc, limes, stages, both, ident32, pair_odd, zstack, load_group, banks):
    NTOK = B * NT
    with ExitStack() as ctx:
        def sb(name, shape, dt):
            return ctx.enter_context(nc.sbuf_tensor(name, shape, dt))

        def sem(name):
            return ctx.enter_context(nc.semaphore(name))

        z_t = stages[0:RANK, :, :].rearrange("p a n -> p (a n)")
        lim = sb("lim", [E, RANK], F32)
        tops = sb("tops", [P, 2], F32)
        top_all = sb("top_all", [P, 2], F32)
        half_inv = sb("half_inv", [P, 2], F32)
        u = sb("u", [P, NTOK * E], F32)
        logits = sb("logits", [P, NTOK, E], F32)
        work = sb("work", [P, NTOK, E], F32)
        probs = sb("probs", [P, NTOK, E], F32)
        equal = sb("equal", [P, NTOK, E], F32)
        m1 = sb("m1", [P, NTOK], F32)
        m2 = sb("m2", [P, NTOK], F32)
        ties = sb("ties", [P, NTOK], F32)
        weights = sb("weights", [P, NTOK, E], F32)
        w_t = sb("w_t", [E, STEPS, TG], F32)
        zp = sb("zp", [RANK, STEPS, TG], F32)

        loaded = sem("loaded")
        paired = sem("paired")
        w_turned = sem("w_turned")
        mixes = sem("mixes")
        exps_done = sem("exps_done")
        w_copied = sem("w_copied")
        hi_copied = sem("hi_copied")
        reduced = sem("reduced")
        reduced_tops = sem("reduced_tops")
        all_reduced = sem("all_reduced")
        steps_done = sem("steps_done")
        weighted = sem("weighted")
        zp_done = sem("zp_done")

        block = ctx.enter_context(nc.Block())

        @block.sync
        def _(sp):
            sp.dma_start(lim[:, :], limes).then_inc(loaded, 16)
            load_group(sp, 0, 0)

        @block.tensor
        def _(pe):
            nc.tensor.matmul(banks[1][:, :], pair_odd[:, :], both[:, :, :].rearrange("p a n -> p (a n)"),
                             start=True, stop=True).then_inc(paired, 1)
            pe.wait_ge(loaded, 16)
            pe.wait_ge(weighted, 1)
            for i in range(STEPS):
                for t in range(TG // P):
                    last = nc.tensor.matmul(banks[i][0:E, t * P:(t + 1) * P], weights[:, i * 4 + t, :],
                                            ident32[:, :], start=(t == 0), stop=(t == 3))
                last.then_inc(w_turned, 1)
            for i in range(STEPS):
                pe.wait_ge(w_copied, i + 1)
                nc.tensor.matmul(banks[i][0:RANK, :], lim[:, :], w_t[:, i, :], start=True,
                                 stop=True).then_inc(mixes, 1)

        @block.scalar
        def _(act):
            act.wait_ge(reduced, 1)
            nc.scalar.activation(work[:, :, :], work[:, :, :], ACT.Exp).then_inc(exps_done, 1)
            act.wait_ge(reduced, 2)
            nc.scalar.activation(logits[:, :, :], equal[:, :, :], ACT.Exp, scale=-2.0).then_inc(exps_done, 1)
            for i in range(STEPS):
                act.wait_ge(w_turned, i + 1)
                nc.scalar.activation(w_t[:, i, :], banks[i][0:E, :], ACT.Copy).then_inc(w_copied, 1)
            for i in range(STEPS):
                act.wait_ge(zp_done, i + 1)
                toks = slice(i * TG, (i + 1) * TG)
                nc.scalar.activation(zstack[0:RANK, toks], zp[:, i, :], ACT.Copy).then_inc(hi_copied, 1)
                nc.scalar.activation(zstack[2 * RANK:3 * RANK, toks], zp[:, i, :], ACT.Copy)

        @block.gpsimd
        def _(pool):
            pool.wait_ge(reduced_tops, 1)
            nc.gpsimd.partition_all_reduce(top_all[:, :], tops[:, :], P, RMAX).then_inc(all_reduced, 1)

        @block.vector
        def _(dve):
            count = [0]

            def step(ins):
                count[0] += 1
                ins.then_inc(steps_done, 1)
                dve.wait_ge(steps_done, count[0])

            def wide(t):
                return t[:, :].unsqueeze(2).to_broadcast([P, NTOK, E])

            dve.wait_ge(paired, 1)
            nc.vector.tensor_reduce(tops[:, :], banks[1][:, :].rearrange("p (a n) -> p a n", a=2), AX.X, ALU.max,
                                    apply_absolute_value=True).then_inc(reduced_tops, 1)
            dve.wait_ge(all_reduced, 1)
            step(nc.vector.tensor_scalar(top_all[:, :], top_all[:, :], SCALE_EPS, None, ALU.max))
            step(nc.vector.reciprocal(half_inv[:, :], top_all[:, :]))
            step(nc.vector.tensor_scalar(half_inv[:, :], half_inv[:, :], 0.5, None, ALU.mult))
            step(nc.vector.tensor_scalar(u[:, :], banks[1][:, 0:NTOK * E], half_inv[:, 0:1], None, ALU.mult))
            step(nc.vector.scalar_tensor_tensor(logits[:, :, :].rearrange("p t e -> p (t e)"),
                                                banks[1][:, NTOK * E:2 * NTOK * E], half_inv[:, 1:2], u[:, :],
                                                ALU.mult, ALU.add))
            step(nc.vector.tensor_reduce(m1[:, :], logits[:, :, :], AX.X, ALU.max))
            nc.vector.tensor_tensor(work[:, :, :], logits[:, :, :], wide(m1), ALU.subtract).then_inc(reduced, 1)
            dve.wait_ge(exps_done, 1)
            step(nc.vector.tensor_reduce(m2[:, :], work[:, :, :], AX.X, ALU.add))
            step(nc.vector.reciprocal(m2[:, :], m2[:, :]))
            step(nc.vector.tensor_tensor(probs[:, :, :], work[:, :, :], wide(m2), ALU.mult))
            step(nc.vector.tensor_reduce(m1[:, :], probs[:, :, :], AX.X, ALU.max))
            step(nc.vector.tensor_tensor(equal[:, :, :], probs[:, :, :], wide(m1), ALU.is_equal))
            step(nc.vector.tensor_reduce(ties[:, :], equal[:, :, :], AX.X, ALU.add))
            step(nc.vector.scalar_tensor_tensor(work[:, :, :].rearrange("p t e -> p (t e)"),
                                                equal[:, :, :].rearrange("p t e -> p (t e)"), -2.0,
                                                probs[:, :, :].rearrange("p t e -> p (t e)"), ALU.mult, ALU.add))
            step(nc.vector.tensor_reduce(m2[:, :], work[:, :, :], AX.X, ALU.max))
            step(nc.vector.tensor_scalar(ties[:, :], ties[:, :], 2.0, None, ALU.is_ge))
            step(nc.vector.tensor_tensor(ties[:, :], ties[:, :], m1[:, :], ALU.mult))
            step(nc.vector.tensor_tensor(m2[:, :], m2[:, :], ties[:, :], ALU.max))
            nc.vector.tensor_tensor(equal[:, :, :], probs[:, :, :], wide(m2), ALU.subtract).then_inc(reduced, 1)
            dve.wait_ge(exps_done, 2)
            step(nc.vector.tensor_scalar(logits[:, :, :], logits[:, :, :], 1.0, None, ALU.add))
            step(nc.vector.reciprocal(logits[:, :, :], logits[:, :, :]))
            step(nc.vector.tensor_tensor(work[:, :, :], probs[:, :, :], logits[:, :, :], ALU.mult))
            step(nc.vector.tensor_reduce(m1[:, :], work[:, :, :], AX.X, ALU.add))
            step(nc.vector.tensor_scalar(m1[:, :], m1[:, :], 1e-9, None, ALU.add))
            step(nc.vector.reciprocal(m1[:, :], m1[:, :]))
            nc.vector.tensor_tensor(weights[:, :, :], work[:, :, :], wide(m1), ALU.mult).then_inc(weighted, 1)

            def low_part(i):
                toks = slice(i * TG, (i + 1) * TG)
                dve.wait_ge(hi_copied, i + 1)
                nc.vector.tensor_tensor(zstack[RANK:2 * RANK, toks], zp[:, i, :], zstack[0:RANK, toks], ALU.subtract)

            for i in range(STEPS):
                dve.wait_ge(mixes, i + 1)
                nc.vector.scalar_tensor_tensor(zp[:, i, :], banks[i][0:RANK, :], ALPHA_OVER_RANK,
                                               z_t[:, i * TG:(i + 1) * TG], ALU.mult, ALU.mult).then_inc(zp_done, 1)
                if i:
                    low_part(i - 1)
            low_part(STEPS - 1)


def attend(nc, ctx_parts, w_out, w_hi, w_lo, q_stack, k_stack, v_slot, qk_loaded, load_group,
           ident16, ident_bf, mask_q, mask_k, mask_early, mask_late, banks):
    order, lead = attention_order()
    UNITS = len([1 for o in order if o[0] == "values"])
    BANKS = len([1 for o in order if o[0] in ("bank", "row")])
    LEAD_BANKS = len([1 for k, _ in lead if k in ("bank", "row")])
    LEAD_ROWS = len([1 for k, _ in lead if k == "row"])
    LEAD_FOLDS = len([1 for k, _ in lead if k == "fold"])
    SUMS = [o for o in order if o[0] == "sums"]
    ADDED = [o for o in SUMS if o[4][1] is not None]
    ADDS = [(g, j) for g, o in enumerate(ADDED) for j in range(len(o[4][2]))]
    STEPS2 = GROUPS // 2
    with ExitStack() as ctx:
        def sb(name, shape, dt):
            return ctx.enter_context(nc.sbuf_tensor(name, shape, dt))

        def sem(name):
            return ctx.enter_context(nc.semaphore(name))

        ones = sb("ones", [P, HD], F32)
        partial = [sb(f"partial{i}", [P, NCH, 3, QH * (TG // P)], F32) for i in range(2)]
        top = [sb(f"top{i}", [P, NCH, QH * (TG // P)], F32) for i in range(2)]
        shift = [sb(f"shift{i}", [P, NCH, QH * (TG // P)], F16) for i in range(2)]
        shift_row = [sb(f"shift_row{i}", [QH * (TG // P), P], F16) for i in range(2)]
        probs = [sb(f"probs{i}", [P, QH, TG], F32) for i in range(PROBRING)]
        added = [sb(f"added{i}", [P, QH, TG], F32) for i in range(ADDRING)]
        total = [sb(f"total{i}", [P, TG], F32) for i in range(2)]
        context = [sb(f"context{i}", [P, TG], F32) for i in range(2)]
        turned_total = sb("turned_total", [P, TG], F32)
        compact = sb("compact", [P, TG // HD], F32)
        scaled = sb("scaled", [P, TG], F32)
        c_hi = [sb(f"c_hi{i}", [P, TG], F16) for i in range(2)]
        c_lo = [sb(f"c_lo{i}", [P, TG], F16) for i in range(2)]
        wst = sb("wst", [P, D], F32)

        MAXB, SCOREB, CTXB, SUMB = banks[0:MAXRING], banks[MAXRING:MAXRING + SCORERING], banks[6], banks[7]

        set_up = sem("set_up")
        max_full = sem("max_full")
        max_read = sem("max_read")
        folded = sem("folded")
        shift_done = sem("shift_done")
        row_placed = [sem(f"row_placed{i}") for i in range(2)]
        score_full = sem("score_full")
        prob_done = sem("prob_done")
        values_done = sem("values_done")
        units_added = sem("units_added")
        summed = sem("summed")
        total_out = sem("total_out")
        context_out = sem("context_out")
        inverted = sem("inverted")
        scaled_done = sem("scaled_done")
        c_lo_done = sem("c_lo_done")
        c_stored = [sem(f"c_stored{i}") for i in range(2)]
        wst_loaded = sem("wst_loaded")
        wst_hi = sem("wst_hi")
        wst_lo = sem("wst_lo")

        TILES = TG // P
        INVERSIONS = 3

        MAX0 = MAXRING
        PROB0 = SCORERING
        VAL0 = PROBRING
        CTX0 = 2
        PLACED = 16 * QH
        ROW0 = PLACED
        ONE0 = 1

        LOADS = 10 * 16

        def unit_end(s, c):
            return sum(len(key_units(i)) for i in range(NCH)) * s + sum(len(key_units(i)) for i in range(c + 1))

        def prob_slot(unit):
            return unit % PROBRING

        def first_unit(s, c):
            return unit_end(s, c) - len(key_units(c))

        def sums_before(s, c):
            return len([1 for o in SUMS if (o[1], o[2]) < (s, c)])

        def freed_by(unit):
            adds = sums = 0
            before = unit - PROBRING
            a = 0
            for n, (_, s, c, _, (members, _, steps, direct), _) in enumerate(SUMS):
                at = first_unit(s, c)
                for j, (m, _, _) in enumerate(steps):
                    a += 1
                    if before >= 0 and before in [at + x for x in (members[:2] if j == 0 else (m,))]:
                        adds = a
                if before >= 0 and before in [at + m for m, _, _ in direct]:
                    sums = n + 1
            return adds, sums

        block = ctx.enter_context(nc.Block())

        @block.sync
        def _(sp):
            w_v = w_out.rearrange("(m p) d -> m p d", p=P)

            def load_weights(r, i):
                sp.wait_ge(wst_lo, ONE0 + 2 * r + i)
                sp.dma_start(wst[:, :], w_v[r * 2 + i]).then_inc(wst_loaded, 16)

            def store(r, s, c):
                k = (s * NCH + c) % 2
                sp.wait_ge(c_lo_done, CTX0 + r * 2 * NCH + s * NCH + c + 1)
                for part, half in enumerate((c_hi, c_lo)):
                    sp.dma_start(ctx_parts[part, r * 2 + s, c], half[k][:, :]).then_inc(c_stored[k], 16)

            def place_row(r, k, n, c, slot):
                sp.wait_ge(max_read, MAX0 + r * BANKS + k + 1)
                for h in range(QH):
                    sp.dma_start(q_stack[slot][STACK:STACK + 1, h, c * TG:(c + 1) * TG],
                                 shift_row[n % 2][h * TILES:(h + 1) * TILES, :]).then_inc(row_placed[n % 2], 16)

            k = n = 0
            for kind, m in lead:
                if kind == "row":
                    place_row(0, k, n, m, 0)
                    n += 1
                k += kind != "fold"
            with sp.Fori(0, STEPS2) as r:
                sp.wait_ge(values_done, VAL0 + r * UNITS)
                load_group(sp, 1, r)
                load_weights(r, 0)
                k, n = LEAD_BANKS, LEAD_ROWS
                for o in order:
                    if o[0] == "row":
                        place_row(r, k, n, o[2], o[1] % 2)
                        n += 1
                    if o[0] in ("bank", "row"):
                        k += 1
                    if o[0] == "split":
                        _, s, c = o
                        if s * NCH + c:
                            store(r, (s * NCH + c - 1) // NCH, (s * NCH + c - 1) % NCH)
                    if o[0] == "context":
                        _, s, c = o
                        if (s, c) == (0, 2):
                            load_weights(r, 1)
                        if (s, c) == (0, NCH - 1):
                            sp.wait_ge(values_done, VAL0 + r * UNITS + UNITS // 2)
                            load_group(sp, 0, r + 1)
                store(r, 1, NCH - 1)
            sp.wait_ge(qk_loaded[0], LOADS * (STEPS2 + 1))
            for i in range(2):
                sp.wait_ge(row_placed[i], ROW0 + PLACED * (GROUPS * NCH // 2 + (LEAD_ROWS + 1 - i) // 2))
            for i in range(2):
                sp.wait_ge(c_stored[i], 32 + 32 * GROUPS * NCH // 2)

        @block.gpsimd
        def _(pool):
            for i in range(2):
                nc.gpsimd.memset(k_stack[i][STACK:STACK + 1, :], SHIFT).then_inc(set_up, 1)
            pool.sem_inc(units_added, ONE0)
            pool.sem_inc(c_lo_done, CTX0)
            pool.sem_inc(c_stored[0], 32)
            pool.sem_inc(c_stored[1], 32)

            def split(r, s, c):
                k = (s * NCH + c) % 2
                n = r * 2 * NCH + s * NCH + c + 1
                pool.wait_ge(context_out, CTX0 + n)
                pool.wait_ge(c_stored[k], 32 + r * 32 * NCH + 32 * ((s * NCH + c) // 2))
                pool.wait_ge(c_lo_done, CTX0 + n - 1)
                pool.wait_ge(inverted, r * 2 * NCH * INVERSIONS + (s * NCH + c + 1) * INVERSIONS)
                nc.gpsimd.tensor_tensor(c_hi[k][:, :], context[k][:, :], total[k][:, :], ALU.mult)
                nc.gpsimd.tensor_tensor(scaled[:, :], context[k][:, :], total[k][:, :], ALU.mult).then_inc(scaled_done, 1)
                pool.wait_ge(scaled_done, n)
                nc.gpsimd.tensor_tensor(c_lo[k][:, :], scaled[:, :], c_hi[k][:, :],
                                        ALU.subtract).then_inc(c_lo_done, 1)

            def add(r, a):
                g, j = ADDS[a]
                _, s, c, _, (members, span, steps, _), _ = ADDED[g]
                m, start, width = steps[j]

                def of(member):
                    at = (key_units(c)[member][1] - c * (TG // BLK)) * BLK
                    return probs[prob_slot(first_unit(s, c) + member)][:, :, start - at:start - at + width]

                pool.wait_ge(prob_done, PROB0 + r * QH * UNITS + (first_unit(s, c) + m + 1) * QH)
                dst = added[g % ADDRING][:, :, start - span[0]:start - span[0] + width]
                if j == 0:
                    pool.wait_ge(summed, ONE0 + r * len(SUMS) + (SUMS.index(ADDED[g - ADDRING]) + 1 if g >= ADDRING else 0))
                    nc.gpsimd.tensor_tensor(dst, of(members[0]), of(m), ALU.add).then_inc(units_added, 1)
                else:
                    pool.wait_ge(units_added, ONE0 + r * len(ADDS) + a)
                    nc.gpsimd.tensor_tensor(dst, dst, of(m), ALU.add).then_inc(units_added, 1)

            with pool.Fori(0, STEPS2) as r:
                a = unit = 0
                for o in order:
                    if o[0] == "scores" and o[5] == QH - 1:
                        unit += 1
                        if a < len(ADDS):
                            g, j = ADDS[a]
                            _, s, c, _, (_, _, steps, _), _ = ADDED[g]
                            if first_unit(s, c) + steps[j][0] + 1 == unit:
                                add(r, a)
                                a += 1
                    elif o[0] == "split":
                        split(r, o[1], o[2])

        @block.scalar
        def _(act):
            act.sem_inc(prob_done, PROB0)
            act.sem_inc(context_out, CTX0)
            act.sem_inc(total_out, ONE0)
            with act.Fori(0, STEPS2) as r:
                k = 0
                unit = -1
                for o in order:
                    if o[0] == "scores":
                        _, s, c, i, (j, lo, n, diagonal, far), h = o
                        if h == 0:
                            unit += 1
                            act.wait_ge(values_done, r * UNITS + max(unit + 1, VAL0))
                            adds, sums = freed_by(unit)
                            if adds or unit < PROBRING:
                                act.wait_ge(units_added, ONE0 + r * len(ADDS) + adds)
                            if sums or unit < PROBRING:
                                act.wait_ge(summed, ONE0 + r * len(SUMS) + sums)
                        act.wait_ge(score_full, r * QH * UNITS + k + 1)
                        nc.scalar.activation(probs[prob_slot(unit)][:, h, 0:BLK * n], SCOREB[k % SCORERING][:, 0:BLK * n],
                                             ACT.Exp, scale=SM_SCALE).then_inc(prob_done, 1)
                        k += 1
                    elif o[0] == "context":
                        _, s, c = o
                        q = s * NCH + c
                        act.wait_ge(values_done, VAL0 + r * UNITS + unit_end(s, c))
                        act.wait_ge(c_lo_done, r * 2 * NCH + q + 1)
                        nc.scalar.activation(context[q % 2][:, :], CTXB[:, :], ACT.Copy).then_inc(context_out, 1)
                        if q in (1, 5):
                            i = q // 4
                            act.wait_ge(wst_loaded, 32 * r + 16 * i + 16)
                            nc.scalar.activation(w_hi[:, r * 2 + i, :], wst[:, :], ACT.Copy,
                                                 scale=WS).then_inc(wst_hi, 1)
                    elif o[0] == "totals":
                        _, s, c = o
                        q = s * NCH + c
                        act.wait_ge(summed, ONE0 + r * len(SUMS) + sums_before(s, c) + len(sum_groups(c)))
                        act.wait_ge(c_lo_done, r * 2 * NCH + q + 1)
                        nc.scalar.activation(total[q % 2][:, :], SUMB[:, :], ACT.Copy,
                                             scale=1.0 / CS).then_inc(total_out, 1)

        @block.vector
        def _(dve):
            for i in range(2):
                nc.vector.memset(partial[i][:, :, :, :], LOWEST).then_inc(set_up, 1)
            nc.vector.memset(ones[:, :], 1.0).then_inc(set_up, 1)
            dve.sem_inc(max_read, MAX0)
            dve.sem_inc(wst_lo, ONE0)
            dve.wait_ge(set_up, 5)

            def take(r, k, bank, slot):
                t, c = bank["t"], bank["t"] // TILES
                heads = bank["heads"]
                w = sum(x for _, x in bank["pieces"])
                dve.wait_ge(max_full, r * BANKS + k + 1)
                dst = partial[slot][:, c, bank["seg"], heads[0] * TILES + t % TILES:heads[-1] * TILES + t % TILES + 1:TILES]
                src = MAXB[k % MAXRING][:, 0:len(heads) * w].rearrange("p (h w) -> p h w", w=w)
                nc.vector.tensor_reduce(dst, src, AX.X, ALU.max).then_inc(max_read, 1)

            def fold(r, k, c, slot, n):
                dve.wait_ge(max_read, MAX0 + r * BANKS + k)
                nc.vector.tensor_reduce(top[slot][:, c, :], partial[slot][:, c, :, :].rearrange("p s n -> p n s"),
                                        AX.X, ALU.max).then_inc(folded, 1)
                dve.wait_ge(folded, r * 2 * NCH + n + 1)
                nc.vector.tensor_scalar(shift[slot][:, c, :], top[slot][:, c, :], -1.0 / SHIFT, None,
                                        ALU.mult).then_inc(shift_done, 1)

            def row(r, k, n):
                dve.wait_ge(max_full, r * BANKS + k + 1)
                dve.wait_ge(row_placed[n % 2], PLACED * (NCH * r + n // 2) + ROW0)
                nc.vector.tensor_copy(shift_row[n % 2][:, :], MAXB[k % MAXRING][0:QH * TILES, 0:P]).then_inc(max_read, 1)

            dve.sem_inc(row_placed[0], ROW0)
            dve.sem_inc(row_placed[1], ROW0)

            k = n = f = 0
            for kind, m in lead:
                if kind == "bank":
                    take(0, k, m, 0)
                    k += 1
                elif kind == "fold":
                    fold(0, k, m, 0, f)
                    f += 1
                else:
                    row(0, k, n)
                    n += 1
                    k += 1
            with dve.Fori(0, STEPS2) as r:
                k, n, f = LEAD_BANKS, LEAD_ROWS, LEAD_FOLDS
                for o in order:
                    if o[0] == "bank":
                        take(r, k, o[2], o[1] % 2)
                        k += 1
                    elif o[0] == "fold":
                        fold(r, k, o[2], o[1] % 2, f)
                        f += 1
                    elif o[0] == "row":
                        row(r, k, n)
                        n += 1
                        k += 1
                    elif o[0] == "invert":
                        _, s, c, piece = o
                        q = s * NCH + c
                        done = r * 2 * NCH * INVERSIONS + q * INVERSIONS
                        if piece == 0:
                            dve.wait_ge(total_out, ONE0 + r * 2 * NCH + q + 1)
                            nc.vector.transpose(turned_total[:, :], total[q % 2][:, :]).then_inc(inverted, 1)
                        else:
                            dve.wait_ge(inverted, done + 1)
                            nc.vector.reciprocal(compact[:, :], turned_total[:, 0:TG:HD]).then_inc(inverted, 1)
                            dve.wait_ge(inverted, done + 2)
                            nc.vector.transpose(total[q % 2][:, :],
                                                compact[:, :].unsqueeze(2).to_broadcast([P, TG // HD, HD])
                                                ).then_inc(inverted, 1)
                        if piece == 0 and q in (1, 5):
                            i = q // 4
                            dve.wait_ge(wst_hi, 2 * r + i + 1)
                            nc.vector.scalar_tensor_tensor(w_lo[:, r * 2 + i, :], wst[:, :], WS, w_hi[:, r * 2 + i, :],
                                                           ALU.mult, ALU.subtract).then_inc(wst_lo, 1)

        @block.tensor
        def _(pe):
            pe.sem_inc(values_done, VAL0)
            pe.sem_inc(summed, ONE0)
            pe.wait_ge(set_up, 5)

            def wait_max_bank(r, k):
                if isinstance(r, int):
                    if k >= MAXRING:
                        pe.wait_ge(max_read, k + 1)
                else:
                    pe.wait_ge(max_read, r * BANKS + (max(k + 1, LEAD_BANKS + MAX0) if BANKS % MAXRING else k + 1))

            def max_bank(r, k, bank, slot):
                dst = MAXB[k % MAXRING]
                wait_max_bank(r, k)
                t = bank["t"]
                w = sum(x for _, x in bank["pieces"])
                first = True
                mms = []
                for i, h in enumerate(bank["heads"]):
                    at = i * w
                    for start, width in bank["pieces"]:
                        mms.append((dst[:, at:at + width], q_stack[slot][0:STACK, h, t * P:(t + 1) * P],
                                    k_stack[slot][0:STACK, start:start + width]))
                        at += width
                whole = dst[:, 0:len(bank["heads"]) * w].rearrange("p (h w) -> p h w", w=w)
                if bank["mask"] == "diagonal":
                    mms.append((whole[:, :, w - P:w], ident_bf[:, :],
                                mask_q[:, :].unsqueeze(1).to_broadcast([P, len(bank["heads"]), P])))
                elif bank["mask"] == "late queries":
                    mms.append((whole[:, :, 0:BLK], ident_bf[:, :],
                                mask_late[:, :].unsqueeze(1).to_broadcast([P, QH, BLK])))
                for m, (o, a, b) in enumerate(mms):
                    last = nc.tensor.matmul(o, a, b, start=(m == 0), stop=(m == len(mms) - 1), skip_group_check=True)
                last.then_inc(max_full, 1)

            def max_row(r, k, n, c, slot):
                wait_max_bank(r, k)
                pe.wait_ge(shift_done, r * 2 * NCH + n + 1)
                nc.tensor.matmul(MAXB[k % MAXRING][0:QH * TILES, 0:P], shift[slot][:, c, :], ident16[:, :], start=True,
                                 stop=True).then_inc(max_full, 1)

            def scores(r, k, s, u, h):
                j, lo, n, diagonal, far = u
                dst = SCOREB[k % SCORERING]
                pe.wait_ge(prob_done, r * QH * UNITS + max(k + 1, PROB0))
                mms = [(dst[:, 0:BLK * n], k_stack[s][:, j * P:(j + 1) * P], q_stack[s][:, h, lo * BLK:(lo + n) * BLK])]
                if diagonal:
                    mms.append((dst[:, 0:P], ident_bf[:, :], mask_k[:, :]))
                if far:
                    mms.append((dst[:, BLK * (n - far):BLK * n].rearrange("p (a w) -> p a w", w=BLK), ident_bf[:, :],
                                mask_early[:, :].unsqueeze(1).to_broadcast([P, far, BLK])))
                for m, (o, a, b) in enumerate(mms):
                    last = nc.tensor.matmul(o, a, b, start=(m == 0), stop=(m == len(mms) - 1), skip_group_check=True)
                last.then_inc(score_full, 1)

            def products(r, unit, s, c, i, u, last_of_chunk):
                j, lo, n, diagonal, far = u
                at = (lo - c * (TG // BLK)) * BLK
                pe.wait_ge(prob_done, PROB0 + r * QH * UNITS + (unit + 1) * QH)
                if i == 0:
                    pe.wait_ge(context_out, CTX0 + r * 2 * NCH + s * NCH + c)
                for h in range(QH):
                    last = nc.tensor.matmul(CTXB[h * HD:(h + 1) * HD, at:at + BLK * n], v_slot[s][:, j, :],
                                            probs[prob_slot(unit)][:, h, 0:BLK * n], start=(i == 0),
                                            stop=last_of_chunk, skip_group_check=True, tile_position=(0, h * HD))
                last.then_inc(values_done, 1)

            def sums(r, a, s, c, n, group, last_of_chunk):
                members, span, steps, direct = group
                if n == 0:
                    pe.wait_ge(total_out, ONE0 + r * 2 * NCH + s * NCH + c)
                if direct:
                    pe.wait_ge(prob_done, PROB0 + r * QH * UNITS + (first_unit(s, c) + members[-1] + 1) * QH)
                if steps:
                    last_add = max(i for i, (g, _) in enumerate(ADDS) if g == a)
                    pe.wait_ge(units_added, ONE0 + r * len(ADDS) + last_add + 1)
                pieces = [(added[a % ADDRING], 0, *span)] if steps else []
                for m, start, width in direct:
                    at = (key_units(c)[m][1] - c * (TG // BLK)) * BLK
                    pieces.append((probs[prob_slot(first_unit(s, c) + m)], start - at, start, width))
                for x, (src, at, start, width) in enumerate(pieces):
                    for h in range(QH):
                        last = nc.tensor.matmul(SUMB[h * HD:(h + 1) * HD, start:start + width], ones[:, :],
                                                src[:, h, at:at + width], start=(n == 0 and x == 0),
                                                stop=last_of_chunk and x == len(pieces) - 1,
                                                skip_group_check=True, tile_position=(0, h * HD))
                last.then_inc(summed, 1)

            pe.wait_ge(qk_loaded[0], LOADS)
            k = n = 0
            for kind, m in lead:
                if kind == "bank":
                    max_bank(0, k, m, 0)
                    k += 1
                elif kind == "row":
                    max_row(0, k, n, m, 0)
                    k += 1
                    n += 1
            with pe.Fori(0, STEPS2) as r:
                k, n = LEAD_BANKS, LEAD_ROWS
                kk = 0
                unit = a = 0
                seen = set()
                for o in order:
                    if o[0] == "bank":
                        if o[1] > 0 and o[1] not in seen:
                            seen.add(o[1])
                            pe.wait_ge(qk_loaded[o[1] % 2], LOADS * r + (LOADS if o[1] == 1 else 2 * LOADS))
                        max_bank(r, k, o[2], o[1] % 2)
                        k += 1
                    elif o[0] == "row":
                        max_row(r, k, n, o[2], o[1] % 2)
                        k += 1
                        n += 1
                    elif o[0] == "scores":
                        _, s, c, i, u, h = o
                        if i == 0 and h == 0:
                            q = s * NCH + c
                            pe.wait_ge(row_placed[q % 2], ROW0 + PLACED * (NCH * r + q // 2 + 1))
                        scores(r, kk, s, u, h)
                        kk += 1
                    elif o[0] == "values":
                        _, s, c, i, u, last = o
                        products(r, unit, s, c, i, u, last)
                        unit += 1
                    elif o[0] == "sums":
                        _, s, c, i, group, last = o
                        sums(r, a, s, c, i, group, last)
                        a += group[1] is not None


def finish(nc, x, xt_parts, ctx_parts, w_hi, w_lo, zstack, bstack, b_out, out, banks):
    TT, NH = TG // P, D // PSUM_BANK
    PAIRS = TT * NH
    with ExitStack() as ctx:
        def sb(name, shape, dt):
            return ctx.enter_context(nc.sbuf_tensor(name, shape, dt))

        def sem(name):
            return ctx.enter_context(nc.semaphore(name))

        xt = [[sb(f"xt{s}_{part}", [P, KC, TG], F16) for part in range(2)] for s in range(2)]
        ct = [[sb(f"ct{s}_{part}", [P, N_KV, TG], F16) for part in range(2)] for s in range(2)]
        xres = [sb(f"xres{s}", [P, TT, D], F32) for s in range(2)]
        bias = sb("bias", [P, D], F32)
        gate = [sb(f"gate{i}", [P, PSUM_BANK], F32) for i in range(2)]
        dense = [sb(f"dense{i}", [P, PSUM_BANK], F32) for i in range(2)]
        gated = [sb(f"gated{i}", [P, PSUM_BANK], F32) for i in range(2)]
        result = [sb(f"result{i}", [P, PSUM_BANK], F32) for i in range(2)]

        GATEB, DENSEB = banks[0:4], banks[4:8]

        bias_loaded = sem("bias_loaded")
        xt_loaded = [sem(f"xt_loaded{s}") for s in range(2)]
        ct_loaded = [sem(f"ct_loaded{s}") for s in range(2)]
        xres_loaded = [sem(f"xres_loaded{s}") for s in range(2)]
        gate_full = sem("gate_full")
        dense_full = sem("dense_full")
        gate_done = sem("gate_done")
        dense_done = sem("dense_done")
        gated_done = sem("gated_done")
        result_done = sem("result_done")
        stored = [sem(f"stored{i}") for i in range(2)]

        RING4, RING2 = 4, 2
        FULL0 = RESULTS0 = 2 * PAIRS
        LOADS = 2 * 16

        block = ctx.enter_context(nc.Block())

        @block.sync
        def _(sp):
            x_v = x.rearrange("(i t p) d -> i p t d", t=TT, p=P)
            sp.dma_start(bias[:, :], b_out.partition_broadcast(P)).then_inc(bias_loaded, 16)
            with sp.Fori(0, NCH) as r:
                for s in range(B):
                    sp.wait_ge(dense_full, r * 2 * PAIRS + (s + 1) * PAIRS)
                    sp.wait_ge(result_done, r * 2 * PAIRS + (s + 1) * PAIRS)
                    for part in range(2):
                        sp.dma_start(xt[s][part][:, :, :].rearrange("p k t -> p (k t)"),
                                     xt_parts[part, s * NCH + r]).then_inc(xt_loaded[s], 16)
                    for part in range(2):
                        sp.dma_start(ct[s][part][:, :, :],
                                     ctx_parts[part, s:GROUPS:2, r].rearrange("g p t -> p g t")).then_inc(ct_loaded[s], 16)
                    sp.dma_start(xres[s][:, :, :], x_v[s * NCH + r]).then_inc(xres_loaded[s], 16)

        @block.gpsimd
        def _(pool):
            pool.sem_inc(result_done, RESULTS0)
            with pool.Fori(0, STEPS // 2) as r:
                for n in range(2 * PAIRS):
                    s, t, half = n // PAIRS, n % PAIRS // NH, n % NH
                    if n % PAIRS == 0:
                        pool.wait_ge(xres_loaded[s], 16 * r + 16)
                    pool.wait_ge(stored[n % 2], 16 + r * 16 * PAIRS + 16 * (n // 2))
                    pool.wait_ge(gated_done, RING2 + r * 2 * PAIRS + n + 1)
                    nc.gpsimd.tensor_tensor(result[n % 2][:, :], gated[n % 2][:, :],
                                            xres[s][:, t, half * PSUM_BANK:(half + 1) * PSUM_BANK],
                                            ALU.add).then_inc(result_done, 1)

        @block.scalar
        def _(act):
            act.sem_inc(gate_done, RING4)
            act.sem_inc(stored[0], 16)
            act.sem_inc(stored[1], 16)
            o_v = out.rearrange("(i t p) d -> i t p d", t=TT, p=P)
            with act.Fori(0, STEPS // 2) as r:

                def store(n):
                    act.wait_ge(result_done, RESULTS0 + r * 2 * PAIRS + n + 1)
                    s, t, half = n // PAIRS, n % PAIRS // NH, n % NH
                    act.dma_start(o_v[s * NCH + r, t][:, half * PSUM_BANK:(half + 1) * PSUM_BANK],
                                  result[n % 2][:, :]).then_inc(stored[n % 2], 16)

                for n in range(2 * PAIRS):
                    act.wait_ge(gate_full, r * 2 * PAIRS + n + 1)
                    act.wait_ge(gated_done, r * 2 * PAIRS + n + 1)
                    nc.scalar.activation(gate[n % 2][:, :], GATEB[n % 4][:, :], ACT.Silu,
                                         scale=1.0 / WS).then_inc(gate_done, 1)
                    if n:
                        store(n - 1)
                store(2 * PAIRS - 1)
            for i in range(2):
                act.wait_ge(stored[i], 16 + 16 * STEPS * PAIRS // 2)

        @block.vector
        def _(dve):
            dve.sem_inc(dense_done, RING4)
            dve.sem_inc(gated_done, RING2)
            dve.wait_ge(bias_loaded, 16)
            with dve.Fori(0, STEPS // 2) as r:
                for n in range(2 * PAIRS):
                    half = n % NH
                    dve.wait_ge(dense_full, FULL0 + r * 2 * PAIRS + n + 1)
                    nc.vector.scalar_tensor_tensor(dense[n % 2][:, :], DENSEB[n % 4][:, :], 1.0 / (WS * CS),
                                                   bias[:, half * PSUM_BANK:(half + 1) * PSUM_BANK],
                                                   ALU.mult, ALU.add).then_inc(dense_done, 1)
                    dve.wait_ge(dense_done, RING4 + r * 2 * PAIRS + n + 1)
                    dve.wait_ge(gate_done, RING4 + r * 2 * PAIRS + n + 1)
                    dve.wait_ge(result_done, RESULTS0 - RING2 + r * 2 * PAIRS + n + 1)
                    nc.vector.tensor_tensor(gated[n % 2][:, :], dense[n % 2][:, :], gate[n % 2][:, :],
                                            ALU.mult).then_inc(gated_done, 1)

        @block.tensor
        def _(pe):
            pe.sem_inc(dense_full, FULL0)
            with pe.Fori(0, STEPS // 2) as r:

                def gates(n):
                    s, t, half = n // PAIRS, n % PAIRS // NH, n % NH
                    if n % PAIRS == 0:
                        pe.wait_ge(xt_loaded[s], LOADS * r + LOADS)
                    toks, cols = slice(t * P, (t + 1) * P), slice(half * PSUM_BANK, (half + 1) * PSUM_BANK)
                    pe.wait_ge(gate_done, r * 2 * PAIRS + n + 1)
                    for k in range(KC):
                        for m, (part, w) in enumerate(((0, w_hi), (0, w_lo), (1, w_hi))):
                            nc.tensor.matmul(GATEB[n % 4][:, :], xt[s][part][:, k, toks], w[:, KC + k, cols],
                                             start=(k == 0 and m == 0), stop=False)
                    nc.tensor.matmul(GATEB[n % 4][:, :], zstack[0:ZROWS, bass.ds(r * TG + s * S + t * P, P)],
                                     bstack[0:ZROWS, cols], start=False, stop=True).then_inc(gate_full, 1)

                def outputs(n):
                    s, t, half = n // PAIRS, n % PAIRS // NH, n % NH
                    if n % PAIRS == 0:
                        pe.wait_ge(ct_loaded[s], LOADS * r + LOADS)
                    toks, cols = slice(t * P, (t + 1) * P), slice(half * PSUM_BANK, (half + 1) * PSUM_BANK)
                    pe.wait_ge(dense_done, r * 2 * PAIRS + n + 1)
                    for k in range(KC):
                        for m, (part, w) in enumerate(((0, w_hi), (0, w_lo), (1, w_hi))):
                            last = nc.tensor.matmul(DENSEB[n % 4][:, :], ct[s][part][:, k, toks], w[:, k, cols],
                                                    start=(k == 0 and m == 0), stop=(k == KC - 1 and m == 2))
                    last.then_inc(dense_full, 1)

                gates(0)
                for n in range(2 * PAIRS):
                    if n + 1 < 2 * PAIRS:
                        gates(n + 1)
                    outputs(n)



def kernel(L0_attn_hidden_states, L0_attn_w_qkv, L0_attn_b_qkv, L0_attn_w_dense, L0_attn_b_dense,
           L0_ffn_W, L0_ffn_b, L0_ffn_A, L0_ffn_Bmat, L0_ffn_LiMEs):
    import numpy as np
    import concourse.bacc as bacc
    from concourse.bass_utils import run_bass_kernel_spmd

    w = np.asarray(L0_attn_w_qkv).reshape(N_KV, QH + 2, 2, HALF, D)
    bias = np.asarray(L0_attn_b_qkv).reshape(N_KV, QH + 2, 2, HALF)
    w_q = w[:, :QH].transpose(0, 2, 1, 3, 4).reshape(N_KV * QH * HD, D)
    b_q = bias[:, :QH].transpose(0, 2, 1, 3).reshape(-1)
    w_k = w[:, QH].reshape(2, N_KV // 2, 2, HALF, D).transpose(0, 2, 1, 3, 4).reshape(N_KV * HD, D)
    b_k = bias[:, QH].reshape(2, N_KV // 2, 2, HALF).transpose(0, 2, 1, 3).reshape(-1)
    w_v = w[:, QH + 1].reshape(NV, D)
    b_v = np.concatenate([bias[:, QH + 1].reshape(-1), np.asarray(L0_ffn_b)[:E], np.zeros(RANK, np.float32)]).reshape(1, -1)
    ffn_w = np.asarray(L0_ffn_W)
    w1 = np.concatenate([w_v.T, ffn_w[:E].T, np.asarray(L0_ffn_A), w_q.T, w_k.T], axis=1)
    w_out = np.concatenate([np.asarray(L0_attn_w_dense).T, ffn_w.T], axis=0)

    f32 = np.float32
    inv_freq = (1.0 / 1000000.0 ** (np.arange(0, HD, 2) / HD)).astype(f32)
    angle = np.arange(S, dtype=f32)[None, :] * inv_freq[:, None]
    cos, sin = np.cos(angle.astype(np.float64)), np.sin(angle.astype(np.float64))
    rope = np.stack([np.tile(cos, (2 * QH, 1)), np.concatenate([np.tile(sin, (QH, 1)), np.tile(-sin, (QH, 1))])], axis=1)
    i = np.arange(P)
    later = np.where(i[None, :] > i[:, None], NEG, 0.0)
    consts = np.concatenate([np.eye(P), i[:, None] == 2 * (i[None, :] // 2) + 1, later, later.T,
                             np.repeat(np.where(i < BLK, NEG, 0.0)[:, None], BLK, axis=1),
                             np.repeat(np.where(i >= BLK, NEG, 0.0)[:, None], BLK, axis=1)], axis=1)
    arrays = {
        "x": np.asarray(L0_attn_hidden_states).reshape(B * S, D),
        "w1": w1,
        "b_qk": np.concatenate([b_q, b_k]).reshape(NF, P).T,
        "b_v": b_v,
        "w_out": w_out,
        "b_out": np.asarray(L0_attn_b_dense).reshape(1, D),
        "b_ffn": np.asarray(L0_ffn_b).reshape(1, D),
        "adapter_out": np.asarray(L0_ffn_Bmat),
        "limes": np.asarray(L0_ffn_LiMEs),
        "limes_t": np.asarray(L0_ffn_LiMEs).T,
        "rope": rope.astype(f32),
        "consts": consts.astype(f32),
    }
    arrays = {name: np.ascontiguousarray(a) for name, a in arrays.items()}
    nc = bacc.Bacc("TRN2", target_bir_lowering=False, num_devices=1)
    args = [nc.dram_tensor(name, a.shape, F32, kind="ExternalInput").ap() for name, a in arrays.items()]
    out = nc.dram_tensor("out", (B * S, D), F32, kind="ExternalOutput").ap()
    mk_recurrent_d1(nc, *args, out)
    r = run_bass_kernel_spmd(nc, [arrays], core_ids=[0])
    return r.results[0]["out"].reshape(B, S, D)
```
